# Optimizing a Trainium2 kernel written in Bass

```python
import numpy as np
import jax
import jax.numpy as jnp

def _softmax(x, axis=-1):
    return jax.nn.softmax(x, axis=axis)

def _gelu(x):
    return jax.nn.gelu(x, approximate=True)

def _silu(x):
    return jax.nn.silu(x)

def _sigmoid(x):
    return jax.nn.sigmoid(x)

def _layernorm(x, axis=-1, eps=1e-05):
    m = jnp.mean(x, axis=axis, keepdims=True)
    v = jnp.var(x, axis=axis, keepdims=True)
    return (x - m) / jnp.sqrt(v + eps)

def _scatter_add(tgt, idx, src, axis=0):
    return tgt.at[idx].add(src)

def _segment_sum(src, seg, n):
    return jax.ops.segment_sum(src, seg, n)
kernel_name = 'mk_recurrent_d4_jaxref_r8_efa8a8'

def setup_inputs(seed: int=0):
    np.random.seed(seed)
    _w = jnp.asarray

    def _L0_attn_setup():
        import jax, jax.numpy as jnp
        import numpy as np
        B, S, H_DIM = (2, 256, 256)
        N_HEADS, D_HEAD = (16, 128)
        key = jax.random.key(seed)
        k1, k2, k3 = jax.random.split(key, 3)
        x = jax.random.normal(k1, (B, S, H_DIM), dtype=jnp.float32)
        w_qkv = jax.random.normal(k2, (H_DIM, 3 * N_HEADS * D_HEAD), dtype=jnp.float32) * 0.02
        w_o = jax.random.normal(k3, (N_HEADS * D_HEAD, H_DIM), dtype=jnp.float32) * 0.02
        return {'x': x, 'w_qkv': w_qkv, 'w_o': w_o}
    _L0_attn_in = _L0_attn_setup()

    def _L0_ffn_setup():
        import jax, jax.numpy as jnp
        import numpy as np
        from jax import lax
        DIM = 256
        E = 8
        K = 2
        RANK = 32
        CAP_FACTOR = 1.25

        def gelu(x):
            return jax.nn.gelu(x, approximate=False)

        def _moe_forward(x, gate_w, w1, b1, w2, b2, wd, wu, sw1, sb1, sw2, sb2, swd, swu):
            B, S, D = x.shape
            T = B * S
            cap = max(1, int(T * CAP_FACTOR / E))
            xt = x.reshape(T, D)
            logits = xt @ gate_w
            probs_full = jax.nn.softmax(logits, axis=-1)
            top_p, top_i = lax.top_k(probs_full, K)
            out = jnp.zeros_like(xt)
            for k in range(K):
                e = top_i[:, k]
                w = top_p[:, k]
                onehot = jax.nn.one_hot(e, E, dtype=jnp.int32)
                pos_all = jnp.cumsum(onehot, axis=0) - 1
                pos = jnp.take_along_axis(pos_all, e[:, None], axis=1)[:, 0]
                keep = pos < cap
                pos_c = jnp.where(keep, pos, cap)
                buf = jnp.zeros((E, cap, D), x.dtype).at[e, pos_c].set(xt * keep[:, None].astype(x.dtype), mode='drop')
                h = gelu(jnp.einsum('ecd,edf->ecf', buf, w1) + b1[:, None, :])
                y = jnp.einsum('ecf,efd->ecd', h, w2) + b2[:, None, :]
                a = jnp.einsum('ecr,erd->ecd', gelu(jnp.einsum('ecd,edr->ecr', buf, wd)), wu)
                y = y + a
                tok = y[e, jnp.minimum(pos_c, cap - 1)]
                out = out + tok * keep[:, None].astype(x.dtype) * w[:, None]
            sh = gelu(xt @ sw1 + sb1) @ sw2 + sb2
            sh = sh + gelu(xt @ swd) @ swu
            out = out + 0.2 * sh
            return out.reshape(B, S, D)
        key = jax.random.key(seed)
        ks = jax.random.split(key, 16)
        s = 0.02
        d, h = (DIM, 4 * DIM)
        inp = {'x': jax.random.normal(ks[0], (4, 256, d), dtype=jnp.float32), 'gate_w': jax.random.normal(ks[1], (d, E), dtype=jnp.float32) * s, 'w1': jax.random.normal(ks[2], (E, d, h), dtype=jnp.float32) * s, 'b1': jnp.zeros((E, h), dtype=jnp.float32), 'w2': jax.random.normal(ks[3], (E, h, d), dtype=jnp.float32) * s, 'b2': jnp.zeros((E, d), dtype=jnp.float32), 'wd': jax.random.normal(ks[4], (E, d, RANK), dtype=jnp.float32) * s, 'wu': jax.random.normal(ks[5], (E, RANK, d), dtype=jnp.float32) * s, 'sw1': jax.random.normal(ks[6], (d, h), dtype=jnp.float32) * s, 'sb1': jnp.zeros((h,), dtype=jnp.float32), 'sw2': jax.random.normal(ks[7], (h, d), dtype=jnp.float32) * s, 'sb2': jnp.zeros((d,), dtype=jnp.float32), 'swd': jax.random.normal(ks[8], (d, RANK), dtype=jnp.float32) * s, 'swu': jax.random.normal(ks[9], (RANK, d), dtype=jnp.float32) * s}
        return inp
    _L0_ffn_in = _L0_ffn_setup()

    def _L1_attn_setup():
        import math
        import jax, jax.numpy as jnp
        import numpy as np
        B, T, C = (4, 256, 256)
        LAYER_ID, N_LAYER = (12, 24)
        key = jax.random.key(seed)
        kx, kk, kv, kr, ko = jax.random.split(key, 5)
        x = jax.random.normal(kx, (B, T, C), dtype=jnp.float32)
        ratio_1_to_almost0 = 1.0 - LAYER_ID / N_LAYER
        ratio_0_to_1 = LAYER_ID / (N_LAYER - 1)
        h = np.arange(C, dtype=np.float64)
        zigzag = ((np.arange(C) + 1) % 3 - 1) * 0.5
        time_first = jnp.asarray(np.ones(C) * math.log(0.3) + zigzag, dtype=jnp.float32)
        base = h / C
        time_mix_k = jnp.asarray((base ** ratio_1_to_almost0)[None, None, :], dtype=jnp.float32)
        time_mix_v = jnp.asarray((base ** ratio_1_to_almost0 + 0.3 * ratio_0_to_1)[None, None, :], dtype=jnp.float32)
        time_mix_r = jnp.asarray((base ** (0.5 * ratio_1_to_almost0))[None, None, :], dtype=jnp.float32)
        xx = jnp.ones((1, 1, C), dtype=jnp.float32)
        aa = jnp.ones((1, 1, C), dtype=jnp.float32)
        bb = jnp.ones((1, 1, C), dtype=jnp.float32)
        pp = jnp.full((1, 1, C), -1e+30, dtype=jnp.float32)
        scale = 0.02
        w_key = jax.random.normal(kk, (C, C), dtype=jnp.float32) * scale
        w_value = jax.random.normal(kv, (C, C), dtype=jnp.float32) * scale
        w_rec = jax.random.normal(kr, (C, C), dtype=jnp.float32) * scale
        w_out = jax.random.normal(ko, (C, C), dtype=jnp.float32) * scale
        return {'x': x, 'time_first': time_first, 'time_mix_k': time_mix_k, 'time_mix_v': time_mix_v, 'time_mix_r': time_mix_r, 'xx': xx, 'aa': aa, 'bb': bb, 'pp': pp, 'w_key': w_key, 'w_value': w_value, 'w_rec': w_rec, 'w_out': w_out}
    _L1_attn_in = _L1_attn_setup()

    def _L1_ffn_setup():
        import jax, jax.numpy as jnp
        import numpy as np
        key = jax.random.key(seed)
        k1, k2, k3, k4 = jax.random.split(key, 4)
        B, S, D_IN, D_OUT = (4, 512, 256, 256)
        x = jax.random.normal(k1, (B, S, D_IN), dtype=jnp.float32)
        weight = jax.random.normal(k2, (D_OUT, D_IN), dtype=jnp.float32) * 0.02
        scale_weight = jax.random.uniform(k3, (D_OUT,), dtype=jnp.float32, minval=0.5, maxval=1.5)
        bias = jax.random.normal(k4, (D_OUT,), dtype=jnp.float32) * 0.02
        return {'x': x, 'weight': weight, 'scale_weight': scale_weight, 'bias': bias}
    _L1_ffn_in = _L1_ffn_setup()

    def _L2_attn_setup():
        import jax, jax.numpy as jnp
        import numpy as np
        NUM_HEADS = 16
        ROPE_BASE = 10000.0

        def _rotate_half(x):
            x1, x2 = jnp.split(x, 2, axis=-1)
            return jnp.concatenate([-x2, x1], axis=-1)

        def _rope_cos_sin(seq_len, dim, dtype):
            inv_freq = 1.0 / ROPE_BASE ** (jnp.arange(0, dim, 2, dtype=jnp.float32) / dim)
            t = jnp.arange(seq_len, dtype=jnp.float32)
            freqs = jnp.einsum('s,d->sd', t, inv_freq)
            emb = jnp.concatenate([freqs, freqs], axis=-1)
            cos = jnp.cos(emb).astype(dtype)[:, None, None, :]
            sin = jnp.sin(emb).astype(dtype)[:, None, None, :]
            return (cos, sin)
        key = jax.random.key(seed)
        k1, k2, k3 = jax.random.split(key, 3)
        S, B, H = (256, 2, 256)
        x = jax.random.normal(k1, (S, B, H), dtype=jnp.float32)
        w_qkv = jax.random.normal(k2, (H, 3 * H), dtype=jnp.float32) * 0.02
        w_dense = jax.random.normal(k3, (H, H), dtype=jnp.float32) * 0.02
        return {'x': x, 'w_qkv': w_qkv, 'w_dense': w_dense}
    _L2_attn_in = _L2_attn_setup()

    def _L2_ffn_setup():
        import jax, jax.numpy as jnp
        import numpy as np
        GOLDEN_CENTER = 1.0 / np.e
        GOLDEN_LOWER = 0.5 - np.log(4.0 / 3.0)
        GOLDEN_UPPER = 0.5

        def _golden_weights(x, Wr, temperature):
            inh = jax.nn.sigmoid(x @ Wr / temperature)
            in_zone = (inh >= GOLDEN_LOWER) & (inh <= GOLDEN_UPPER)
            distance = jnp.abs(inh - GOLDEN_CENTER)
            weights = jnp.exp(-distance / 0.1) * in_zone.astype(x.dtype)
            wsum = jnp.sum(weights, axis=-1, keepdims=True)
            no_expert = wsum < 1e-08
            fb = jnp.exp(-distance / 0.3)
            _, top2 = jax.lax.top_k(fb, 2)
            fb_mask = jnp.sum(jax.nn.one_hot(top2, weights.shape[-1], dtype=x.dtype), axis=-2)
            fb_w = fb * fb_mask
            fb_w = fb_w / jnp.maximum(jnp.sum(fb_w, axis=-1, keepdims=True), 1e-08)
            weights = jnp.where(no_expert, fb_w, weights)
            weights = weights / jnp.maximum(jnp.sum(weights, axis=-1, keepdims=True), 1e-08)
            return weights
        key = jax.random.key(seed)
        ks = jax.random.split(key, 5)
        B, T, D, E, F = (2, 256, 256, 8, 256)
        s_in = 1.0 / np.sqrt(D)
        s_f = 1.0 / np.sqrt(F)
        return {'x': jax.random.normal(ks[0], (B, T, D), dtype=jnp.float32), 'Wg': jax.random.normal(ks[1], (E, D, F), dtype=jnp.float32) * s_in, 'Wu': jax.random.normal(ks[2], (E, D, F), dtype=jnp.float32) * s_in, 'Wd': jax.random.normal(ks[3], (E, F, D), dtype=jnp.float32) * s_f, 'Wr': jax.random.normal(ks[4], (D, E), dtype=jnp.float32) * s_in, 'temperature': jnp.ones((1,), dtype=jnp.float32)}
    _L2_ffn_in = _L2_ffn_setup()

    def _L3_attn_setup():
        import jax, jax.numpy as jnp
        import numpy as np
        N_EMBD = 256
        N_HEAD = 8
        HEAD_DIM = 32
        HALF = HEAD_DIM // 2
        LAMBDA_INIT = 0.8
        RMS_EPS = 1.1920929e-07

        def _rms_norm(x):
            return x * jax.lax.rsqrt(jnp.mean(x * x, axis=-1, keepdims=True) + RMS_EPS)

        def _causal_attn(q, k, v, mask):
            scale = 1.0 / jnp.sqrt(jnp.asarray(q.shape[-1], q.dtype))
            scores = jnp.einsum('bhqd,bhkd->bhqk', q, k) * scale
            scores = jnp.where(mask, scores, -jnp.inf)
            attn = jax.nn.softmax(scores, axis=-1)
            return jnp.einsum('bhqk,bhkd->bhqd', attn, v)
        key = jax.random.key(seed)
        ks = jax.random.split(key, 10)
        B, T, C = (2, 256, N_EMBD)
        x = jax.random.normal(ks[0], (B, T, C), dtype=jnp.float32)
        wq = jax.random.normal(ks[1], (C, C), dtype=jnp.float32) * 0.02
        wk = jax.random.normal(ks[2], (C, C), dtype=jnp.float32) * 0.02
        wv = jax.random.normal(ks[3], (C, C), dtype=jnp.float32) * 0.02
        wo = jax.random.normal(ks[4], (C, C), dtype=jnp.float32) * 0.02
        lq1 = jax.random.normal(ks[5], (HEAD_DIM,), dtype=jnp.float32) * 0.1
        lk1 = jax.random.normal(ks[6], (HEAD_DIM,), dtype=jnp.float32) * 0.1
        lq2 = jax.random.normal(ks[7], (HEAD_DIM,), dtype=jnp.float32) * 0.1
        lk2 = jax.random.normal(ks[8], (HEAD_DIM,), dtype=jnp.float32) * 0.1
        return {'x': x, 'wq': wq, 'wk': wk, 'wv': wv, 'wo': wo, 'lq1': lq1, 'lk1': lk1, 'lq2': lq2, 'lk2': lk2}
    _L3_attn_in = _L3_attn_setup()

    def _L3_ffn_setup():
        import jax, jax.numpy as jnp
        import numpy as np
        B, S, D, H = (4, 256, 256, 1024)

        def fwht(x):
            orig_shape = x.shape
            n = orig_shape[-1]
            x = x.reshape(-1, n)
            h = 1
            while h < n:
                xb = x.reshape(-1, n // (2 * h), 2, h)
                a = xb[:, :, 0, :]
                b = xb[:, :, 1, :]
                x = jnp.stack([a + b, a - b], axis=2).reshape(-1, n)
                h *= 2
            scale = jnp.asarray(1.0 / np.sqrt(n), dtype=x.dtype)
            return (x * scale).reshape(orig_shape)
        key = jax.random.key(seed)
        kx, k1, k2, k3 = jax.random.split(key, 4)
        x = jax.random.normal(kx, (B, S, D), dtype=jnp.float32)
        W1 = jax.random.normal(k1, (H, D), dtype=jnp.float32) * (1.0 / np.sqrt(D))
        W2 = jax.random.normal(k2, (D, H), dtype=jnp.float32) * (1.0 / np.sqrt(H))
        W3 = jax.random.normal(k3, (H, D), dtype=jnp.float32) * (1.0 / np.sqrt(D))
        return {'x': x, 'W1': W1, 'W2': W2, 'W3': W3}
    _L3_ffn_in = _L3_ffn_setup()
    _d = {'L0_attn_x': _L0_attn_in['x'], 'L0_attn_w_qkv': _L0_attn_in['w_qkv'], 'L0_attn_w_o': _L0_attn_in['w_o'], 'L0_ffn_gate_w': _L0_ffn_in['gate_w'], 'L0_ffn_w1': _L0_ffn_in['w1'], 'L0_ffn_b1': _L0_ffn_in['b1'], 'L0_ffn_w2': _L0_ffn_in['w2'], 'L0_ffn_b2': _L0_ffn_in['b2'], 'L0_ffn_wd': _L0_ffn_in['wd'], 'L0_ffn_wu': _L0_ffn_in['wu'], 'L0_ffn_sw1': _L0_ffn_in['sw1'], 'L0_ffn_sb1': _L0_ffn_in['sb1'], 'L0_ffn_sw2': _L0_ffn_in['sw2'], 'L0_ffn_sb2': _L0_ffn_in['sb2'], 'L0_ffn_swd': _L0_ffn_in['swd'], 'L0_ffn_swu': _L0_ffn_in['swu'], 'L1_attn_time_first': _L1_attn_in['time_first'], 'L1_attn_time_mix_k': _L1_attn_in['time_mix_k'], 'L1_attn_time_mix_v': _L1_attn_in['time_mix_v'], 'L1_attn_time_mix_r': _L1_attn_in['time_mix_r'], 'L1_attn_xx': _L1_attn_in['xx'], 'L1_attn_aa': _L1_attn_in['aa'], 'L1_attn_bb': _L1_attn_in['bb'], 'L1_attn_pp': _L1_attn_in['pp'], 'L1_attn_w_key': _L1_attn_in['w_key'], 'L1_attn_w_value': _L1_attn_in['w_value'], 'L1_attn_w_rec': _L1_attn_in['w_rec'], 'L1_attn_w_out': _L1_attn_in['w_out'], 'L1_ffn_weight': _L1_ffn_in['weight'], 'L1_ffn_scale_weight': _L1_ffn_in['scale_weight'], 'L1_ffn_bias': _L1_ffn_in['bias'], 'L2_attn_w_qkv': _L2_attn_in['w_qkv'], 'L2_attn_w_dense': _L2_attn_in['w_dense'], 'L2_ffn_Wg': _L2_ffn_in['Wg'], 'L2_ffn_Wu': _L2_ffn_in['Wu'], 'L2_ffn_Wd': _L2_ffn_in['Wd'], 'L2_ffn_Wr': _L2_ffn_in['Wr'], 'L2_ffn_temperature': _L2_ffn_in['temperature'], 'L3_attn_wq': _L3_attn_in['wq'], 'L3_attn_wk': _L3_attn_in['wk'], 'L3_attn_wv': _L3_attn_in['wv'], 'L3_attn_wo': _L3_attn_in['wo'], 'L3_attn_lq1': _L3_attn_in['lq1'], 'L3_attn_lk1': _L3_attn_in['lk1'], 'L3_attn_lq2': _L3_attn_in['lq2'], 'L3_attn_lk2': _L3_attn_in['lk2'], 'L3_ffn_W1': _L3_ffn_in['W1'], 'L3_ffn_W2': _L3_ffn_in['W2'], 'L3_ffn_W3': _L3_ffn_in['W3']}
    _x0 = _d['L0_attn_x']
    _d['L0_attn_x'] = jax.random.normal(jax.random.fold_in(jax.random.key(seed), 1), (2, 512, 256), dtype=_x0.dtype)
    del _x0
    return _d

def reference(L0_attn_x, L0_attn_w_qkv, L0_attn_w_o, L0_ffn_gate_w, L0_ffn_w1, L0_ffn_b1, L0_ffn_w2, L0_ffn_b2, L0_ffn_wd, L0_ffn_wu, L0_ffn_sw1, L0_ffn_sb1, L0_ffn_sw2, L0_ffn_sb2, L0_ffn_swd, L0_ffn_swu, L1_attn_time_first, L1_attn_time_mix_k, L1_attn_time_mix_v, L1_attn_time_mix_r, L1_attn_xx, L1_attn_aa, L1_attn_bb, L1_attn_pp, L1_attn_w_key, L1_attn_w_value, L1_attn_w_rec, L1_attn_w_out, L1_ffn_weight, L1_ffn_scale_weight, L1_ffn_bias, L2_attn_w_qkv, L2_attn_w_dense, L2_ffn_Wg, L2_ffn_Wu, L2_ffn_Wd, L2_ffn_Wr, L2_ffn_temperature, L3_attn_wq, L3_attn_wk, L3_attn_wv, L3_attn_wo, L3_attn_lq1, L3_attn_lk1, L3_attn_lq2, L3_attn_lk2, L3_ffn_W1, L3_ffn_W2, L3_ffn_W3):

    def _L0_attn_ref(x, w_qkv, w_o):
        import jax, jax.numpy as jnp
        import numpy as np
        B, S, H_DIM = (2, 256, 256)
        N_HEADS, D_HEAD = (16, 128)
        b, s, _ = x.shape
        qkv = jnp.einsum('bsh,hf->bsf', x, w_qkv)
        qkv = qkv.reshape(b, s, 3, N_HEADS, D_HEAD)
        q, k, v = (qkv[:, :, 0], qkv[:, :, 1], qkv[:, :, 2])
        q = q.transpose(0, 2, 1, 3)
        k = k.transpose(0, 2, 1, 3)
        v = v.transpose(0, 2, 1, 3)
        scores = jnp.einsum('bhqd,bhkd->bhqk', q, k) / jnp.sqrt(jnp.float32(D_HEAD))
        probs = jax.nn.softmax(scores, axis=-1)
        values = jnp.einsum('bhqk,bhkd->bhkd', probs, v)
        values = values.transpose(0, 2, 1, 3).reshape(b, s, N_HEADS * D_HEAD)
        out = jnp.einsum('bsf,fh->bsh', values, w_o)
        return out

    def _L0_ffn_ref(x, gate_w, w1, b1, w2, b2, wd, wu, sw1, sb1, sw2, sb2, swd, swu):
        import jax, jax.numpy as jnp
        import numpy as np
        from jax import lax
        DIM = 256
        E = 8
        K = 2
        RANK = 32
        CAP_FACTOR = 1.25

        def gelu(x):
            return jax.nn.gelu(x, approximate=False)

        def _moe_forward(x, gate_w, w1, b1, w2, b2, wd, wu, sw1, sb1, sw2, sb2, swd, swu):
            B, S, D = x.shape
            T = B * S
            cap = max(1, int(T * CAP_FACTOR / E))
            xt = x.reshape(T, D)
            logits = xt @ gate_w
            probs_full = jax.nn.softmax(logits, axis=-1)
            top_p, top_i = lax.top_k(probs_full, K)
            out = jnp.zeros_like(xt)
            for k in range(K):
                e = top_i[:, k]
                w = top_p[:, k]
                onehot = jax.nn.one_hot(e, E, dtype=jnp.int32)
                pos_all = jnp.cumsum(onehot, axis=0) - 1
                pos = jnp.take_along_axis(pos_all, e[:, None], axis=1)[:, 0]
                keep = pos < cap
                pos_c = jnp.where(keep, pos, cap)
                buf = jnp.zeros((E, cap, D), x.dtype).at[e, pos_c].set(xt * keep[:, None].astype(x.dtype), mode='drop')
                h = gelu(jnp.einsum('ecd,edf->ecf', buf, w1) + b1[:, None, :])
                y = jnp.einsum('ecf,efd->ecd', h, w2) + b2[:, None, :]
                a = jnp.einsum('ecr,erd->ecd', gelu(jnp.einsum('ecd,edr->ecr', buf, wd)), wu)
                y = y + a
                tok = y[e, jnp.minimum(pos_c, cap - 1)]
                out = out + tok * keep[:, None].astype(x.dtype) * w[:, None]
            sh = gelu(xt @ sw1 + sb1) @ sw2 + sb2
            sh = sh + gelu(xt @ swd) @ swu
            out = out + 0.2 * sh
            return out.reshape(B, S, D)
        return _moe_forward(x, gate_w, w1, b1, w2, b2, wd, wu, sw1, sb1, sw2, sb2, swd, swu)

    def _L1_attn_ref(x, time_first, time_mix_k, time_mix_v, time_mix_r, xx, aa, bb, pp, w_key, w_value, w_rec, w_out):
        import math
        import jax, jax.numpy as jnp
        import numpy as np
        B, T, C = (4, 256, 256)
        LAYER_ID, N_LAYER = (12, 24)
        xk = x * time_mix_k + (1.0 - time_mix_k) * xx
        xv = x * time_mix_v + (1.0 - time_mix_v) * xx
        xr = x * time_mix_r + (1.0 - time_mix_r) * xx
        k = jnp.einsum('btc,oc->bto', xk, w_key)
        v = jnp.einsum('btc,oc->bto', xv, w_value)
        r = jax.nn.sigmoid(jnp.einsum('btc,oc->bto', xr, w_rec))
        t = x.shape[1]
        aa_p = jnp.pad(aa, ((0, 0), (0, t - 1), (0, 0)))
        bb_p = jnp.pad(bb, ((0, 0), (0, t - 1), (0, 0)))
        pp_p = jnp.pad(pp, ((0, 0), (0, t - 1), (0, 0)))
        ww = time_first + k
        qq = jnp.maximum(pp_p, ww)
        e1 = jnp.exp(pp_p - qq)
        e2 = jnp.exp(ww - qq)
        wkv = (e1 * aa_p + e2 * v) / (e1 * bb_p + e2)
        return jnp.einsum('btc,oc->bto', r * wkv, w_out)

    def _L1_ffn_ref(x, weight, scale_weight, bias):
        import jax, jax.numpy as jnp
        import numpy as np
        w = weight * scale_weight[:, None]
        out = jnp.einsum('bsi,oi->bso', x, w) + bias
        return out

    def _L2_attn_ref(x, w_qkv, w_dense):
        import jax, jax.numpy as jnp
        import numpy as np
        NUM_HEADS = 16
        ROPE_BASE = 10000.0

        def _rotate_half(x):
            x1, x2 = jnp.split(x, 2, axis=-1)
            return jnp.concatenate([-x2, x1], axis=-1)

        def _rope_cos_sin(seq_len, dim, dtype):
            inv_freq = 1.0 / ROPE_BASE ** (jnp.arange(0, dim, 2, dtype=jnp.float32) / dim)
            t = jnp.arange(seq_len, dtype=jnp.float32)
            freqs = jnp.einsum('s,d->sd', t, inv_freq)
            emb = jnp.concatenate([freqs, freqs], axis=-1)
            cos = jnp.cos(emb).astype(dtype)[:, None, None, :]
            sin = jnp.sin(emb).astype(dtype)[:, None, None, :]
            return (cos, sin)
        S, B, H = x.shape
        hd = H // NUM_HEADS
        qkv = jnp.einsum('sbh,hk->sbk', x, w_qkv)
        qkv = qkv.reshape(S, B, NUM_HEADS, 3 * hd)
        q, k, v = jnp.split(qkv, 3, axis=-1)
        cos, sin = _rope_cos_sin(S, hd, x.dtype)
        q = q * cos + _rotate_half(q) * sin
        k = k * cos + _rotate_half(k) * sin
        norm_factor = jnp.asarray(np.sqrt(hd), dtype=x.dtype)
        scores = jnp.einsum('sbhd,tbhd->bhst', q, k) / norm_factor
        causal = jnp.tril(jnp.ones((S, S), dtype=bool))
        scores = jnp.where(causal, scores, jnp.asarray(-10000.0, dtype=scores.dtype))
        probs = jax.nn.softmax(scores.astype(jnp.float32), axis=-1).astype(x.dtype)
        ctx = jnp.einsum('bhst,tbhd->sbhd', probs, v).reshape(S, B, H)
        out = jnp.einsum('sbh,hk->sbk', ctx, w_dense)
        return out

    def _L2_ffn_ref(x, Wg, Wu, Wd, Wr, temperature):
        import jax, jax.numpy as jnp
        import numpy as np
        GOLDEN_CENTER = 1.0 / np.e
        GOLDEN_LOWER = 0.5 - np.log(4.0 / 3.0)
        GOLDEN_UPPER = 0.5

        def _golden_weights(x, Wr, temperature):
            inh = jax.nn.sigmoid(x @ Wr / temperature)
            in_zone = (inh >= GOLDEN_LOWER) & (inh <= GOLDEN_UPPER)
            distance = jnp.abs(inh - GOLDEN_CENTER)
            weights = jnp.exp(-distance / 0.1) * in_zone.astype(x.dtype)
            wsum = jnp.sum(weights, axis=-1, keepdims=True)
            no_expert = wsum < 1e-08
            fb = jnp.exp(-distance / 0.3)
            _, top2 = jax.lax.top_k(fb, 2)
            fb_mask = jnp.sum(jax.nn.one_hot(top2, weights.shape[-1], dtype=x.dtype), axis=-2)
            fb_w = fb * fb_mask
            fb_w = fb_w / jnp.maximum(jnp.sum(fb_w, axis=-1, keepdims=True), 1e-08)
            weights = jnp.where(no_expert, fb_w, weights)
            weights = weights / jnp.maximum(jnp.sum(weights, axis=-1, keepdims=True), 1e-08)
            return weights
        weights = _golden_weights(x, Wr, temperature)
        gate = jnp.einsum('btd,edf->betf', x, Wg)
        up = jnp.einsum('btd,edf->betf', x, Wu)
        h = jax.nn.silu(gate) * up
        e_out = jnp.einsum('betf,efd->betd', h, Wd)
        out = jnp.einsum('bte,betd->btd', weights, e_out)
        return out

    def _L3_attn_ref(x, wq, wk, wv, wo, lq1, lk1, lq2, lk2):
        import jax, jax.numpy as jnp
        import numpy as np
        N_EMBD = 256
        N_HEAD = 8
        HEAD_DIM = 32
        HALF = HEAD_DIM // 2
        LAMBDA_INIT = 0.8
        RMS_EPS = 1.1920929e-07

        def _rms_norm(x):
            return x * jax.lax.rsqrt(jnp.mean(x * x, axis=-1, keepdims=True) + RMS_EPS)

        def _causal_attn(q, k, v, mask):
            scale = 1.0 / jnp.sqrt(jnp.asarray(q.shape[-1], q.dtype))
            scores = jnp.einsum('bhqd,bhkd->bhqk', q, k) * scale
            scores = jnp.where(mask, scores, -jnp.inf)
            attn = jax.nn.softmax(scores, axis=-1)
            return jnp.einsum('bhqk,bhkd->bhqd', attn, v)
        B, T, C = x.shape
        lambda_1 = jnp.exp(jnp.sum(lq1 * lk1))
        lambda_2 = jnp.exp(jnp.sum(lq2 * lk2))
        lambda_full = lambda_1 - lambda_2 + LAMBDA_INIT
        q = (x @ wq.T).reshape(B, T, N_HEAD, 2, HALF).transpose(0, 2, 1, 3, 4)
        k = (x @ wk.T).reshape(B, T, N_HEAD, 2, HALF).transpose(0, 2, 1, 3, 4)
        v = (x @ wv.T).reshape(B, T, N_HEAD, HEAD_DIM).transpose(0, 2, 1, 3)
        q1 = _rms_norm(q[..., 0, :])
        q2 = _rms_norm(q[..., 1, :])
        k1 = _rms_norm(k[..., 0, :])
        k2 = _rms_norm(k[..., 1, :])
        mask = jnp.tril(jnp.ones((T, T), dtype=bool))
        y1 = _causal_attn(q1, k1, v, mask)
        y2 = _causal_attn(q2, k2, v, mask)
        y = y1 - lambda_full * y2
        y = y.transpose(0, 2, 1, 3).reshape(B, T, C)
        return y @ wo.T * (1.0 - LAMBDA_INIT)

    def _L3_ffn_ref(x, W1, W2, W3):
        import jax, jax.numpy as jnp
        import numpy as np
        B, S, D, H = (4, 256, 256, 1024)

        def fwht(x):
            orig_shape = x.shape
            n = orig_shape[-1]
            x = x.reshape(-1, n)
            h = 1
            while h < n:
                xb = x.reshape(-1, n // (2 * h), 2, h)
                a = xb[:, :, 0, :]
                b = xb[:, :, 1, :]
                x = jnp.stack([a + b, a - b], axis=2).reshape(-1, n)
                h *= 2
            scale = jnp.asarray(1.0 / np.sqrt(n), dtype=x.dtype)
            return (x * scale).reshape(orig_shape)
        up_gate = jnp.einsum('bsd,hd->bsh', x, W1)
        up_lin = jnp.einsum('bsd,hd->bsh', x, W3)
        hidden = jax.nn.silu(up_gate) * up_lin
        hidden = fwht(hidden)
        out = jnp.einsum('bsh,dh->bsd', hidden, W2)
        return out
    x = L0_attn_x
    xn = _layernorm(x, axis=-1)
    s = _L0_attn_ref(xn, L0_attn_w_qkv, L0_attn_w_o)
    g = _silu(_L0_ffn_ref(xn, L0_ffn_gate_w, L0_ffn_w1, L0_ffn_b1, L0_ffn_w2, L0_ffn_b2, L0_ffn_wd, L0_ffn_wu, L0_ffn_sw1, L0_ffn_sb1, L0_ffn_sw2, L0_ffn_sb2, L0_ffn_swd, L0_ffn_swu))
    x = x + s * g
    xn = _layernorm(x, axis=-1)
    s = _L1_attn_ref(xn, L1_attn_time_first, L1_attn_time_mix_k, L1_attn_time_mix_v, L1_attn_time_mix_r, L1_attn_xx, L1_attn_aa, L1_attn_bb, L1_attn_pp, L1_attn_w_key, L1_attn_w_value, L1_attn_w_rec, L1_attn_w_out)
    g = _silu(_L1_ffn_ref(xn, L1_ffn_weight, L1_ffn_scale_weight, L1_ffn_bias))
    x = x + s * g
    xn = _layernorm(x, axis=-1)
    s = _L2_attn_ref(xn, L2_attn_w_qkv, L2_attn_w_dense)
    g = _silu(_L2_ffn_ref(xn, L2_ffn_Wg, L2_ffn_Wu, L2_ffn_Wd, L2_ffn_Wr, L2_ffn_temperature))
    x = x + s * g
    xn = _layernorm(x, axis=-1)
    s = _L3_attn_ref(xn, L3_attn_wq, L3_attn_wk, L3_attn_wv, L3_attn_wo, L3_attn_lq1, L3_attn_lk1, L3_attn_lq2, L3_attn_lk2)
    g = _silu(_L3_ffn_ref(xn, L3_ffn_W1, L3_ffn_W2, L3_ffn_W3))
    x = x + s * g
    return x

_drawn_inputs = setup_inputs


def setup_inputs(seed=0):
    import zlib

    import numpy as np

    out = dict(_drawn_inputs(seed))
    spreads = {'L0_ffn_b1': (0.0, 0.1),
     'L0_ffn_b2': (0.0, 0.1),
     'L0_ffn_sb1': (0.0, 0.1),
     'L0_ffn_sb2': (0.0, 0.1),
     'L1_attn_xx': (1.0, 0.2),
     'L1_attn_aa': (1.0, 0.2),
     'L1_attn_bb': (1.0, 0.2),
     'L1_attn_pp': (-1.0000000150474662e+30, 0.2)}
    factors = {}
    for name, (base, spread) in spreads.items():
        noise = np.random.default_rng([zlib.crc32(name.encode()), seed]).standard_normal(out[name].shape)
        drawn = base * np.exp(spread * noise) if base else spread * noise
        out[name] = jnp.asarray(drawn.astype(out[name].dtype))
    for name, factor in factors.items():
        out[name] = (out[name] * factor).astype(out[name].dtype)
    return out
```

```python
from contextlib import ExitStack

import numpy as np

import concourse.bass as bass
from concourse import mybir

F32 = mybir.dt.float32
I32 = mybir.dt.int32
ALU = mybir.AluOpType
ACT = mybir.ActivationFunctionType
AX = mybir.AxisListType

P = 128
B, S, D = 2, 512, 256
T = B * S
NT = T // P
DC = D // P
ST = S // P
LN_EPS = 1e-5

NH, DH = 16, 128
NE, CAP, FF, RANK = 8, 160, 1024, 32
NF = FF // P
SLOTS = 2 * CAP
SROWS = [128, 128, SLOTS - 256]
WPACK = DC * FF + NF * D + DC * RANK + NF
NO_SLOT = 4096.0
OUT_OF_REACH = -3.0e38

H2, HD2 = 16, 16
E2 = 8
GOLD_C = float(1.0 / np.e)
GOLD_LO = 0.5 - np.log(4.0 / 3.0)
Z_LO = float(np.log(GOLD_LO / (1.0 - GOLD_LO)))
BLOCKED = -10000.0

H3, G3 = 8, 16
RMS_EPS = 1.1920929e-07
LAMBDA_INIT = 0.8

C_ID, C_TRI, C_HAD, C_CAUSAL, C_IOTA, C_COS, C_SIN, C_SEL = 0, 128, 256, 384, 512, 576, 832, 1088
C_END = 1096


def constants():
    c = np.zeros((P, C_END), np.float32)
    i = np.arange(P)
    c[:, C_ID:C_ID + P] = np.eye(P)
    c[:, C_TRI:C_TRI + P] = i[:, None] < i[None, :]
    had = np.array([[1.0]])
    while had.shape[0] < P:
        had = np.block([[had, had], [had, -had]])
    c[:, C_HAD:C_HAD + P] = had
    c[:, C_CAUSAL:C_CAUSAL + P] = i[:, None] <= i[None, :]
    c[:, C_IOTA:C_IOTA + 64] = np.tile(np.arange(8) - 8.0, 8)
    inv = 1.0 / 10000.0 ** (np.arange(0, HD2, 2, dtype=np.float32) / np.float32(HD2))
    ang = np.concatenate([inv, inv]).astype(np.float32)
    sign = np.where(np.arange(HD2) < HD2 // 2, -1.0, 1.0)
    c[:, C_COS:C_COS + D] = np.tile(np.cos(ang), H2)
    c[:, C_SIN:C_SIN + D] = np.tile(np.sin(ang) * sign, H2)
    c[:, C_SEL:C_SEL + 8] = (i[:, None] // G3) == np.arange(8)[None, :]
    return c


class Link:

    def __init__(self, eng, sem):
        self.eng, self.sem, self.n, self.turn, self.step = eng, sem, 0, 0, 0

    def loop(self, turn, step):
        self.turn, self.step, self.start = turn, step, self.n

    def end(self, turns):
        assert self.n - self.start == self.step, (self.n - self.start, self.step)
        self.n = self.start + turns * self.step
        self.turn, self.step = 0, 0

    def __call__(self, ins):
        self.n += 1
        ins.then_inc(self.sem, 1)
        self.eng.wait_ge(self.sem, self.n + self.turn * self.step if self.step else self.n)


def build(nc, a, out, layers=4):
    ctx = ExitStack()
    with ctx:
        def sem(name):
            return ctx.enter_context(nc.semaphore(name))

        def sb(name, shape, dt=F32):
            return ctx.enter_context(nc.sbuf_tensor(name, shape, dt))

        bank = [ctx.enter_context(nc.psum_tensor(f"bank{i}", [P, 512], F32)) for i in range(8)]

        x = sb("x", [P, NT, D])
        xn = sb("xn", [P, NT, D])
        xnT = sb("xnT", [P, DC, T])
        s_tok = sb("s_tok", [P, NT, D])
        g_tok = sb("g_tok", [P, NT, D])
        con = sb("con", [P, C_END])
        ones = sb("ones", [P, P])
        stats = sb("stats", [P, NT, 6])
        meanvar = sb("meanvar", [P, NT, 2])
        veps = sb("veps", [P, NT])
        rstd = sb("rstd", [P, NT])
        mhalf = sb("mhalf", [P, 256])
        ident = con[:, C_ID:C_ID + P]

        arenaB = sb("arenaB", [P, 16384])
        arenaC = sb("arenaC", [P, 12800])
        arenaD = sb("arenaD", [P, 2 * (WPACK + 2 * D)])
        small = sb("small", [P, 1536])

        def part(arena, at, n, **kw):
            v = arena[:, at:at + n]
            return v.rearrange(kw.pop("r"), **kw) if "r" in kw else v

        vals = part(arenaB, 0, NH * T, r="p (h t) -> p h t", h=NH)
        wqkv = [part(arenaC, 768 * q, 768, r="p (c w) -> p c w", c=DC) for q in range(2)]
        wo = part(arenaC, 1536, NH * D, r="p (h d) -> p h d", h=NH)
        qT = [part(arenaC, 5632 + 1024 * q, T) for q in range(2)]
        kT = [part(arenaC, 7680 + 1024 * q, T) for q in range(2)]
        vT = [part(arenaC, 9728 + 1024 * q, T) for q in range(2)]
        acc = [part(arenaC, 11776 + 512 * b, S) for b in range(B)]
        prob = [g_tok[:, 2 * q:2 * q + 2, :].rearrange("p a d -> p (a d)") for q in range(4)]
        wexp = [part(arenaD, (WPACK + 2 * D) * q, WPACK + 2 * D) for q in range(2)]
        w1 = [w[:, 0:DC * FF].rearrange("p (c f) -> p c f", c=DC) for w in wexp]
        w2 = [w[:, DC * FF:DC * FF + NF * D].rearrange("p (f d) -> p f d", f=NF) for w in wexp]
        wd = [w[:, DC * FF + NF * D:DC * FF + NF * D + DC * RANK].rearrange("p (c r) -> p c r", c=DC) for w in wexp]
        b1 = [w[:, WPACK - NF:WPACK] for w in wexp]
        wu = [w[0:RANK, WPACK:WPACK + D] for w in wexp]
        b2 = [w[:, WPACK + D:WPACK + 2 * D] for w in wexp]
        xe = [part(arenaC, 5632 + 768 * q, 768, r="p (s d) -> p s d", s=3) for q in range(2)]
        xeT = [part(arenaC, 640 * q, 640, r="p (c n) -> p c n", c=DC) for q in range(2)]
        hE = part(arenaC, 1280, NF * SLOTS, r="p (f n) -> p f n", f=NF)
        aE = arenaC[0:RANK, 3840:3840 + SLOTS]
        yE = [part(arenaC, 7168 + 768 * q, 768, r="p (s d) -> p s d", s=3) for q in range(2)]
        hS = part(arenaB, 0, NF * T, r="p (f t) -> p f t", f=NF)
        sw = part(arenaB, 8192, DC * FF + NF * D + DC * RANK + NF + D)
        sw1 = sw[:, 0:DC * FF].rearrange("p (c f) -> p c f", c=DC)
        sw2 = sw[:, DC * FF:DC * FF + NF * D].rearrange("p (f d) -> p f d", f=NF)
        swd = sw[:, DC * FF + NF * D:DC * FF + NF * D + DC * RANK].rearrange("p (c r) -> p c r", c=DC)
        sb1 = sw[:, WPACK - NF:WPACK]
        sb2 = sw[:, WPACK:WPACK + D]
        swu = arenaB[0:RANK, 12616:12616 + D]
        aS = arenaB[0:RANK, 12872:12872 + T]
        got = [part(arenaC, 8704 + NT * D * k, NT * D, r="p (t d) -> p t d", t=NT) for k in range(2)]
        gate = part(small, 0, DC * NE, r="p (c e) -> p c e", c=DC)
        lg = part(small, 16, 64, r="p (t e) -> p t e", t=NT)
        eq = part(small, 80, 64, r="p (t e) -> p t e", t=NT)
        ex = part(small, 144, 64, r="p (t e) -> p t e", t=NT)
        oh = part(small, 208, 128, r="p (t k e) -> p t k e", t=NT, k=2)
        before = part(small, 336, 128, r="p (t k e) -> p t k e", t=NT, k=2)
        ohp = part(small, 464, 128, r="p (t k e) -> p t k e", t=NT, k=2)
        top = part(small, 592, 16, r="p (k t) -> p k t", k=2)
        idx = part(small, 608, 16, r="p (t k) -> p t k", k=2)
        pos = part(small, 624, 16, r="p (t k) -> p t k", k=2)
        keep = part(small, 640, 16, r="p (t k) -> p t k", k=2)
        base = part(small, 656, 16, r="p (t k) -> p t k", k=2)
        slot = part(small, 672, 16, r="p (t k) -> p t k", k=2)
        wt = part(small, 688, 16, r="p (t k) -> p t k", k=2)
        esum = part(small, 704, 8)
        einv = part(small, 712, 8)
        kslot = part(small, 720, 16, r="p (t k) -> p t k", k=2)
        gap = part(small, 748, 8)
        negmax = part(small, 736, 4)
        rowsum = part(small, 740, 4)
        rowinv = part(small, 744, 4)
        w_rwkv = part(arenaB, 13896, 4 * DC * D, r="p (i c o) -> p i c o", i=4, c=DC)
        w_lin = part(arenaC, 4160, DC * D, r="p (c o) -> p c o", c=DC)
        lin_scale, lin_bias = part(arenaC, 4672, D), part(arenaC, 4928, D)
        vec = part(small, 756, 16, r="p (i c) -> p i c", i=8)
        offs = part(small, 772, 6, r="p (i c) -> p i c", i=3)
        mixed = part(arenaB, 0, 3 * DC * T, r="p (i c t) -> p i c t", i=3, c=DC)
        kk, vv, rr = (part(arenaB, 6144 + 2048 * i, DC * T, r="p (c t) -> p c t", c=DC) for i in range(3))
        first = part(small, 780, 16, r="p (i c b) -> p i c b", i=4, c=DC)
        w_qkv2 = part(arenaC, 0, DC * 768, r="p (c n) -> p c n", c=DC)
        w_dense = part(arenaC, 1536, DC * D, r="p (c n) -> p c n", c=DC)
        w_qkv3 = part(arenaC, 2048, DC * 768, r="p (c n) -> p c n", c=DC)
        w_out3 = part(arenaC, 3584, DC * D, r="p (c n) -> p c n", c=DC)
        qkv2 = part(arenaB, 0, NT * 768, r="p (t n) -> p t n", t=NT)
        rot = part(arenaB, 6144, 1024, r="p (t h e) -> p t h e", t=4, h=H2)
        prod = part(arenaB, 7168, 1024, r="p (t h e) -> p t h e", t=4, h=H2)
        ctx_tok = part(arenaB, 8192, NT * D, r="p (t n) -> p t n", t=NT)
        ctxT = part(arenaB, 10240, DC * T, r="p (c t) -> p c t", c=DC)
        tree = part(arenaB, 12288, 1024)
        sc2 = part(arenaB, 13312, 256, r="p (s u m) -> p s u m", s=2, u=2)
        mx2 = part(arenaB, 13568, 128, r="p (s m) -> p s m", s=2)
        wexp2 = [part(arenaD, 1536 * q, 1536, r="p (i c n) -> p i c n", i=3, c=DC) for q in range(2)]
        gu = [part(arenaC, 8704 + 2048 * q, DC * T, r="p (f t) -> p f t", f=DC) for q in range(2)]
        gs = [part(arenaC, 5184 + 512 * q, S) for q in range(2)]
        gate2 = part(small, 800, DC * E2, r="p (c e) -> p c e", c=DC)
        temp = part(small, 816, 1)
        z2, inh, dist, gw, fb, zone, cand, mask2 = (part(small, 820 + 64 * i, 64, r="p (t e) -> p t e", t=NT) for i in range(8))
        red8 = part(small, 1332, 48, r="p (i t) -> p i t", i=6)
        w_gate3 = part(arenaD, 3072, DC * FF, r="p (c n) -> p c n", c=DC)
        w_up3 = part(arenaD, 5120, DC * FF, r="p (c n) -> p c n", c=DC)
        w_down3 = part(arenaD, 7168, NF * D, r="p (f d) -> p f d", f=NF)
        had_b = part(arenaC, 6208, NF * D, r="p (f d) -> p f d", f=NF)
        qk3 = part(arenaC, 4096, NT * 512, r="p (t n) -> p t n", t=NT)
        v3 = part(arenaC, 8192, NT * D, r="p (t n) -> p t n", t=NT)
        prob3 = part(arenaC, 4096, 4096, r="p (q h n) -> p q h n", q=2, h=4)
        y3 = part(arenaC, 10240, 1024, r="p (i n) -> p i n", i=2)
        zinv = part(arenaC, 11264, 512)
        gs3 = [part(arenaC, 11776 + 512 * q, S) for q in range(2)]
        yT3 = part(arenaC, 0, DC * T, r="p (c t) -> p c t", c=DC)
        q3T = g_tok[:, :, :].rearrange("p a d -> p (a d)").rearrange("p (c t) -> p c t", c=DC)
        k3T = s_tok[:, :, :].rearrange("p a d -> p (a d)").rearrange("p (c t) -> p c t", c=DC)
        kz = part(arenaB, 0, 8192, r="p (c g t) -> p c g t", c=DC, g=8)
        hid3 = part(arenaB, 8192, NF * T, r="p (f t) -> p f t", f=NF)
        sq3 = part(arenaD, 0, 1024, r="p (q n) -> p q n", q=2)
        ms3 = part(small, 1380, 32)
        rms = sb("rms", [P, NT, 32])
        rmsr = sb("rmsr", [P, NT, 32])
        lam_in = sb("lam_in", [P, 4, 32])
        lam = part(small, 1420, 8)
        put_at = sb("put_at", [P, NT, 2], I32)
        get_at = sb("get_at", [P, NT, 2], I32)

        slots_d = nc.dram_tensor("slots", (NE * SLOTS, D), F32, kind="Internal").ap()
        rows_d = nc.dram_tensor("rows", (NE * SLOTS, D), F32, kind="Internal").ap()

        x_in, con_in, gate_in, wo_in = sem("x_in"), sem("con_in"), sem("gate_in"), sem("wo_in")
        wqkv_in = [sem(f"wqkv_in{q}") for q in range(2)]
        wexp_in = [sem(f"wexp_in{q}") for q in range(2)]
        xe_in = [sem(f"xe_in{q}") for q in range(2)]
        sw_in, x_out = sem("sw_in"), sem("x_out")
        slots_zero, slots_put, rows_got = sem("slots_zero"), sem("slots_put"), sem("rows_got")
        rows_out = [sem(f"rows_out{q}") for q in range(2)]
        dve_link, act_link, pool_link = sem("dve_link"), sem("act_link"), sem("pool_link")
        ones_set, zeros_set, mhalf_set = sem("ones_set"), sem("zeros_set"), sem("mhalf_set")
        ln_var, ln_rstd, xn_done = sem("ln_var"), sem("ln_rstd"), sem("xn_done")
        turn_ready, xnT_act, xnT_dve = sem("turn_ready"), sem("xnT_act"), sem("xnT_dve")
        logits_ready, lg_shift, ex_done = sem("logits_ready"), sem("lg_shift"), sem("ex_done")
        oh_done, place_ready, at_done = sem("oh_done"), sem("place_ready"), sem("at_done")
        proj_ready = sem("proj_ready")
        q_done, k_done, v_done = sem("q_done"), sem("k_done"), sem("v_done")
        score_ready, max_done, exp_done, acc_done = sem("score_ready"), sem("max_done"), sem("exp_done"), sem("acc_done")
        colsum_ready, vals_done = sem("colsum_ready"), sem("vals_done")
        s_ready, s_done = sem("s_ready"), sem("s_done")
        xeT_ready, xeT_done, hid_ready, hid_done = sem("xeT_ready"), sem("xeT_done"), sem("hid_ready"), sem("hid_done")
        y_ready, y_done = sem("y_ready"), sem("y_done")
        shid_ready, shid_done, sh_ready, sh_done = sem("shid_ready"), sem("shid_done"), sem("sh_ready"), sem("sh_done")
        w1_in, wlin_in, mix_done, kvr_ready = sem("w1_in"), sem("wlin_in"), sem("mix_done"), sem("kvr_ready")
        kr_done, vv_done, low_done, e_done, rwkv_done = sem("kr_done"), sem("vv_done"), sem("low_done"), sem("e_done"), sem("rwkv_done")
        wlin_done, g_ready, g_done, vec_in = sem("wlin_done"), sem("g_ready"), sem("g_done"), sem("vec_in")
        w2_in, w3_in, wff3_in = sem("w2_in"), sem("w3_in"), sem("wff3_in")
        had_ready, had_copied, had_done = sem("had_ready"), sem("had_copied"), sem("had_done")
        qkv_ready, qkv_done = sem("qkv_ready"), sem("qkv_done")
        z_ready, z_done, inh_done, dist_done, gexp_done = sem("z_ready"), sem("z_done"), sem("inh_done"), sem("dist_done"), sem("gexp_done")
        w2exp_in = [sem(f"w2exp_in{q}") for q in range(2)]
        gate_ready, up_ready, silu2_done, gu_done = sem("gate_ready"), sem("up_ready"), sem("silu2_done"), sem("gu_done")
        e2_ready, e2_done = sem("e2_ready"), sem("e2_done")
        sc_done, low2_done, sexp_done, prob2_done, ctx_done = sem("sc_done"), sem("low2_done"), sem("sexp_done"), sem("prob2_done"), sem("ctx_done")
        ctxT_ready, ctxT_done = sem("ctxT_ready"), sem("ctxT_done")
        ms_done, rms_done, qk_done = sem("ms_done"), sem("rms_done"), sem("qk_done")
        qkT_ready, qT_done, kT_done, kz_done = sem("qkT_ready"), sem("qT_done"), sem("kT_done"), sem("kz_done")
        gate3_ready, up3_ready, silu3_done, hid3_done = sem("gate3_ready"), sem("up3_ready"), sem("silu3_done"), sem("hid3_done")
        sc3_ready, exp3_done, causal_done, av_ready, norm3_done = sem("sc3_ready"), sem("exp3_done"), sem("causal_done"), sem("av_ready"), sem("norm3_done")
        g3_ready, lam_in_s, lam_exp, lam_sum = sem("g3_ready"), sem("lam_in_s"), sem("lam_exp"), sem("lam_sum")
        ffn_done, silu_done, x_done = sem("ffn_done"), sem("silu_done"), sem("x_done")

        EXP0, ACC0, VALS0, HID0, Y0, TURN0, ROWS0, GU0, E20 = 4, 4, 1, 3, 3, 2, 32, 2, 8

        block = ctx.enter_context(nc.Block())

        @block.sync
        def _(sp):
            sp.dma_start(x[:, :, :], a["x"].rearrange("(n p) d -> p n d", p=P)).then_inc(x_in, 16)
            sp.dma_start(con[:, :], a["con"]).then_inc(con_in, 16)
            sp.dma_start(gate, a["gate"].rearrange("p (c e) -> p c e", c=DC)).then_inc(gate_in, 16)
            sp.dma_start(part(small, 756, 16), a["vec"]).then_inc(vec_in, 16)
            sp.dma_start(part(small, 800, DC * E2), a["gate2"]).then_inc(vec_in, 16)
            sp.dma_start(temp, a["temp"].to_broadcast([P, 1])).then_inc(vec_in, 16)
            sp.dma_start(lam_in[:, :, :], a["lam"].to_broadcast([P, 128]).rearrange("p (i n) -> p i n", i=4)).then_inc(lam_in_s, 16)
            for h in range(2):
                sp.dma_start(wqkv[h], a["wqkv"][h].rearrange("p (c w) -> p c w", c=DC)).then_inc(wqkv_in[h], 16)
            sp.wait_ge(zeros_set, 1)
            sp.dma_start(slots_d.rearrange("(p n) d -> p n d", p=P),
                         arenaB[:, 0:NE * SLOTS // P * D].rearrange("p (n d) -> p n d", d=D)).then_inc(slots_zero, 16)
            sp.dma_start(wo, a["wo"].rearrange("p (h d) -> p h d", h=NH)).then_inc(wo_in, 16)

            def load_expert(e, q):
                sp.dma_start(wexp[q][:, 0:WPACK], a["wexp"][e]).then_inc(wexp_in[q], 16)
                sp.dma_start(wu[q], a["wu"][e]).then_inc(wexp_in[q], 16)
                sp.dma_start(b2[q], a["b2"][e].to_broadcast([P, D])).then_inc(wexp_in[q], 16)

            for e in range(2):
                load_expert(e, e)
            with sp.Fori(1, NH // 2) as pair:
                for q in range(2):
                    sp.wait_ge(proj_ready, 12 * pair + 6 * q - 6)
                    sp.dma_start(wqkv[q], a["wqkv"][bass.ds(2 * pair + q, 1)].rearrange("h p (c w) -> (h p) c w", c=DC)
                                 ).then_inc(wqkv_in[q], 16)

            def load_slots(e, q):
                r = a_slots(e)
                sp.dma_start(xe[q][:, 0:2, :], r[0:256, :].rearrange("(s p) d -> p s d", p=P)).then_inc(xe_in[q], 16)
                sp.dma_start(xe[q][0:SROWS[2], 2, :], r[256:SLOTS, :]).then_inc(xe_in[q], 16)

            def a_slots(e):
                if isinstance(e, int):
                    return slots_d[e * SLOTS:(e + 1) * SLOTS, :]
                return slots_d.rearrange("(e r) d -> e r d", e=NE)[bass.ds(e, 1)].rearrange("e r d -> (e r) d")

            sp.wait_ge(vals_done, VALS0 + 2 * NH)
            sp.wait_ge(slots_put, 16 * 2 * NT)
            for e in range(2):
                load_slots(e, e)
            sp.wait_ge(s_done, NT // 2)
            sp.dma_start(sw[:, 0:WPACK], a["sw"]).then_inc(sw_in, 16)
            sp.dma_start(swu, a["swu"]).then_inc(sw_in, 16)
            sp.dma_start(sb2, a["sb2"].to_broadcast([P, D])).then_inc(sw_in, 16)

            rows_e = rows_d.rearrange("(e r) d -> e r d", e=NE)

            def store_rows(e, q):
                sp.wait_ge(y_done, Y0 + 3 * e + 3)
                r = rows_e[bass.ds(e, 1)].rearrange("e r d -> (e r) d")
                sp.dma_start(r[0:256, :].rearrange("(s p) d -> p s d", p=P), yE[q][:, 0:2, :]).then_inc(rows_out[q], 16)
                sp.dma_start(r[256:SLOTS, :], yE[q][0:SROWS[2], 2, :]).then_inc(rows_out[q], 16)

            with sp.Fori(0, NE // 2 - 1) as pair:
                for q in range(2):
                    store_rows(2 * pair + q, q)
                    load_expert(2 * pair + 2 + q, q)
                    load_slots(2 * pair + 2 + q, q)
            for q in range(2):
                store_rows(NE - 2 + q, q)

            if layers > 1:
                sp.dma_start(w_rwkv, a["w_rwkv"].rearrange("p (i c o) -> p i c o", i=4, c=DC)).then_inc(w1_in, 16)
                sp.dma_start(part(arenaC, 4160, DC * D), a["w_lin"]).then_inc(wlin_in, 16)
                sp.dma_start(lin_scale, a["lin_scale"].to_broadcast([P, D])).then_inc(wlin_in, 16)
                sp.dma_start(lin_bias, a["lin_bias"].to_broadcast([P, D])).then_inc(wlin_in, 16)
            if layers > 2:
                sp.wait_ge(x_done, NT // 2)
                sp.dma_start(part(arenaD, 7168, NF * D), a["w_down3"]).then_inc(wff3_in, 16)
                sp.dma_start(part(arenaC, 0, 2048), a["w2"]).then_inc(w2_in, 16)
                for q in range(2):
                    sp.dma_start(wexp2[q], a["wexp2"][q].rearrange("p (i c n) -> p i c n", i=3, c=DC)).then_inc(w2exp_in[q], 16)
                sp.dma_start(part(arenaC, 2048, 2048), a["w3"]).then_inc(w3_in, 16)
                sp.dma_start(part(arenaD, 3072, 4096), a["wff3"]).then_inc(w3_in, 16)
                with sp.Fori(1, E2 // 2) as pair:
                    for q in range(2):
                        sp.wait_ge(e2_ready, 16 * pair + 8 * q - 8)
                        sp.dma_start(wexp2[q], a["wexp2"][bass.ds(2 * pair + q, 1)].rearrange("e p (i c n) -> (e p) i c n", i=3, c=DC)
                                     ).then_inc(w2exp_in[q], 16)
            sp.wait_ge(x_done, layers * NT // 2)
            sp.dma_start(out.rearrange("(n p) d -> p n d", p=P), x[:, :, :]).then_inc(x_out, 16)
            sp.wait_ge(x_out, 16)

        @block.gpsimd
        def _(pool):
            pool.memset(mhalf[:, :], -0.5).then_inc(mhalf_set, 1)
            pool.memset(ones[:, :], 1.0).then_inc(ones_set, 1)
            pool.memset(arenaB[:, 0:NE * SLOTS // P * D], 0.0).then_inc(zeros_set, 1)
            for q in range(2):
                pool.sem_inc(rows_out[q], ROWS0)

            def rsqrt(layer):
                pool.wait_ge(mhalf_set, 1)
                pool.wait_ge(ln_var, layer + 1)
                pool.tensor_tensor(rstd[:, :], veps[:, :], mhalf[:, 0:NT], ALU.pow).then_inc(ln_rstd, 1)

            def rotary_attention():
                def heads(s0, which):
                    return qkv2[:, 4 * s0:4 * s0 + 4, which * D:(which + 1) * D]

                def table(at, half=None):
                    v = con[:, at:at + D]
                    if half is None:
                        return v.unsqueeze(1).to_broadcast([P, 4, D])
                    return v.rearrange("p (h two i) -> p h two i", h=H2, two=2)[:, :, half, :].unsqueeze(1).to_broadcast([P, 4, H2, 8])

                def halves(v, half):
                    return v.rearrange("p t (h two i) -> p t h two i", h=H2, two=2)[:, :, :, half, :]

                pool.wait_ge(qkv_done, 2 * NT)
                r3, p3 = (m.rearrange("p t h e -> p t (h e)") for m in (rot, prod))
                for which in range(2):
                    v = heads(1, which)
                    for half in range(2):
                        link(pool.tensor_tensor(halves(r3, half), halves(v, 1 - half), table(C_SIN, half), ALU.mult))
                    link(pool.tensor_tensor(v, v, table(C_COS), ALU.mult))
                    link(pool.tensor_tensor(v, v, r3, ALU.add))
                link(pool.memset(sc2[:, 0, 1, :], 4.0 * BLOCKED))
                for s0, u0 in ((0, 0), (1, 0), (1, 1)):
                    link(pool.tensor_tensor(p3, heads(s0, 0), heads(u0, 1), ALU.mult))
                    src = p3.rearrange("p t (h e) -> p (t h) e", h=H2)
                    for lv, w in enumerate((8, 4, 2, 1)):
                        dst = tree[:, 0:64 * w].rearrange("p (m e) -> p m e", e=w) if w > 1 and lv % 2 == 0 else \
                            tree[:, 512:512 + 64 * w].rearrange("p (m e) -> p m e", e=w) if w > 1 else \
                            sc2[:, s0, u0, :].unsqueeze(2)
                        link(pool.tensor_tensor(dst, src[:, :, 0:w], src[:, :, w:2 * w], ALU.add))
                        src = dst
                pool.tensor_scalar(sc2, sc2, HD2 ** -0.5, None, ALU.mult).then_inc(sc_done, 1)
                pool.wait_ge(prob2_done, 2)
                for s0 in range(2):
                    for u0 in range(2):
                        w = sc2[:, s0, u0, :].rearrange("p (t h) -> p t h", h=H2).unsqueeze(3).to_broadcast([P, 4, H2, HD2])
                        v = heads(u0, 2).rearrange("p t (h e) -> p t h e", h=H2)
                        link(pool.tensor_tensor(rot if u0 == 0 else prod, v, w, ALU.mult))
                    pool.tensor_tensor(ctx_tok[:, 4 * s0:4 * s0 + 4, :], r3, p3, ALU.add).then_inc(ctx_done, 1)
                    pool.wait_ge(ctx_done, s0 + 1)

            link = Link(pool, pool_link)
            rsqrt(0)
            pool.wait_ge(at_done, 2)
            pool.wait_ge(slots_zero, 16)
            for t in range(NT):
                for k in range(2):
                    pool.indirect_dma_start(out=slots_d, out_offset=bass.IndirectOffsetOnAxis(put_at[:, t, k:k + 1], 0),
                                            in_=xn[:, t, :], in_offset=None, bounds_check=NE * SLOTS - 1,
                                            oob_is_err=False).then_inc(slots_put, 16)
            for q in range(2):
                pool.wait_ge(rows_out[q], ROWS0 + 32 * NE // 2)
            for t in range(NT):
                for k in range(2):
                    pool.indirect_dma_start(out=got[k][:, t, :], out_offset=None, in_=rows_d,
                                            in_offset=bass.IndirectOffsetOnAxis(get_at[:, t, k:k + 1], 0),
                                            bounds_check=NE * SLOTS - 1, oob_is_err=False).then_inc(rows_got, 16)

            if layers > 1:
                rsqrt(1)
            if layers > 2:
                pool.wait_ge(had_copied, 4)
                for stage, (src, dst) in enumerate([(had_b, w_down3), (w_down3, had_b), (had_b, w_down3)]):
                    step = 1 << stage
                    v = [m.rearrange("p (u two w) d -> p u two (w d)", two=2, w=step) for m in (src, dst)]
                    pool.tensor_tensor(v[1][:, :, 0], v[0][:, :, 0], v[0][:, :, 1], ALU.add).then_inc(had_done, 1)
                    pool.tensor_tensor(v[1][:, :, 1], v[0][:, :, 0], v[0][:, :, 1], ALU.subtract).then_inc(had_done, 1)
                    pool.wait_ge(had_done, 2 * stage + 2)
                rsqrt(2)
                rotary_attention()
            if layers > 3:
                rsqrt(3)
                for t in range(NT):
                    pool.wait_ge(ms_done, t + 1)
                    pool.tensor_tensor(rmsr[:, t, :], rms[:, t, :], mhalf[:, 0:32], ALU.pow).then_inc(rms_done, 1)
                for u in range(32):
                    pool.wait_ge(exp3_done, 4 * u + 4)
                    d = prob3[:, u % 2, :, 0:P]
                    pool.tensor_tensor(d, d, con[:, C_CAUSAL:C_CAUSAL + P].unsqueeze(1).to_broadcast([P, 4, P]), ALU.mult
                                       ).then_inc(causal_done, 1)

        @block.tensor
        def _(pe):
            def turn_xn(layer):
                pe.wait_ge(con_in, 16)
                for t in range(NT):
                    pe.wait_ge(xn_done, NT * layer + t + 1)
                    for c in range(DC):
                        o = bank[t // 2][:, (t % 2) * 256 + c * P:(t % 2) * 256 + (c + 1) * P]
                        mm = pe.transpose(o, xn[:, t, c * P:(c + 1) * P], ident)
                    mm.then_inc(turn_ready, 1)
                pe.wait_ge(xnT_act, 2 * layer + 2)
                pe.wait_ge(xnT_dve, 2 * layer + 2)

            turn_xn(0)
            pe.wait_ge(gate_in, 16)
            for t in range(NT):
                for c in range(DC):
                    mm = pe.matmul(bank[7][:, t * NE:(t + 1) * NE], xnT[:, c, t * P:(t + 1) * P], gate[:, c, :],
                                   start=(c == 0), stop=(c == DC - 1))
            mm.then_inc(logits_ready, 1)

            PROJ = [(0, 0), (1, 0), (0, 1), (1, 1), (2, 0), (2, 1)]

            def project_tile(h, q, n, first=False):
                w, b = PROJ[n]
                if not first or n >= 3:
                    s, v = [(k_done, 2 * h), (v_done, 2 * h - 1), (v_done, 2 * h),
                            (q_done, 2 * h + 1), (k_done, 2 * h + 1), (q_done, 2 * h + 2)][n]
                    pe.wait_ge(s, v)
                for c in range(DC):
                    mm = pe.matmul(bank[n % 3][:, :], wqkv[q][:, c, w * DH:(w + 1) * DH], xnT[:, c, b * S:(b + 1) * S],
                                   start=(c == 0), stop=(c == DC - 1))
                mm.then_inc(proj_ready, 1)

            def projecting(h, q, pair):
                def go(n):
                    if n == 0:
                        pe.wait_ge(wqkv_in[q], 16 * pair + 16)
                    project_tile(h, q, n)
                return go

            def score(h, q, n):
                b = n // ST
                if n % ST == 0:
                    pe.wait_ge(q_done, 2 * h + 1 + b)
                    pe.wait_ge(k_done, 2 * h + 1 + b)
                pe.wait_ge(exp_done, 8 * h + n + 1)
                pe.matmul(bank[3 + n % 4][:, :], qT[q][:, n * P:(n + 1) * P], kT[q][:, b * S:(b + 1) * S],
                          start=True, stop=True).then_inc(score_ready, 1)

            def colsum(h, b):
                pe.wait_ge(acc_done, ACC0 + 8 * h + 4 * b + 4)
                pe.wait_ge(vals_done, 2 * h + b + 1)
                pe.matmul(bank[7][:, :], ones[:, :], acc[b], start=True, stop=True).then_inc(colsum_ready, 1)

            def head(h, q, nxt):
                for n in range(4):
                    score(h, q, n)
                for n in range(4):
                    if nxt:
                        nxt(n)
                    score(h, q, 4 + n)
                if nxt:
                    nxt(4)
                colsum(h, 0)
                if nxt:
                    nxt(5)
                colsum(h, 1)

            pe.wait_ge(wqkv_in[0], 16)
            for n in range(6):
                project_tile(0, 0, n, first=True)
            pe.wait_ge(ones_set, 1)
            pe.wait_ge(oh_done, 1)
            pe.matmul(bank[7][:, 0:128], con[:, C_TRI:C_TRI + P], oh.rearrange("p t k e -> p (t k e)"), start=True, stop=False)
            pe.matmul(bank[7][:, 0:128], ones[:, :], before.rearrange("p t k e -> p (t k e)"), start=False, stop=True
                      ).then_inc(place_ready, 1)
            with pe.Fori(0, NH // 2 - 1) as pair:
                head(2 * pair, 0, projecting(2 * pair + 1, 1, pair))
                head(2 * pair + 1, 1, projecting(2 * pair + 2, 0, pair + 1))
            head(NH - 2, 0, projecting(NH - 1, 1, NH // 2 - 1))
            head(NH - 1, 1, None)

            pe.wait_ge(wo_in, 16)
            pe.wait_ge(vals_done, VALS0 + 2 * NH)
            for t in range(NT):
                for h in range(NH):
                    mm = pe.matmul(bank[t // 2][:, (t % 2) * D:(t % 2 + 1) * D], vals[:, h, t * P:(t + 1) * P], wo[:, h, :],
                                   start=(h == 0), stop=(h == NH - 1))
                mm.then_inc(s_ready, 1)

            pe.wait_ge(s_done, NT // 2)

            def turn(e, pair, q):
                pe.wait_ge(xe_in[q], 32 * pair + 32)
                pe.wait_ge(xeT_done, 2 * e + 2)
                for c in range(DC):
                    for s, rows in enumerate(SROWS):
                        mm = pe.transpose(bank[c][:, s * P:s * P + rows], xe[q][0:rows, s, c * P:(c + 1) * P],
                                          ident[0:rows, 0:rows])
                    mm.then_inc(xeT_ready, 1)

            def hidden(e, pair, q):
                pe.wait_ge(wexp_in[q], 48 * pair + 48)
                pe.wait_ge(xeT_done, 2 * e + 4)
                for f in range(NF + 1):
                    pe.wait_ge(hid_done, 9 * e + f + 1)
                    for c in range(DC):
                        w = w1[q][:, c, f * P:(f + 1) * P] if f < NF else wd[q][:, c, :]
                        m = P if f < NF else RANK
                        mm = pe.matmul(bank[2 + f % 3][0:m, 0:SLOTS], w, xeT[q][:, c, :], start=(c == 0), stop=(c == DC - 1))
                    mm.then_inc(hid_ready, 1)

            def rows_of(e, pair, q):
                pe.wait_ge(hid_done, HID0 + 9 * e + 9)
                for s, rows in enumerate(SROWS):
                    pe.wait_ge(y_done, 3 * e + s + 1)
                    o = bank[5 + s][0:rows, 0:D]
                    for f in range(NF):
                        pe.matmul(o, hE[:, f, s * P:s * P + rows], w2[q][:, f, :], start=(f == 0), stop=False)
                    pe.matmul(o, aE[:, s * P:s * P + rows], wu[q], start=False, stop=True).then_inc(y_ready, 1)

            turn(0, 0, 0)
            with pe.Fori(0, NE // 2 - 1) as pair:
                for q in range(2):
                    e = 2 * pair + q
                    hidden(e, pair, q)
                    turn(e + 1, pair + q, 1 - q)
                    rows_of(e, pair, q)
            hidden(NE - 2, NE // 2 - 1, 0)
            turn(NE - 1, NE // 2 - 1, 1)
            rows_of(NE - 2, NE // 2 - 1, 0)
            hidden(NE - 1, NE // 2 - 1, 1)
            rows_of(NE - 1, NE // 2 - 1, 1)

            pe.wait_ge(sw_in, 48)
            for f in range(NF + 1):
                for b in range(B):
                    n = B * f + b
                    if n >= 4:
                        pe.wait_ge(shid_done, n - 3)
                    for c in range(DC):
                        w = sw1[:, c, f * P:(f + 1) * P] if f < NF else swd[:, c, :]
                        m = P if f < NF else RANK
                        mm = pe.matmul(bank[n % 4][0:m, :], w, xnT[:, c, b * S:(b + 1) * S], start=(c == 0), stop=(c == DC - 1))
                    mm.then_inc(shid_ready, 1)
            pe.wait_ge(shid_done, B * (NF + 1))
            pe.wait_ge(y_done, Y0 + 3 * NE)
            for t in range(NT):
                o = bank[4 + t // 2][:, (t % 2) * D:(t % 2 + 1) * D]
                for f in range(NF):
                    pe.matmul(o, hS[:, f, t * P:(t + 1) * P], sw2[:, f, :], start=(f == 0), stop=False)
                pe.matmul(o, aS[:, t * P:(t + 1) * P], swu, start=False, stop=True).then_inc(sh_ready, 1)


            def token_major(lhs, w, first_bank, free, ready):
                for t in range(NT):
                    if free and t % 2 == 0:
                        free(t // 2)
                    for c in range(DC):
                        mm = pe.matmul(bank[first_bank + t // 2][:, (t % 2) * D:(t % 2 + 1) * D], lhs[:, c, t * P:(t + 1) * P],
                                       w[:, c, :], start=(c == 0), stop=(c == DC - 1))
                    mm.then_inc(ready, 1)

            def qkv_rows(w, layer):
                for t in range(NT):
                    if t >= 3:
                        pe.wait_ge(qkv_done, 2 * (NT * (layer - 2) + t) - 4)
                    b0 = 2 * (t % 3)
                    for o, w0, n in ((bank[b0][:, :], 0, 512), (bank[b0 + 1][:, 0:D], 512, D)):
                        for c in range(DC):
                            mm = pe.matmul(o, xnT[:, c, t * P:(t + 1) * P], w[:, c, w0:w0 + n], start=(c == 0), stop=(c == DC - 1))
                    mm.then_inc(qkv_ready, 1)

            if layers > 1:
                turn_xn(1)
                pe.wait_ge(w1_in, 16)
                n = 0
                for b in range(B):
                    for i in range(3):
                        pe.wait_ge(mix_done, 3 * b + i + 1)
                        for o in range(DC):
                            if n >= 4:
                                m = n - 4
                                bb_, ii, oo = m // 6, m % 6 // 2, m % 2
                                if ii == 1:
                                    pe.wait_ge(vv_done, 2 * bb_ + oo + 1)
                                else:
                                    pe.wait_ge(kr_done, 4 * bb_ + (2 if ii else 0) + oo + 1)
                            for c in range(DC):
                                mm = pe.matmul(bank[4 + n % 4][:, :], w_rwkv[:, i, c, o * P:(o + 1) * P],
                                               mixed[:, i, c, b * S:(b + 1) * S], start=(c == 0), stop=(c == DC - 1))
                            mm.then_inc(kvr_ready, 1)
                            n += 1
                pe.wait_ge(wlin_done, 1)
                token_major(xnT, w_lin, 0, None, g_ready)
                pe.wait_ge(kr_done, 8)
                pe.wait_ge(rwkv_done, 2)
                token_major(rr, w_rwkv[:, 3], 4, None, s_ready)
            if layers > 2:
                pe.wait_ge(g_done, 4)
                pe.wait_ge(wff3_in, 16)
                for i in range(4):
                    pe.matmul(bank[i][:, :], con[:, C_HAD:C_HAD + P], w_down3[:, 2 * i:2 * i + 2, :].rearrange("p f d -> p (f d)"),
                              start=True, stop=True).then_inc(had_ready, 1)
                pe.wait_ge(had_copied, 4)
                turn_xn(2)
                for t in range(NT):
                    for c in range(DC):
                        mm = pe.matmul(bank[7][:, t * E2:(t + 1) * E2], xnT[:, c, t * P:(t + 1) * P], gate2[:, c, :],
                                       start=(c == 0), stop=(c == DC - 1))
                mm.then_inc(z_ready, 1)
                pe.wait_ge(w2_in, 16)
                qkv_rows(w_qkv2, 2)
                pe.wait_ge(qkv_done, 2 * NT)
                pe.wait_ge(z_done, 1)

                def gate_up(e, pair, q):
                    pe.wait_ge(w2exp_in[q], 16 * pair + 16)
                    for n in range(4):
                        f, b = n // 2, n % 2
                        for i, (rdy, done) in enumerate(((gate_ready, silu2_done), (up_ready, gu_done))):
                            pe.wait_ge(done, 4 * e + n + 1)
                            for c in range(DC):
                                mm = pe.matmul(bank[2 * i + n % 2][:, :], wexp2[q][:, i, c, f * P:(f + 1) * P],
                                               xnT[:, c, b * S:(b + 1) * S], start=(c == 0), stop=(c == DC - 1))
                            mm.then_inc(rdy, 1)

                def down(e, q):
                    pe.wait_ge(gu_done, GU0 + 4 * e + 4)
                    for t in range(NT):
                        if t % 2 == 0:
                            pe.wait_ge(e2_done, 8 * e + t + 2)
                        for f in range(DC):
                            mm = pe.matmul(bank[4 + t // 2][:, (t % 2) * D:(t % 2 + 1) * D], gu[q][:, f, t * P:(t + 1) * P],
                                           wexp2[q][:, 2, f, :], start=(f == 0), stop=(f == DC - 1))
                        mm.then_inc(e2_ready, 1)

                gate_up(0, 0, 0)
                with pe.Fori(0, E2 // 2 - 1) as pair:
                    for q in range(2):
                        gate_up(2 * pair + q + 1, pair + q, 1 - q)
                        down(2 * pair + q, q)
                gate_up(E2 - 1, E2 // 2 - 1, 1)
                down(E2 - 2, 0)
                pe.wait_ge(gu_done, GU0 + 4 * E2)
                pe.wait_ge(ctx_done, 2)
                for t in range(NT):
                    for c in range(DC):
                        mm = pe.transpose(bank[t // 2][:, (t % 2) * 256 + c * P:(t % 2) * 256 + (c + 1) * P],
                                          ctx_tok[:, t, c * P:(c + 1) * P], ident)
                    mm.then_inc(ctxT_ready, 1)
                down(E2 - 1, 1)
                pe.wait_ge(ctxT_done, 4)
                token_major(ctxT, w_dense, 0, None, s_ready)
            if layers > 3:
                turn_xn(3)
                pe.wait_ge(w3_in, 32)
                qkv_rows(w_qkv3, 3)
                pe.wait_ge(qkv_done, 4 * NT)

                def turn_qk(t):
                    pe.wait_ge(qk_done, t + 1)
                    if t >= 4:
                        pe.wait_ge(qT_done, t - 3)
                        pe.wait_ge(kT_done, t - 3)
                    for j in range(4):
                        mm = pe.transpose(bank[4 + t % 4][:, j * P:(j + 1) * P], qk3[:, t, j * P:(j + 1) * P], ident)
                    mm.then_inc(qkT_ready, 1)

                for n in range(2 * NF):
                    f, b = n // 2, n % 2
                    for i, (w, rdy, done) in enumerate(((w_gate3, gate3_ready, silu3_done), (w_up3, up3_ready, hid3_done))):
                        if n >= 2:
                            pe.wait_ge(done, n - 1)
                        for c in range(DC):
                            mm = pe.matmul(bank[2 * i + n % 2][:, :], w[:, c, f * P:(f + 1) * P], xnT[:, c, b * S:(b + 1) * S],
                                           start=(c == 0), stop=(c == DC - 1))
                        mm.then_inc(rdy, 1)
                    if n >= 6 and n % 2 == 0 and (n - 6) // 2 < 5:
                        turn_qk((n - 6) // 2)
                for t in range(5, NT):
                    turn_qk(t)
                pe.wait_ge(qT_done, NT)
                pe.wait_ge(kT_done, NT)
                pe.wait_ge(silu3_done, 2 * NF)
                pe.wait_ge(hid3_done, 2 * NF)

                def unit(u):
                    return u // 16, u // 8 % 2, u // 4 % 2, u % 4

                def scores3(u):
                    b, c, j, kt = unit(u)
                    if u % 8 == 0:
                        pe.wait_ge(kz_done, 8 * (u // 8) + 8)
                    for hh in range(4):
                        if u:
                            pe.wait_ge(exp3_done, 4 * u - 3 + hh)
                        pe.matmul(bank[hh][:, 0:S - kt * P], kz[:, c, 2 * hh + j, kt * P:(kt + 1) * P],
                                  q3T[:, c, b * S + kt * P:(b + 1) * S], start=True, stop=True).then_inc(sc3_ready, 1)

                def mix3(u):
                    b, c, j, kt = unit(u)
                    pe.wait_ge(causal_done, u + 1)
                    if kt == 0 and u >= 8:
                        pe.wait_ge(norm3_done, u // 4 - 1)
                    for o, which in ((bank[4 + j], 0), (bank[6 + j], 1)):
                        for hh in range(4):
                            head = 4 * c + hh
                            w = ones[:, 0:32] if which else v3[:, ST * b + kt, 32 * head:32 * head + 32]
                            mm = pe.matmul(o[32 * hh:32 * hh + 32, kt * P:S], w, prob3[:, u % 2, hh, 0:S - kt * P],
                                           start=(kt == 0), stop=(kt == ST - 1), tile_position=(0, 32 * hh))
                    mm.then_inc(av_ready, 1)

                scores3(0)
                for u in range(32):
                    if u < 31:
                        scores3(u + 1)
                    mix3(u)
                pe.wait_ge(had_done, 6)
                for t in range(NT):
                    for f in range(NF):
                        mm = pe.matmul(bank[t // 2][:, (t % 2) * D:(t % 2 + 1) * D], hid3[:, f, t * P:(t + 1) * P], w_down3[:, f, :],
                                       start=(f == 0), stop=(f == NF - 1))
                    mm.then_inc(g3_ready, 1)
                pe.wait_ge(norm3_done, 8)
                token_major(yT3, w_out3, 4, None, s_ready)

        @block.vector
        def _(dve):
            link = Link(dve, dve_link)
            dve.sem_inc(vals_done, VALS0)
            dve.sem_inc(y_done, Y0)
            dve.sem_inc(acc_done, ACC0)

            def layernorm(layer):
                for t in range(NT):
                    ins = dve.bn_stats(stats[:, t, :], x[:, t, :])
                link(ins)
                for t in range(NT):
                    ins = dve.bn_aggr(meanvar[:, t, :], stats[:, t, :])
                link(ins)
                dve.tensor_scalar(veps[:, :], meanvar[:, :, 1], LN_EPS, None, ALU.add).then_inc(ln_var, 1)
                dve.wait_ge(ln_rstd, layer + 1)
                for t in range(NT):
                    dve.tensor_scalar(xn[:, t, :], x[:, t, :], meanvar[:, t, 0:1], rstd[:, t:t + 1],
                                      ALU.subtract, ALU.mult).then_inc(xn_done, 1)
                for i in (1, 3):
                    dve.wait_ge(turn_ready, NT * layer + 2 * i + 2)
                    dve.tensor_copy(xnT[:, :, i * 256:(i + 1) * 256].rearrange("p c (t n) -> p t c n", t=2),
                                    bank[i][:, :].rearrange("p (t c n) -> p t c n", t=2, c=DC)).then_inc(xnT_dve, 1)

            dve.wait_ge(x_in, 16)
            layernorm(0)

            def bc(v):
                return v.unsqueeze(2).to_broadcast([P, NT, NE])

            iota = con[:, C_IOTA:C_IOTA + 64].rearrange("p (t e) -> p t e", t=NT)
            dve.wait_ge(con_in, 16)
            dve.wait_ge(logits_ready, 1)
            link(dve.tensor_copy(lg, bank[7][:, 0:64].rearrange("p (t e) -> p t e", t=NT)))

            def choose(k):
                link(dve.tensor_reduce(top[:, k, :], lg, AX.X, ALU.max))
                link(dve.tensor_tensor(eq, lg, bc(top[:, k, :]), ALU.is_equal))
                link(dve.tensor_tensor(eq, eq, iota, ALU.mult))
                link(dve.tensor_reduce(idx[:, :, k], eq, AX.X, ALU.min))
                link(dve.tensor_tensor(oh[:, :, k, :], iota, bc(idx[:, :, k]), ALU.is_equal))

            choose(0)
            dve.tensor_tensor(ex, lg, bc(top[:, 0, :]), ALU.subtract).then_inc(lg_shift, 1)
            link(dve.scalar_tensor_tensor(lg, oh[:, :, 0, :], OUT_OF_REACH, lg, ALU.mult, ALU.add))
            choose(1)
            dve.tensor_tensor(gap, top[:, 1, :], top[:, 0, :], ALU.subtract).then_inc(lg_shift, 1)
            dve.memset(before[:, 0, :, :], 0.0)
            for t in range(1, NT):
                if t == 1:
                    link(dve.tensor_copy(before[:, 1, :, :], oh[:, 0, :, :]))
                else:
                    link(dve.tensor_tensor(before[:, t, :, :], before[:, t - 1, :, :], oh[:, t - 1, :, :], ALU.add))
            dve.memset(kslot[:, :, 0], 8.0 * SLOTS).then_inc(oh_done, 1)
            link(dve.memset(kslot[:, :, 1], 8.0 * SLOTS + CAP))
            def keys(h, q, b):
                dve.wait_ge(proj_ready, 6 * h + 2 + 2 * b)
                dve.tensor_copy(kT[q][:, b * S:(b + 1) * S], bank[0 if b else 1][:, :]).then_inc(k_done, 1)

            keys(0, 0, 0)
            keys(0, 0, 1)
            dve.wait_ge(place_ready, 1)
            link(dve.tensor_tensor(ohp.rearrange("p t k e -> p (t k e)"), oh.rearrange("p t k e -> p (t k e)"),
                                   bank[7][:, 0:128], ALU.mult))
            link(dve.tensor_reduce(pos.rearrange("p t k -> p (t k)"), ohp.rearrange("p t k e -> p (t k) e"), AX.X, ALU.add))
            link(dve.tensor_scalar(keep, pos, float(CAP), None, ALU.is_lt))
            link(dve.scalar_tensor_tensor(base, idx, float(SLOTS), kslot, ALU.mult, ALU.add))
            link(dve.tensor_tensor(slot, base, pos, ALU.add))
            link(dve.scalar_tensor_tensor(slot, keep, -NO_SLOT, slot, ALU.mult, ALU.add))
            dve.tensor_scalar(put_at[:, :, :], slot, NO_SLOT, None, ALU.add).then_inc(at_done, 1)
            link(dve.tensor_scalar(pos, pos, CAP - 1.0, None, ALU.min))
            dve.tensor_tensor(get_at[:, :, :], base, pos, ALU.add).then_inc(at_done, 1)
            dve.wait_ge(ex_done, 2)
            link(dve.tensor_reduce(esum, ex, AX.X, ALU.add))
            link(dve.reciprocal(einv, esum))
            link(dve.tensor_tensor(wt[:, :, 0], keep[:, :, 0], einv, ALU.mult))
            link(dve.tensor_tensor(wt[:, :, 1], keep[:, :, 1], einv, ALU.mult))
            link(dve.tensor_tensor(wt[:, :, 1], wt[:, :, 1], gap, ALU.mult))

            def row_max(h, n):
                dve.wait_ge(score_ready, 8 * h + n + 1)
                dve.tensor_reduce(negmax[:, n % 4:n % 4 + 1], bank[3 + n % 4][:, :], AX.X, ALU.max, negate=True
                                  ).then_inc(max_done, 1)

            def accumulate(h, n):
                r = n % 4
                dve.wait_ge(exp_done, EXP0 + 8 * h + n + 1)
                link(dve.reciprocal(rowinv[:, r:r + 1], rowsum[:, r:r + 1]))
                if n % ST == 0:
                    ins = dve.tensor_scalar(acc[n // ST], prob[r], rowinv[:, r:r + 1], None, ALU.mult)
                else:
                    ins = dve.scalar_tensor_tensor(acc[n // ST], prob[r], rowinv[:, r:r + 1], acc[n // ST], ALU.mult, ALU.add)
                ins.then_inc(acc_done, 1)
                dve.wait_ge(acc_done, ACC0 + 8 * h + n + 1)

            def values(h, q, b):
                dve.wait_ge(colsum_ready, 2 * h + b + 1)
                dve.wait_ge(v_done, 2 * h + b + 1)
                o = vals[:, h, b * S:(b + 1) * S] if isinstance(h, int) else \
                    vals[:, bass.ds(h, 1), b * S:(b + 1) * S].rearrange("p h t -> p (h t)")
                dve.tensor_tensor(o, bank[7][:, :], vT[q][:, b * S:(b + 1) * S], ALU.mult).then_inc(vals_done, 1)

            def head(h, q, nxt):
                row_max(h, 0)
                for n in range(1, 8):
                    row_max(h, n)
                    accumulate(h, n - 1)
                    if nxt and n in (4, 6):
                        keys(h + 1, 1 - q, n // 2 - 2)
                accumulate(h, 7)
                values(h, q, 0)
                values(h, q, 1)

            dve.wait_ge(slots_zero, 16)
            turns = NH // 2 - 1
            with dve.Fori(0, turns) as pair:
                link.loop(pair, 16)
                head(2 * pair, 0, True)
                head(2 * pair + 1, 1, True)
            link.end(turns)
            head(NH - 2, 0, True)
            head(NH - 1, 1, False)
            for i in (1, 3):
                dve.wait_ge(s_ready, 2 * i + 2)
                dve.tensor_copy(s_tok[:, 2 * i:2 * i + 2, :].rearrange("p a d -> p (a d)"), bank[i][:, :]).then_inc(s_done, 1)

            with dve.Fori(0, NE // 2) as pair:
                for q in range(2):
                    e = 2 * pair + q
                    dve.wait_ge(xeT_ready, 2 * e + 2)
                    dve.tensor_copy(xeT[q][:, 1, :], bank[1][:, 0:SLOTS]).then_inc(xeT_done, 1)
                    dve.wait_ge(rows_out[q], 32 * pair + 32)
                    for s, rows in enumerate(SROWS):
                        dve.wait_ge(y_ready, 3 * e + s + 1)
                        dve.tensor_tensor(yE[q][0:rows, s, :], bank[5 + s][0:rows, 0:D], b2[q][0:rows, :], ALU.add
                                          ).then_inc(y_done, 1)
            for i in range(NT // 2):
                dve.wait_ge(sh_ready, 2 * i + 2)
                dve.tensor_tensor(g_tok[:, 2 * i:2 * i + 2, :], bank[4 + i][:, :].rearrange("p (t d) -> p t d", t=2),
                                  sb2.unsqueeze(1).to_broadcast([P, 2, D]), ALU.add).then_inc(sh_done, 1)
            dve.wait_ge(sh_done, NT // 2)
            link(dve.tensor_scalar(g_tok[:, :, :], g_tok[:, :, :], 0.2, None, ALU.mult))
            dve.wait_ge(rows_got, 16 * 2 * NT)
            for k in range(2):
                for t in range(NT):
                    ins = dve.scalar_tensor_tensor(g_tok[:, t, :], got[k][:, t, :], wt[:, t, k:k + 1], g_tok[:, t, :],
                                                   ALU.mult, ALU.add)
                link(ins)
            dve.sem_inc(ffn_done, 1)

            def residual(layer):
                dve.wait_ge(silu_done, layer + 1)
                dve.wait_ge(s_done, (layer + 1) * NT // 2)
                link(dve.tensor_tensor(g_tok[:, :, :], g_tok[:, :, :], s_tok[:, :, :], ALU.mult))
                for i in range(NT // 2):
                    ins = dve.tensor_tensor(x[:, 2 * i:2 * i + 2, :], x[:, 2 * i:2 * i + 2, :], g_tok[:, 2 * i:2 * i + 2, :], ALU.add)
                    ins.then_inc(x_done, 1)
                link(dve.memset(veps[:, :], 0.0))

            def golden():
                def per(v):
                    return v.unsqueeze(2).to_broadcast([P, NT, E2])

                dve.wait_ge(vec_in, 48)
                dve.wait_ge(z_ready, 1)
                link(dve.reciprocal(temp, temp))
                link(dve.tensor_scalar(z2, bank[7][:, 0:64].rearrange("p (t e) -> p t e", t=NT), temp, None, ALU.mult))
                dve.sem_inc(z_done, 1)
                dve.wait_ge(inh_done, 1)
                link(dve.tensor_scalar(dist, inh, GOLD_C, None, ALU.subtract))
                dve.scalar_tensor_tensor(dist, dist, -1.0, dist, ALU.mult, ALU.max).then_inc(dist_done, 1)
                link(dve.tensor_scalar(zone, z2, Z_LO, None, ALU.is_ge))
                link(dve.scalar_tensor_tensor(zone, z2, 0.0, zone, ALU.is_le, ALU.mult))
                dve.wait_ge(gexp_done, 2)
                link(dve.tensor_tensor(gw, gw, zone, ALU.mult))
                link(dve.tensor_reduce(red8[:, 0, :], gw, AX.X, ALU.add))
                link(dve.tensor_scalar(red8[:, 1, :], red8[:, 0, :], 1e-8, None, ALU.is_lt))
                link(dve.tensor_copy(cand, fb))
                link(dve.memset(mask2, 0.0))
                for k in range(2):
                    link(dve.tensor_reduce(red8[:, 2, :], cand, AX.X, ALU.max))
                    link(dve.tensor_tensor(zone, cand, per(red8[:, 2, :]), ALU.is_equal))
                    link(dve.tensor_tensor(zone, zone, iota, ALU.mult))
                    link(dve.tensor_reduce(red8[:, 3, :], zone, AX.X, ALU.min))
                    link(dve.tensor_tensor(zone, iota, per(red8[:, 3, :]), ALU.is_equal))
                    link(dve.tensor_tensor(mask2, mask2, zone, ALU.add))
                    link(dve.scalar_tensor_tensor(cand, zone, -4.0, cand, ALU.mult, ALU.add))
                link(dve.tensor_tensor(fb, fb, mask2, ALU.mult))

                def normal(v):
                    link(dve.tensor_reduce(red8[:, 4, :], v, AX.X, ALU.add))
                    link(dve.tensor_scalar(red8[:, 4, :], red8[:, 4, :], 1e-8, None, ALU.max))
                    link(dve.reciprocal(red8[:, 4, :], red8[:, 4, :]))
                    link(dve.tensor_tensor(v, v, per(red8[:, 4, :]), ALU.mult))

                normal(fb)
                link(dve.tensor_tensor(fb, fb, per(red8[:, 1, :]), ALU.mult))
                link(dve.tensor_scalar(red8[:, 1, :], red8[:, 1, :], -1.0, 1.0, ALU.mult, ALU.add))
                link(dve.tensor_tensor(gw, gw, per(red8[:, 1, :]), ALU.mult))
                link(dve.tensor_tensor(gw, gw, fb, ALU.add))
                normal(gw)

            residual(0)


            def s_copy(layer):
                first_bank = (0, 4, 0, 4)[layer]
                for i in (1, 3):
                    dve.wait_ge(s_ready, NT * layer + 2 * i + 2)
                    o, v = s_tok[:, 2 * i:2 * i + 2, :].rearrange("p a d -> p (a d)"), bank[first_bank + i][:, :]
                    if layer == 3:
                        dve.tensor_scalar(o, v, 1.0 - LAMBDA_INIT, None, ALU.mult).then_inc(s_done, 1)
                    else:
                        dve.tensor_copy(o, v).then_inc(s_done, 1)

            if layers > 1:
                layernorm(1)
                dve.wait_ge(vec_in, 48)
                link(dve.tensor_scalar(offs, vec[:, 0:3, :], -1.0, 1.0, ALU.mult, ALU.add))
                link(dve.tensor_tensor(offs, offs, vec[:, 3:4, :].to_broadcast([P, 3, DC]), ALU.mult))
                dve.wait_ge(xnT_act, 4)
                dve.wait_ge(xnT_dve, 4)
                for b in range(B):
                    for i in range(3):
                        for c in range(DC):
                            ins = dve.tensor_scalar(mixed[:, i, c, b * S:(b + 1) * S], xnT[:, c, b * S:(b + 1) * S],
                                                    vec[:, i, c:c + 1], offs[:, i, c:c + 1], ALU.mult, ALU.add)
                        ins.then_inc(mix_done, 1)
                dve.wait_ge(wlin_in, 48)
                dve.tensor_tensor(w_lin, w_lin, lin_scale.unsqueeze(1).to_broadcast([P, DC, D]), ALU.mult).then_inc(wlin_done, 1)
                for b in range(B):
                    for o in range(DC):
                        dve.wait_ge(kvr_ready, 6 * b + 2 + o + 1)
                        dve.tensor_copy(vv[:, o, b * S:(b + 1) * S], bank[4 + (6 * b + 2 + o) % 4][:, :]).then_inc(vv_done, 1)
                for b in range(B):
                    sl = slice(b * S, (b + 1) * S)
                    dve.wait_ge(kr_done, 4 * b + 2)
                    w0 = kk[:, :, b * S:b * S + 1]
                    f = [first[:, i, :, b:b + 1] for i in range(4)]
                    pp, aa, bb = (vec[:, i, :].unsqueeze(2) for i in (6, 4, 5))
                    link(dve.tensor_tensor(f[0], w0, pp, ALU.max))
                    link(dve.tensor_tensor(f[1], pp, f[0], ALU.subtract))
                    link(dve.tensor_tensor(f[2], w0, f[0], ALU.subtract))
                    link(dve.tensor_scalar(kk[:, :, sl], kk[:, :, sl], 0.0, None, ALU.min))
                    dve.tensor_copy(w0, f[2]).then_inc(low_done, 1)
                for b in range(B):
                    sl = slice(b * S, (b + 1) * S)
                    dve.wait_ge(e_done, 2 * b + 2)
                    dve.wait_ge(vv_done, 2 * b + 2)
                    f = [first[:, i, :, b:b + 1] for i in range(4)]
                    aa, bb = (vec[:, i, :].unsqueeze(2) for i in (4, 5))
                    n0, d0 = vv[:, :, b * S:b * S + 1], kk[:, :, b * S:b * S + 1]
                    link(dve.tensor_tensor(vv[:, :, sl], vv[:, :, sl], kk[:, :, sl], ALU.mult))
                    link(dve.tensor_tensor(f[2], f[1], aa, ALU.mult))
                    link(dve.tensor_tensor(f[3], f[1], bb, ALU.mult))
                    link(dve.tensor_tensor(n0, n0, f[2], ALU.add))
                    link(dve.tensor_tensor(d0, d0, f[3], ALU.add))
                    link(dve.reciprocal(kk[:, :, sl], kk[:, :, sl]))
                    link(dve.tensor_tensor(vv[:, :, sl], vv[:, :, sl], kk[:, :, sl], ALU.mult))
                    dve.wait_ge(kr_done, 4 * b + 4)
                    dve.tensor_tensor(rr[:, :, sl], rr[:, :, sl], vv[:, :, sl], ALU.mult).then_inc(rwkv_done, 1)
                for i in range(NT // 2):
                    dve.wait_ge(g_ready, 2 * i + 2)
                    dve.tensor_tensor(g_tok[:, 2 * i:2 * i + 2, :], bank[i][:, :].rearrange("p (t d) -> p t d", t=2),
                                      lin_bias.unsqueeze(1).to_broadcast([P, 2, D]), ALU.add).then_inc(g_done, 1)
                dve.wait_ge(g_done, 4)
                dve.sem_inc(ffn_done, 1)
                s_copy(1)
                residual(1)
            if layers > 2:
                dve.sem_inc(gu_done, GU0)
                dve.sem_inc(e2_done, E20)
                layernorm(2)
                golden()
                link(dve.memset(g_tok[:, :, :], 0.0))

                def mult(e, q, n):
                    f, b = n // 2, n % 2
                    dve.wait_ge(up_ready, 4 * e + n + 1)
                    dve.wait_ge(silu2_done, 2 + 4 * e + n + 1)
                    dve.tensor_tensor(gu[q][:, f, b * S:(b + 1) * S], bank[2 + n % 2][:, :], gs[n % 2], ALU.mult
                                      ).then_inc(gu_done, 1)

                def add_expert(e, q):
                    for t in range(NT):
                        dve.wait_ge(e2_ready, 8 * e + 2 * (t // 2) + 2)
                        w = gw[:, t, e:e + 1] if isinstance(e, int) else gw[:, t, bass.ds(e, 1)]
                        dve.scalar_tensor_tensor(g_tok[:, t, :], bank[4 + t // 2][:, (t % 2) * D:(t % 2 + 1) * D], w,
                                                 g_tok[:, t, :], ALU.mult, ALU.add).then_inc(e2_done, 1)
                    dve.wait_ge(e2_done, E20 + 8 * e + 8)

                for n in range(4):
                    mult(0, 0, n)
                with dve.Fori(0, E2 // 2 - 1) as pair:
                    for q in range(2):
                        for n in range(4):
                            mult(2 * pair + q + 1, 1 - q, n)
                        add_expert(2 * pair + q, q)
                dve.wait_ge(sc_done, 1)
                link(dve.tensor_tensor(mx2, sc2[:, :, 0, :], sc2[:, :, 1, :], ALU.max))
                for u0 in range(2):
                    dve.tensor_tensor(sc2[:, :, u0, :], sc2[:, :, u0, :], mx2, ALU.subtract).then_inc(low2_done, 1)
                mult(E2 - 1, 1, 0)
                mult(E2 - 1, 1, 1)
                dve.wait_ge(sexp_done, 1)
                link(dve.tensor_tensor(mx2, sc2[:, :, 0, :], sc2[:, :, 1, :], ALU.add))
                link(dve.reciprocal(mx2, mx2))
                for u0 in range(2):
                    dve.tensor_tensor(sc2[:, :, u0, :], sc2[:, :, u0, :], mx2, ALU.mult).then_inc(prob2_done, 1)
                mult(E2 - 1, 1, 2)
                mult(E2 - 1, 1, 3)
                add_expert(E2 - 2, 0)
                for i in (1, 3):
                    dve.wait_ge(ctxT_ready, 2 * i + 2)
                    dve.tensor_copy(ctxT[:, :, i * 256:(i + 1) * 256].rearrange("p c (t n) -> p t c n", t=2),
                                    bank[i][:, :].rearrange("p (t c n) -> p t c n", t=2, c=DC)).then_inc(ctxT_done, 1)
                add_expert(E2 - 1, 1)
                dve.sem_inc(ffn_done, 1)
                s_copy(2)
                residual(2)
            if layers > 3:
                layernorm(3)
                dve.wait_ge(lam_in_s, 16)
                for i in range(2):
                    link(dve.tensor_tensor(lam_in[:, 2 * i, :], lam_in[:, 2 * i, :], lam_in[:, 2 * i + 1, :], ALU.mult))
                    dve.tensor_reduce(lam[:, i:i + 1], lam_in[:, 2 * i, :], AX.X, ALU.add).then_inc(lam_sum, 1)
                dve.wait_ge(lam_exp, 1)
                link(dve.tensor_tensor(lam[:, 2:3], lam[:, 1:2], lam[:, 0:1], ALU.subtract))
                link(dve.tensor_scalar(lam[:, 2:3], lam[:, 2:3], LAMBDA_INIT, None, ALU.subtract))

                def norm_qk(t):
                    v = qk3[:, t, :].rearrange("p (g e) -> p g e", e=G3)
                    dve.wait_ge(qkv_done, 2 * NT + 2 * t + 2)
                    link(dve.tensor_tensor(sq3[:, t % 2, :], qk3[:, t, :], qk3[:, t, :], ALU.mult))
                    link(dve.tensor_reduce(ms3, sq3[:, t % 2, :].rearrange("p (g e) -> p g e", e=G3), AX.X, ALU.add))
                    dve.tensor_scalar(rms[:, t, :], ms3, 1.0 / G3, RMS_EPS, ALU.mult, ALU.add).then_inc(ms_done, 1)

                def scale_qk(t):
                    v = qk3[:, t, :].rearrange("p (g e) -> p g e", e=G3)
                    dve.wait_ge(rms_done, t + 1)
                    dve.tensor_tensor(v, v, rmsr[:, t, :].unsqueeze(2).to_broadcast([P, 32, G3]), ALU.mult).then_inc(qk_done, 1)

                def keys3(t):
                    dve.wait_ge(qT_done, t + 1)
                    dve.wait_ge(qkT_ready, t + 1)
                    dve.tensor_copy(k3T[:, :, t * P:(t + 1) * P], bank[4 + t % 4][:, 256:512].rearrange("p (c n) -> p c n", c=DC)
                                    ).then_inc(kT_done, 1)

                def masked_keys(b, c):
                    dve.wait_ge(kT_done, NT)
                    if b:
                        dve.wait_ge(av_ready, 8 * c + 8)
                    for g in range(8):
                        dve.tensor_scalar(kz[:, c, g, :], k3T[:, c, b * S:(b + 1) * S], con[:, C_SEL + g:C_SEL + g + 1], None, ALU.mult
                                          ).then_inc(kz_done, 1)

                for t in range(NT):
                    norm_qk(t)
                    if t:
                        scale_qk(t - 1)
                scale_qk(NT - 1)
                for n in range(2 * NF):
                    f, b = n // 2, n % 2
                    dve.wait_ge(up3_ready, n + 1)
                    dve.wait_ge(silu3_done, n + 1)
                    dve.tensor_tensor(hid3[:, f, b * S:(b + 1) * S], bank[2 + n % 2][:, :], gs3[n % 2], ALU.mult).then_inc(hid3_done, 1)
                    if n >= 7 and n % 2 == 1 and (n - 7) // 2 < 5:
                        keys3((n - 7) // 2)
                for t in range(5, NT):
                    keys3(t)
                masked_keys(0, 0)
                masked_keys(0, 1)

                def normalise(b, c, j):
                    i = 4 * b + 2 * c + j
                    dve.wait_ge(av_ready, 4 * i + 4)
                    if i:
                        dve.wait_ge(norm3_done, i)
                    link(dve.reciprocal(zinv, bank[6 + j][:, :]))
                    if j == 0:
                        dve.tensor_tensor(y3[:, 0, :], bank[4][:, :], zinv, ALU.mult).then_inc(norm3_done, 1)
                    else:
                        link(dve.tensor_tensor(y3[:, 1, :], bank[5][:, :], zinv, ALU.mult))
                        dve.scalar_tensor_tensor(yT3[:, c, b * S:(b + 1) * S], y3[:, 1, :], lam[:, 2:3], y3[:, 0, :],
                                                 ALU.mult, ALU.add).then_inc(norm3_done, 1)

                for b in range(B):
                    for c in range(DC):
                        normalise(b, c, 0)
                        normalise(b, c, 1)
                        if b == 0:
                            masked_keys(1, c)
                for i in range(NT // 2):
                    dve.wait_ge(g3_ready, 2 * i + 2)
                    dve.tensor_scalar(g_tok[:, 2 * i:2 * i + 2, :].rearrange("p a d -> p (a d)"), bank[i][:, :], FF ** -0.5, None, ALU.mult
                                      ).then_inc(g_done, 1)
                dve.wait_ge(g_done, 8)
                dve.sem_inc(ffn_done, 1)
                s_copy(3)
                residual(3)

        @block.scalar
        def _(act):
            link = Link(act, act_link)
            act.sem_inc(exp_done, EXP0)
            act.sem_inc(hid_done, HID0)
            act.sem_inc(xeT_done, TURN0)

            def turned(layer):
                for i in (0, 2):
                    act.wait_ge(turn_ready, NT * layer + 2 * i + 2)
                    act.copy(xnT[:, :, i * 256:(i + 1) * 256].rearrange("p c (t n) -> p t c n", t=2),
                             bank[i][:, :].rearrange("p (t c n) -> p t c n", t=2, c=DC)).then_inc(xnT_act, 1)

            turned(0)

            def queries(h, q, b):
                act.wait_ge(proj_ready, 6 * h + 1 + 2 * b)
                act.mul(qT[q][:, b * S:(b + 1) * S], bank[2 if b else 0][:, :], DH ** -0.5).then_inc(q_done, 1)

            def value_rows(h, q, b):
                act.wait_ge(proj_ready, 6 * h + 5 + b)
                act.copy(vT[q][:, b * S:(b + 1) * S], bank[1 + b][:, :]).then_inc(v_done, 1)

            def exponent(h, n):
                r = n % 4
                act.wait_ge(max_done, 8 * h + n + 1)
                act.activation(prob[r], bank[3 + r][:, :], ACT.Exp, bias=negmax[:, r:r + 1],
                               accum_out=rowsum[:, r:r + 1]).then_inc(exp_done, 1)

            def head(h, q, nxt):
                for n in range(8):
                    act.wait_ge(acc_done, 8 * h + n + 1)
                    exponent(h, n)
                    if nxt and n in (3, 5):
                        queries(h + 1, 1 - q, (n - 3) // 2)
                if nxt:
                    act.wait_ge(vals_done, 2 * h + 1)
                    value_rows(h + 1, 1 - q, 0)
                    value_rows(h + 1, 1 - q, 1)

            queries(0, 0, 0)
            queries(0, 0, 1)
            value_rows(0, 0, 0)
            value_rows(0, 0, 1)
            act.wait_ge(lg_shift, 1)
            act.activation(ex, ex, ACT.Exp).then_inc(ex_done, 1)
            act.wait_ge(lg_shift, 2)
            act.activation(gap, gap, ACT.Exp).then_inc(ex_done, 1)
            with act.Fori(0, NH // 2 - 1) as pair:
                head(2 * pair, 0, True)
                head(2 * pair + 1, 1, True)
            head(NH - 2, 0, True)
            head(NH - 1, 1, False)
            for i in (0, 2):
                act.wait_ge(s_ready, 2 * i + 2)
                act.copy(s_tok[:, 2 * i:2 * i + 2, :].rearrange("p a d -> p (a d)"), bank[i][:, :]).then_inc(s_done, 1)

            with act.Fori(0, NE // 2) as pair:
                for q in range(2):
                    e = 2 * pair + q
                    act.wait_ge(xeT_ready, 2 * e + 1)
                    act.copy(xeT[q][:, 0, :], bank[0][:, 0:SLOTS]).then_inc(xeT_done, 1)
                    for f in range(NF):
                        act.wait_ge(hid_ready, 9 * e + f + 1)
                        act.activation(hE[:, f, :], bank[2 + f % 3][:, 0:SLOTS], ACT.Gelu, bias=b1[q][:, f:f + 1]
                                       ).then_inc(hid_done, 1)
                    act.wait_ge(hid_ready, 9 * e + NF + 1)
                    act.activation(aE, bank[2 + NF % 3][0:RANK, 0:SLOTS], ACT.Gelu).then_inc(hid_done, 1)
            for f in range(NF + 1):
                for b in range(B):
                    n = B * f + b
                    act.wait_ge(shid_ready, n + 1)
                    if f < NF:
                        ins = act.activation(hS[:, f, b * S:(b + 1) * S], bank[n % 4][:, :], ACT.Gelu, bias=sb1[:, f:f + 1])
                    else:
                        ins = act.activation(aS[:, b * S:(b + 1) * S], bank[n % 4][0:RANK, :], ACT.Gelu)
                    ins.then_inc(shid_done, 1)

            def gate_silu(layer):
                act.wait_ge(ffn_done, layer + 1)
                act.activation(g_tok[:, :, :], g_tok[:, :, :], ACT.Silu).then_inc(silu_done, 1)

            gate_silu(0)

            def s_copy(layer):
                first_bank = (0, 4, 0, 4)[layer]
                for i in (0, 2):
                    act.wait_ge(s_ready, NT * layer + 2 * i + 2)
                    o, v = s_tok[:, 2 * i:2 * i + 2, :].rearrange("p a d -> p (a d)"), bank[first_bank + i][:, :]
                    if layer == 3:
                        act.mul(o, v, 1.0 - LAMBDA_INIT).then_inc(s_done, 1)
                    else:
                        act.copy(o, v).then_inc(s_done, 1)

            if layers > 1:
                turned(1)
                act.wait_ge(vec_in, 48)
                for b in range(B):
                    for i in (0, 2):
                        for o in range(DC):
                            n = 6 * b + 2 * i + o
                            act.wait_ge(kvr_ready, n + 1)
                            v = bank[4 + n % 4][:, :]
                            if i == 0:
                                ins = act.activation(kk[:, o, b * S:(b + 1) * S], v, ACT.Identity, bias=vec[:, 7, o:o + 1])
                            else:
                                ins = act.activation(rr[:, o, b * S:(b + 1) * S], v, ACT.Sigmoid)
                            ins.then_inc(kr_done, 1)
                for b in range(B):
                    act.wait_ge(low_done, b + 1)
                    act.activation(kk[:, :, b * S:(b + 1) * S], kk[:, :, b * S:(b + 1) * S], ACT.Exp).then_inc(e_done, 1)
                    act.activation(first[:, 1, :, b:b + 1], first[:, 1, :, b:b + 1], ACT.Exp).then_inc(e_done, 1)
                gate_silu(1)
                s_copy(1)

            def qkv_copy(layer):
                for t in range(NT):
                    act.wait_ge(qkv_ready, NT * (layer - 2) + t + 1)
                    b0 = 2 * (t % 3)
                    qk, v = (qkv2[:, t, 0:512], qkv2[:, t, 512:768]) if layer == 2 else (qk3[:, t, :], v3[:, t, :])
                    act.copy(qk, bank[b0][:, :]).then_inc(qkv_done, 1)
                    act.copy(v, bank[b0 + 1][:, 0:D]).then_inc(qkv_done, 1)

            if layers > 2:
                for i in range(4):
                    act.wait_ge(had_ready, i + 1)
                    act.copy(had_b[:, 2 * i:2 * i + 2, :].rearrange("p f d -> p (f d)"), bank[i][:, :]).then_inc(had_copied, 1)
                turned(2)
                act.sem_inc(silu2_done, 2)
                act.wait_ge(z_done, 1)
                act.activation(inh, z2, ACT.Sigmoid).then_inc(inh_done, 1)
                act.wait_ge(dist_done, 1)
                act.activation(gw, dist, ACT.Exp, scale=-1.0 / 0.1).then_inc(gexp_done, 1)
                act.activation(fb, dist, ACT.Exp, scale=-1.0 / 0.3).then_inc(gexp_done, 1)
                qkv_copy(2)

                def silu2(e, n):
                    act.wait_ge(gate_ready, 4 * e + n + 1)
                    act.wait_ge(gu_done, 4 * e + n + 1)
                    act.activation(gs[n % 2], bank[n % 2][:, :], ACT.Silu).then_inc(silu2_done, 1)

                for n in range(4):
                    silu2(0, n)
                with act.Fori(0, E2 // 2 - 1) as pair:
                    for q in range(2):
                        for n in range(4):
                            silu2(2 * pair + q + 1, n)
                act.wait_ge(low2_done, 2)
                act.activation(sc2, sc2, ACT.Exp).then_inc(sexp_done, 1)
                for n in range(4):
                    silu2(E2 - 1, n)
                for i in (0, 2):
                    act.wait_ge(ctxT_ready, 2 * i + 2)
                    act.copy(ctxT[:, :, i * 256:(i + 1) * 256].rearrange("p c (t n) -> p t c n", t=2),
                             bank[i][:, :].rearrange("p (t c n) -> p t c n", t=2, c=DC)).then_inc(ctxT_done, 1)
                gate_silu(2)
                s_copy(2)
            if layers > 3:
                turned(3)
                act.wait_ge(lam_sum, 2)
                act.activation(lam[:, 0:2], lam[:, 0:2], ACT.Exp).then_inc(lam_exp, 1)
                qkv_copy(3)

                def queries3(t):
                    act.wait_ge(qkT_ready, t + 1)
                    act.copy(q3T[:, :, t * P:(t + 1) * P], bank[4 + t % 4][:, 0:256].rearrange("p (c n) -> p c n", c=DC)
                             ).then_inc(qT_done, 1)

                for n in range(2 * NF):
                    act.wait_ge(gate3_ready, n + 1)
                    if n >= 2:
                        act.wait_ge(hid3_done, n - 1)
                    act.activation(gs3[n % 2], bank[n % 2][:, :], ACT.Silu).then_inc(silu3_done, 1)
                    if n >= 7 and n % 2 == 1 and (n - 7) // 2 < 5:
                        queries3((n - 7) // 2)
                for t in range(5, NT):
                    queries3(t)
                for u in range(32):
                    w = S - u % 4 * P
                    for hh in range(4):
                        act.wait_ge(sc3_ready, 4 * u + hh + 1)
                        if u >= 2 and hh == 0:
                            act.wait_ge(av_ready, u - 1)
                        act.activation(prob3[:, u % 2, hh, 0:w], bank[hh][:, 0:w], ACT.Exp, scale=G3 ** -0.5).then_inc(exp3_done, 1)
                gate_silu(3)
                s_copy(3)


def _rows(w):
    k, n = w.shape
    return np.ascontiguousarray(w.reshape(k // P, P, n).transpose(1, 0, 2).reshape(P, -1))


def layout(i):
    f = {k: np.asarray(v) for k, v in i.items()}
    w = f["L0_attn_w_qkv"].reshape(DC, P, 3, NH, DH).transpose(3, 1, 0, 2, 4)
    d = {
        "x": f["L0_attn_x"].reshape(T, D),
        "con": constants(),
        "gate": _rows(f["L0_ffn_gate_w"]),
        "wqkv": w.reshape(NH, P, DC * 3 * DH),
        "wo": _rows(f["L0_attn_w_o"]),
        "wexp": np.stack([np.concatenate([_rows(f["L0_ffn_w1"][e]), _rows(f["L0_ffn_w2"][e]), _rows(f["L0_ffn_wd"][e]),
                                          f["L0_ffn_b1"][e].reshape(NF, P).T], 1) for e in range(NE)]),
        "wu": f["L0_ffn_wu"],
        "b2": f["L0_ffn_b2"].reshape(NE, 1, D),
        "sw": np.concatenate([_rows(f["L0_ffn_sw1"]), _rows(f["L0_ffn_sw2"]), _rows(f["L0_ffn_swd"]),
                              f["L0_ffn_sb1"].reshape(NF, P).T], 1),
        "swu": f["L0_ffn_swu"],
        "sb2": f["L0_ffn_sb2"].reshape(1, D),
        "w_rwkv": np.concatenate([_rows(f[f"L1_attn_w_{k}"].T) for k in ("key", "value", "rec", "out")], 1),
        "w_lin": _rows(f["L1_ffn_weight"].T),
        "lin_scale": f["L1_ffn_scale_weight"].reshape(1, D),
        "lin_bias": f["L1_ffn_bias"].reshape(1, D),
        "vec": np.concatenate([_rows(f[f"L1_attn_{k}"].reshape(D, 1)) for k in
                               ("time_mix_k", "time_mix_v", "time_mix_r", "xx", "aa", "bb", "pp", "time_first")], 1),
        "gate2": _rows(f["L2_ffn_Wr"]),
        "temp": f["L2_ffn_temperature"].reshape(1, 1),
        "lam": np.concatenate([f[f"L3_attn_{k}"] for k in ("lq1", "lk1", "lq2", "lk2")]).reshape(1, 128),
        "w2": np.concatenate([_rows(f["L2_attn_w_qkv"].reshape(D, H2, 3, HD2).transpose(0, 2, 1, 3).reshape(D, 3 * D)),
                              _rows(f["L2_attn_w_dense"])], 1),
        "wexp2": np.stack([np.concatenate([_rows(f[f"L2_ffn_{k}"][e]) for k in ("Wg", "Wu", "Wd")], 1) for e in range(E2)]),
        "w3": np.concatenate([_rows(np.concatenate([f[f"L3_attn_{k}"].T for k in ("wq", "wk", "wv")], 1)),
                              _rows(f["L3_attn_wo"].T)], 1),
        "wff3": np.concatenate([_rows(f["L3_ffn_W1"].T), _rows(f["L3_ffn_W3"].T)], 1),
        "w_down3": _rows(f["L3_ffn_W2"].T),
    }
    return {k: np.ascontiguousarray(v) for k, v in d.items()}


def kernel(**inputs):
    import concourse.bacc as bacc
    from concourse.bass_utils import run_bass_kernel_spmd

    nc = bacc.Bacc("TRN2", target_bir_lowering=False, num_devices=1)
    arrays, args = {}, {}
    for name, v in layout(inputs).items():
        arrays[f"in_{name}"] = v
        args[name] = nc.dram_tensor(f"in_{name}", v.shape, F32, kind="ExternalInput").ap()
    out = nc.dram_tensor("out_x", (T, D), F32, kind="ExternalOutput").ap()
    build(nc, args, out)
    r = run_bass_kernel_spmd(nc, [arrays], core_ids=[0])
    return r.results[0]["out_x"].reshape(B, S, D)
```

```python
from contextlib import ExitStack

import numpy as np

import concourse.bass as bass
from concourse import mybir

F32 = mybir.dt.float32
I32 = mybir.dt.int32
F32R = mybir.dt.float32r
ALU = mybir.AluOpType
ACT = mybir.ActivationFunctionType
AX = mybir.AxisListType

P = 128
B, S, D = 2, 512, 256
T = B * S
NT = T // P
DC = D // P
ST = S // P
LN_EPS = 1e-5

NH, DH = 16, 128
NE, CAP, FF, RANK = 8, 160, 1024, 32
NF = FF // P
SLOTS = 2 * CAP
SROWS = [128, 128, SLOTS - 256]
W_D, W_B, W_2 = DC * FF, DC * FF + DC * RANK, DC * FF + DC * RANK + NF
WPACK = W_2 + NF * D
NO_SLOT = 4096.0
OUT_OF_REACH = -3.0e38

H2, HD2 = 16, 16
E2 = 8
GOLD_C = float(1.0 / np.e)
GOLD_LO = 0.5 - np.log(4.0 / 3.0)
Z_LO = float(np.log(GOLD_LO / (1.0 - GOLD_LO)))
BLOCKED = -10000.0

H3, G3 = 8, 16
RMS_EPS = 1.1920929e-07
LAMBDA_INIT = 0.8

C_ID, C_TRI, C_HAD, C_CAUSAL, C_IOTA, C_COS, C_SIN, C_SEL = 0, 128, 256, 384, 512, 576, 832, 1088
C_END = 1096


def constants():
    c = np.zeros((P, C_END), np.float32)
    i = np.arange(P)
    c[:, C_ID:C_ID + P] = np.eye(P)
    c[:, C_TRI:C_TRI + P] = i[:, None] < i[None, :]
    had = np.array([[1.0]])
    while had.shape[0] < P:
        had = np.block([[had, had], [had, -had]])
    c[:, C_HAD:C_HAD + P] = had
    c[:, C_CAUSAL:C_CAUSAL + P] = i[:, None] <= i[None, :]
    c[:, C_IOTA:C_IOTA + 64] = np.tile(np.arange(8) - 8.0, 8)
    inv = 1.0 / 10000.0 ** (np.arange(0, HD2, 2, dtype=np.float32) / np.float32(HD2))
    ang = np.concatenate([inv, inv]).astype(np.float32)
    sign = np.where(np.arange(HD2) < HD2 // 2, -1.0, 1.0)
    c[:, C_COS:C_COS + D] = np.tile(np.cos(ang), H2)
    c[:, C_SIN:C_SIN + D] = np.tile(np.sin(ang) * sign, H2)
    c[:, C_SEL:C_SEL + 8] = (i[:, None] // G3) == np.arange(8)[None, :]
    return c


TWIN = {}


def rounded(v):
    return bass.AP(tensor=TWIN[v.tensor.name], offset=v.offset, ap=v.ap)


def r(v):
    return rounded(v).bitcast(F32R)


def product(pe, o, lhs, rhs, start, stop):
    pe.matmul(o, r(lhs[0]), r(rhs[0]), start=start, stop=False)
    pe.matmul(o, r(lhs[0]), r(rhs[1]), start=False, stop=False)
    return pe.matmul(o, r(lhs[1]), r(rhs[0]), start=False, stop=stop)


class Link:

    def __init__(self, eng, sem):
        self.eng, self.sem, self.n, self.turn, self.step = eng, sem, 0, 0, 0

    def loop(self, turn, step):
        self.turn, self.step, self.start = turn, step, self.n

    def end(self, turns):
        assert self.n - self.start == self.step, (self.n - self.start, self.step)
        self.n = self.start + turns * self.step
        self.turn, self.step = 0, 0

    def __call__(self, ins):
        self.n += 1
        ins.then_inc(self.sem, 1)
        self.eng.wait_ge(self.sem, self.n + self.turn * self.step if self.step else self.n)


def build(nc, a, out, layers=4):
    ctx = ExitStack()
    with ctx:
        def sem(name):
            return ctx.enter_context(nc.semaphore(name))

        def sb(name, shape, dt=F32):
            return ctx.enter_context(nc.sbuf_tensor(name, shape, dt))

        def twinned(name, shape):
            with nc.sbuf_tensor(name + "_rounded", shape, F32) as second:
                TWIN[name] = second
            return sb(name, shape)

        bank = [ctx.enter_context(nc.psum_tensor(f"bank{i}", [P, 512], F32)) for i in range(8)]

        x = sb("x", [P, NT, D])
        xn = twinned("xn", [P, NT, D])
        xnT = twinned("xnT", [P, DC, T])
        s_tok = twinned("s_tok", [P, NT, D])
        g_tok = sb("g_tok", [P, NT, D])
        con = sb("con", [P, C_END])
        ones = sb("ones", [P, P])
        stats = sb("stats", [P, NT, 6])
        meanvar = sb("meanvar", [P, NT, 2])
        veps = sb("veps", [P, NT])
        rstd = sb("rstd", [P, NT])
        mhalf = sb("mhalf", [P, 256])
        ident = con[:, C_ID:C_ID + P]

        arenaB = twinned("arenaB", [P, 16384])
        arenaC = twinned("arenaC", [P, 12800])
        arenaD = twinned("arenaD", [P, 2 * (WPACK + 2 * D)])
        small = twinned("small", [P, 1536])

        def part(arena, at, n, **kw):
            v = arena[:, at:at + n]
            return v.rearrange(kw.pop("r"), **kw) if "r" in kw else v

        vals = part(arenaB, 0, NH * T, r="p (h t) -> p h t", h=NH)
        wqkv = [part(arenaC, 768 * q, 768, r="p (c w) -> p c w", c=DC) for q in range(2)]
        wo = part(arenaC, 1536, NH * D, r="p (h d) -> p h d", h=NH)
        qT = [part(arenaC, 5632 + 1024 * q, T) for q in range(2)]
        kT = [part(arenaC, 7680 + 1024 * q, T) for q in range(2)]
        vT = [part(arenaC, 9728 + 1024 * q, T) for q in range(2)]
        acc = [part(arenaC, 11776 + 512 * b, S) for b in range(B)]
        xlo = s_tok[:, :, :].rearrange("p a d -> p (a d)").rearrange("p (c t) -> p c t", c=DC)
        wqkv_hi = [part(arenaD, 768 * q, 768, r="p (c w) -> p c w", c=DC) for q in range(2)]
        qlo = [part(arenaD, 1536 + 1024 * q, T) for q in range(2)]
        klo = [part(arenaD, 3584 + 1024 * q, T) for q in range(2)]
        prob = [g_tok[:, 2 * q:2 * q + 2, :].rearrange("p a d -> p (a d)") for q in range(4)]
        wexp = [part(arenaD, (WPACK + 2 * D) * q, WPACK + 2 * D) for q in range(2)]
        def w1_of(w):
            return w[:, 0:W_D].rearrange("p (c f) -> p c f", c=DC)

        def wd_of(w):
            return w[:, W_D:W_B].rearrange("p (c r) -> p c r", c=DC)

        def w2_of(w):
            return w[:, W_2:WPACK].rearrange("p (f d) -> p f d", f=NF)

        w1, wd, w2 = ([of(w) for w in wexp] for of in (w1_of, wd_of, w2_of))
        b1 = [w[:, W_B:W_2] for w in wexp]
        wu = [w[0:RANK, WPACK:WPACK + D] for w in wexp]
        b2 = [w[:, WPACK + D:WPACK + 2 * D] for w in wexp]
        xe = [part(arenaC, 5632 + 768 * q, 768, r="p (s d) -> p s d", s=3) for q in range(2)]
        xeT = [part(arenaC, 640 * q, 640, r="p (c n) -> p c n", c=DC) for q in range(2)]
        hE = part(arenaC, 1280, NF * SLOTS, r="p (f n) -> p f n", f=NF)
        aE = arenaC[0:RANK, 3840:3840 + SLOTS]
        yE = [part(arenaC, 7168 + 768 * q, 768, r="p (s d) -> p s d", s=3) for q in range(2)]
        wexp_hi = [part(arenaC, 8704, 4096), part(arenaB, 0, 4096)]
        w1_hi = [w[:, 0:DC * FF].rearrange("p (c f) -> p c f", c=DC) for w in wexp_hi]
        w2_hi = [w[:, DC * FF:4096].rearrange("p (f d) -> p f d", f=NF) for w in wexp_hi]
        wd_hi = [part(small, 820 + DC * RANK * q, DC * RANK, r="p (c r) -> p c r", c=DC) for q in range(2)]
        hE_hi = part(arenaB, 4096, NF * SLOTS, r="p (f n) -> p f n", f=NF)
        xeT_lo = [part(arenaB, 6656 + 640 * q, 640, r="p (c n) -> p c n", c=DC) for q in range(2)]
        hS = part(arenaB, 0, NF * T, r="p (f t) -> p f t", f=NF)
        sw = part(arenaB, 8192, DC * FF + NF * D + DC * RANK + NF + D)
        sw1, swd, sw2 = w1_of(sw), wd_of(sw), w2_of(sw)
        sb1 = sw[:, W_B:W_2]
        sw_hi = part(arenaD, 0, WPACK)
        sw1_hi, swd_hi, sw2_hi = w1_of(sw_hi), wd_of(sw_hi), w2_of(sw_hi)
        hS_hi = [part(arenaD, WPACK + 2 * D, NF * S, r="p (f t) -> p f t", f=NF), part(arenaC, 0, NF * S, r="p (f t) -> p f t", f=NF)]
        sb2 = sw[:, WPACK:WPACK + D]
        swu = arenaB[0:RANK, 12616:12616 + D]
        aS = arenaB[0:RANK, 12872:12872 + T]
        got = [part(arenaC, 8704 + NT * D * k, NT * D, r="p (t d) -> p t d", t=NT) for k in range(2)]
        gate = part(small, 0, DC * NE, r="p (c e) -> p c e", c=DC)
        lg = part(small, 16, 64, r="p (t e) -> p t e", t=NT)
        eq = part(small, 80, 64, r="p (t e) -> p t e", t=NT)
        ex = part(small, 144, 64, r="p (t e) -> p t e", t=NT)
        oh = part(small, 208, 128, r="p (t k e) -> p t k e", t=NT, k=2)
        before = part(small, 336, 128, r="p (t k e) -> p t k e", t=NT, k=2)
        ohp = part(small, 464, 128, r="p (t k e) -> p t k e", t=NT, k=2)
        top = part(small, 592, 16, r="p (k t) -> p k t", k=2)
        idx = part(small, 608, 16, r="p (t k) -> p t k", k=2)
        pos = part(small, 624, 16, r="p (t k) -> p t k", k=2)
        keep = part(small, 640, 16, r="p (t k) -> p t k", k=2)
        base = part(small, 656, 16, r="p (t k) -> p t k", k=2)
        slot = part(small, 672, 16, r="p (t k) -> p t k", k=2)
        wt = part(small, 688, 16, r="p (t k) -> p t k", k=2)
        esum = part(small, 704, 8)
        einv = part(small, 712, 8)
        kslot = part(small, 720, 16, r="p (t k) -> p t k", k=2)
        gap = part(small, 748, 8)
        negmax = part(small, 736, 4)
        rowsum = part(small, 740, 4)
        rowinv = part(small, 744, 4)
        w_rwkv = part(arenaB, 13896, 4 * DC * D, r="p (i c o) -> p i c o", i=4, c=DC)
        w_lin = part(arenaC, 4160, DC * D, r="p (c o) -> p c o", c=DC)
        lin_scale, lin_bias = part(arenaC, 4672, D), part(arenaC, 4928, D)
        vec = part(small, 756, 16, r="p (i c) -> p i c", i=8)
        offs = part(small, 772, 6, r="p (i c) -> p i c", i=3)
        mixed = part(arenaB, 0, 3 * DC * T, r="p (i c t) -> p i c t", i=3, c=DC)
        kk, vv, rr = (part(arenaB, 6144 + 2048 * i, DC * T, r="p (c t) -> p c t", c=DC) for i in range(3))
        first = part(small, 780, 16, r="p (i c b) -> p i c b", i=4, c=DC)
        w_qkv2 = part(arenaC, 0, DC * 768, r="p (c n) -> p c n", c=DC)
        w_dense = part(arenaC, 1536, DC * D, r="p (c n) -> p c n", c=DC)
        w_qkv3 = part(arenaC, 2048, DC * 768, r="p (c n) -> p c n", c=DC)
        w_out3 = part(arenaC, 3584, DC * D, r="p (c n) -> p c n", c=DC)
        qkv2 = part(arenaB, 0, NT * 768, r="p (t n) -> p t n", t=NT)
        rot = part(arenaB, 6144, 1024, r="p (t h e) -> p t h e", t=4, h=H2)
        prod = part(arenaB, 7168, 1024, r="p (t h e) -> p t h e", t=4, h=H2)
        ctx_tok = part(arenaB, 8192, NT * D, r="p (t n) -> p t n", t=NT)
        ctxT = part(arenaB, 10240, DC * T, r="p (c t) -> p c t", c=DC)
        tree = part(arenaB, 12288, 1024)
        sc2 = part(arenaB, 13312, 256, r="p (s u m) -> p s u m", s=2, u=2)
        mx2 = part(arenaB, 13568, 128, r="p (s m) -> p s m", s=2)
        wexp2 = [part(arenaD, 1536 * q, 1536, r="p (i c n) -> p i c n", i=3, c=DC) for q in range(2)]
        w_qkv2_hi = part(arenaC, 10752, DC * 768, r="p (c n) -> p c n", c=DC)
        wexp2_hi = [m.rearrange("p (i c n) -> p i c n", i=3, c=DC)
                    for m in (arenaB[:, 13696:15232], xn[:, 0:6, :].rearrange("p t d -> p (t d)"))]
        gu_hi = [part(arenaC, 6208, DC * T, r="p (f t) -> p f t", f=DC), part(arenaD, 3072, DC * T, r="p (f t) -> p f t", f=DC)]
        gu = [part(arenaC, 8704 + 2048 * q, DC * T, r="p (f t) -> p f t", f=DC) for q in range(2)]
        gs = [part(arenaC, 5184 + 512 * q, S) for q in range(2)]
        gate2 = part(small, 800, DC * E2, r="p (c e) -> p c e", c=DC)
        temp = part(small, 816, 1)
        z2, inh, dist, gw, fb, zone, cand, mask2 = (part(small, 820 + 64 * i, 64, r="p (t e) -> p t e", t=NT) for i in range(8))
        red8 = part(small, 1332, 48, r="p (i t) -> p i t", i=6)
        xlo3 = part(arenaC, 0, DC * T, r="p (c t) -> p c t", c=DC)
        w_qkv3_hi = part(arenaB, 0, DC * 768, r="p (c n) -> p c n", c=DC)
        w_gate3_hi = part(arenaB, 1536, DC * FF, r="p (c n) -> p c n", c=DC)
        w_up3_hi = part(arenaB, 3584, DC * FF, r="p (c n) -> p c n", c=DC)
        w_gate3 = part(arenaD, 3072, DC * FF, r="p (c n) -> p c n", c=DC)
        w_up3 = part(arenaD, 5120, DC * FF, r="p (c n) -> p c n", c=DC)
        w_down3 = part(arenaD, 7168, NF * D, r="p (f d) -> p f d", f=NF)
        had_b = part(arenaC, 6208, NF * D, r="p (f d) -> p f d", f=NF)
        qk3 = part(arenaC, 4096, NT * 512, r="p (t n) -> p t n", t=NT)
        v3 = part(arenaC, 8192, NT * D, r="p (t n) -> p t n", t=NT)
        prob3 = part(arenaC, 4096, 4096, r="p (q h n) -> p q h n", q=2, h=4)
        y3 = part(arenaC, 10240, 1024, r="p (i n) -> p i n", i=2)
        zinv = part(arenaC, 11264, 512)
        gs3 = [part(arenaC, 11776 + 512 * q, S) for q in range(2)]
        yT3 = part(arenaC, 0, DC * T, r="p (c t) -> p c t", c=DC)
        q3T = g_tok[:, :, :].rearrange("p a d -> p (a d)").rearrange("p (c t) -> p c t", c=DC)
        k3T = s_tok[:, :, :].rearrange("p a d -> p (a d)").rearrange("p (c t) -> p c t", c=DC)
        kz = part(arenaB, 0, 8192, r="p (c g t) -> p c g t", c=DC, g=8)
        hid3 = part(arenaB, 8192, NF * T, r="p (f t) -> p f t", f=NF)
        sq3 = part(arenaD, 0, 1024, r="p (q n) -> p q n", q=2)
        ms3 = part(small, 1380, 32)
        rms = sb("rms", [P, NT, 32])
        rmsr = sb("rmsr", [P, NT, 32])
        lam_in = sb("lam_in", [P, 4, 32])
        lam = part(small, 1420, 8)
        put_at = sb("put_at", [P, NT, 2], I32)
        get_at = sb("get_at", [P, NT, 2], I32)

        slots_d = nc.dram_tensor("slots", (NE * SLOTS, D), F32, kind="Internal").ap()
        rows_d = nc.dram_tensor("rows", (NE * SLOTS, D), F32, kind="Internal").ap()

        x_in, con_in, gate_in, wo_in = sem("x_in"), sem("con_in"), sem("gate_in"), sem("wo_in")
        wqkv_in = [sem(f"wqkv_in{q}") for q in range(2)]
        w1exp_in = [sem(f"w1exp_in{q}") for q in range(2)]
        w2exp0_in = [sem(f"w2exp0_in{q}") for q in range(2)]
        xe_in = [sem(f"xe_in{q}") for q in range(2)]
        sw_in, x_out = sem("sw_in"), sem("x_out")
        slots_zero, slots_put, rows_got = sem("slots_zero"), sem("slots_put"), sem("rows_got")
        rows_out = [sem(f"rows_out{q}") for q in range(2)]
        dve_link, act_link, pool_link = sem("dve_link"), sem("act_link"), sem("pool_link")
        ones_set, zeros_set, mhalf_set = sem("ones_set"), sem("zeros_set"), sem("mhalf_set")
        ln_var, ln_rstd, xn_done = sem("ln_var"), sem("ln_rstd"), sem("xn_done")
        turn_ready, xnT_act, xnT_dve = sem("turn_ready"), sem("xnT_act"), sem("xnT_dve")
        logits_ready, lg_shift, ex_done = sem("logits_ready"), sem("lg_shift"), sem("ex_done")
        oh_done, place_ready, at_done = sem("oh_done"), sem("place_ready"), sem("at_done")
        proj_ready = sem("proj_ready")
        q_done, k_done, v_done = sem("q_done"), sem("k_done"), sem("v_done")
        qlo_done, kfull_done, klo_done, inv_done = sem("qlo_done"), sem("kfull_done"), sem("klo_done"), sem("inv_done")
        wqkv_rounded, wqkv_split = sem("wqkv_rounded"), sem("wqkv_split")
        score_ready, max_done, exp_done, acc_done = sem("score_ready"), sem("max_done"), sem("exp_done"), sem("acc_done")
        colsum_ready, vals_done = sem("colsum_ready"), sem("vals_done")
        s_ready, s_done = sem("s_ready"), sem("s_done")
        xeT_ready, xeT_done, hid_ready, hid_done = sem("xeT_ready"), sem("xeT_done"), sem("hid_ready"), sem("hid_done")
        y_ready, y_done = sem("y_ready"), sem("y_done")
        w_rounded, w_split = sem("w_rounded"), sem("w_split")
        h_rounded, h_split, xeT_rounded = sem("h_rounded"), sem("h_split"), sem("xeT_rounded")
        hS_rounded, hS_split = sem("hS_rounded"), sem("hS_split")
        shid_ready, shid_done, sh_ready, sh_done = sem("shid_ready"), sem("shid_done"), sem("sh_ready"), sem("sh_done")
        w1_in, wlin_in, mix_done, kvr_ready = sem("w1_in"), sem("wlin_in"), sem("mix_done"), sem("kvr_ready")
        kr_done, vv_done, low_done, e_done, rwkv_done = sem("kr_done"), sem("vv_done"), sem("low_done"), sem("e_done"), sem("rwkv_done")
        wlin_done, g_ready, g_done, vec_in = sem("wlin_done"), sem("g_ready"), sem("g_done"), sem("vec_in")
        w2_in, w3_in, wff3_in, wgate3_in = sem("w2_in"), sem("w3_in"), sem("wff3_in"), sem("wgate3_in")
        wq_rounded, wq_split = sem("wq_rounded"), sem("wq_split")
        gateup_rounded, gateup_split, down_rounded, down_split = sem("gateup_rounded"), sem("gateup_split"), sem("down_rounded"), sem("down_split")
        gu_rounded, gu_split, ff3_rounded, ff3_split = sem("gu_rounded"), sem("gu_split"), sem("ff3_rounded"), sem("ff3_split")
        wdown_in = [sem(f"wdown_in{q}") for q in range(2)]
        had_ready, had_copied, had_done = sem("had_ready"), sem("had_copied"), sem("had_done")
        qkv_ready, qkv_done = sem("qkv_ready"), sem("qkv_done")
        z_ready, z_done, inh_done, dist_done, gexp_done = sem("z_ready"), sem("z_done"), sem("inh_done"), sem("dist_done"), sem("gexp_done")
        w2exp_in = [sem(f"w2exp_in{q}") for q in range(2)]
        gate_ready, up_ready, silu2_done, gu_done = sem("gate_ready"), sem("up_ready"), sem("silu2_done"), sem("gu_done")
        e2_ready, e2_done = sem("e2_ready"), sem("e2_done")
        sc_done, low2_done, sexp_done, prob2_done, ctx_done = sem("sc_done"), sem("low2_done"), sem("sexp_done"), sem("prob2_done"), sem("ctx_done")
        ctxT_ready, ctxT_done = sem("ctxT_ready"), sem("ctxT_done")
        ms_done, rms_done, qk_done = sem("ms_done"), sem("rms_done"), sem("qk_done")
        qkT_ready, qT_done, kT_done, kz_done = sem("qkT_ready"), sem("qT_done"), sem("kT_done"), sem("kz_done")
        gate3_ready, up3_ready, silu3_done, hid3_done = sem("gate3_ready"), sem("up3_ready"), sem("silu3_done"), sem("hid3_done")
        sc3_ready, exp3_done, causal_done, av_ready, norm3_done = sem("sc3_ready"), sem("exp3_done"), sem("causal_done"), sem("av_ready"), sem("norm3_done")
        g3_ready, lam_in_s, lam_exp, lam_sum = sem("g3_ready"), sem("lam_in_s"), sem("lam_exp"), sem("lam_sum")
        ffn_done, silu_done, x_done = sem("ffn_done"), sem("silu_done"), sem("x_done")

        EXP0, ACC0, VALS0, HID0, Y0, TURN0, ROWS0, GU0, E20 = 4, 4, 1, 3, 3, 2, 32, 2, 8

        SPLIT = [True, False, True, True]
        XLO = [xlo, None, xlo, xlo3]
        XT = [sum(4 if k else 2 for k in SPLIT[:n + 1]) for n in range(4)]

        def quarter(v, i):
            return v[:, :, i * 256:(i + 1) * 256].rearrange("p c (t n) -> p t c n", t=2)

        def turned_bank(i):
            return bank[i][:, :].rearrange("p (t c n) -> p t c n", t=2, c=DC)

        block = ctx.enter_context(nc.Block())

        @block.sync
        def _(sp):
            sp.dma_start(x[:, :, :], a["x"].rearrange("(n p) d -> p n d", p=P)).then_inc(x_in, 16)
            sp.dma_start(con[:, :], a["con"]).then_inc(con_in, 16)
            sp.dma_start(gate, a["gate"].rearrange("p (c e) -> p c e", c=DC)).then_inc(gate_in, 16)
            sp.dma_start(part(small, 756, 16), a["vec"]).then_inc(vec_in, 16)
            sp.dma_start(part(small, 800, DC * E2), a["gate2"]).then_inc(vec_in, 16)
            sp.dma_start(temp, a["temp"].to_broadcast([P, 1])).then_inc(vec_in, 16)
            sp.dma_start(lam_in[:, :, :], a["lam"].to_broadcast([P, 128]).rearrange("p (i n) -> p i n", i=4)).then_inc(lam_in_s, 16)
            for h in range(2):
                sp.dma_start(wqkv[h], a["wqkv"][h].rearrange("p (c w) -> p c w", c=DC)).then_inc(wqkv_in[h], 16)
            sp.wait_ge(zeros_set, 1)
            sp.dma_start(slots_d.rearrange("(p n) d -> p n d", p=P),
                         arenaB[:, 0:NE * SLOTS // P * D].rearrange("p (n d) -> p n d", d=D)).then_inc(slots_zero, 16)
            sp.dma_start(wo, a["wo"].rearrange("p (h d) -> p h d", h=NH)).then_inc(wo_in, 16)

            def load_first(e, q):
                sp.dma_start(wexp[q][:, 0:W_2], a["wexp"][e][:, 0:W_2] if isinstance(e, int) else
                             a["wexp"][bass.ds(e, 1), :, 0:W_2].rearrange("e p n -> (e p) n")).then_inc(w1exp_in[q], 16)

            def load_second(e, q):
                sp.dma_start(wexp[q][:, W_2:WPACK], a["wexp"][e][:, W_2:WPACK] if isinstance(e, int) else
                             a["wexp"][bass.ds(e, 1), :, W_2:WPACK].rearrange("e p n -> (e p) n")).then_inc(w2exp0_in[q], 16)
                sp.dma_start(wu[q], a["wu"][e]).then_inc(w2exp0_in[q], 16)
                sp.dma_start(b2[q], a["b2"][e].to_broadcast([P, D])).then_inc(w2exp0_in[q], 16)

            with sp.Fori(1, NH // 2) as pair:
                for q in range(2):
                    sp.wait_ge(proj_ready, 12 * pair + 6 * q - 6)
                    sp.dma_start(wqkv[q], a["wqkv"][bass.ds(2 * pair + q, 1)].rearrange("h p (c w) -> (h p) c w", c=DC)
                                 ).then_inc(wqkv_in[q], 16)

            def load_slots(e, q):
                r = a_slots(e)
                sp.dma_start(xe[q][:, 0:2, :], r[0:256, :].rearrange("(s p) d -> p s d", p=P)).then_inc(xe_in[q], 16)
                sp.dma_start(xe[q][0:SROWS[2], 2, :], r[256:SLOTS, :]).then_inc(xe_in[q], 16)

            def a_slots(e):
                if isinstance(e, int):
                    return slots_d[e * SLOTS:(e + 1) * SLOTS, :]
                return slots_d.rearrange("(e r) d -> e r d", e=NE)[bass.ds(e, 1)].rearrange("e r d -> (e r) d")

            sp.wait_ge(vals_done, VALS0 + 2 * NH)
            for e in range(2):
                load_first(e, e)
                load_second(e, e)
            sp.wait_ge(slots_put, 16 * 2 * NT)
            for e in range(2):
                load_slots(e, e)
            sp.wait_ge(s_done, NT // 2)
            sp.dma_start(sw[:, 0:WPACK], a["sw"]).then_inc(sw_in, 16)
            sp.dma_start(swu, a["swu"]).then_inc(sw_in, 16)
            sp.dma_start(sb2, a["sb2"].to_broadcast([P, D])).then_inc(sw_in, 16)

            rows_e = rows_d.rearrange("(e r) d -> e r d", e=NE)

            def store_rows(e, q):
                sp.wait_ge(y_done, Y0 + 3 * e + 3)
                r = rows_e[bass.ds(e, 1)].rearrange("e r d -> (e r) d")
                sp.dma_start(r[0:256, :].rearrange("(s p) d -> p s d", p=P), yE[q][:, 0:2, :]).then_inc(rows_out[q], 16)
                sp.dma_start(r[256:SLOTS, :], yE[q][0:SROWS[2], 2, :]).then_inc(rows_out[q], 16)

            with sp.Fori(0, NE // 2 - 1) as pair:
                for q in range(2):
                    e = 2 * pair + q
                    sp.wait_ge(hid_done, HID0 + 9 * e + 9)
                    load_first(e + 2, q)
                    store_rows(e, q)
                    load_second(e + 2, q)
                    load_slots(e + 2, q)
            for q in range(2):
                store_rows(NE - 2 + q, q)

            if layers > 1:
                sp.dma_start(w_rwkv, a["w_rwkv"].rearrange("p (i c o) -> p i c o", i=4, c=DC)).then_inc(w1_in, 16)
                sp.dma_start(part(arenaC, 4160, DC * D), a["w_lin"]).then_inc(wlin_in, 16)
                sp.dma_start(lin_scale, a["lin_scale"].to_broadcast([P, D])).then_inc(wlin_in, 16)
                sp.dma_start(lin_bias, a["lin_bias"].to_broadcast([P, D])).then_inc(wlin_in, 16)
            if layers > 2:
                sp.wait_ge(x_done, NT // 2)
                sp.dma_start(part(arenaD, 7168, NF * D), a["w_down3"]).then_inc(wff3_in, 16)
                sp.dma_start(part(arenaC, 0, 2048), a["w2"]).then_inc(w2_in, 16)

                def gateup_in(e, q):
                    src = a["wexp2"][e] if isinstance(e, int) else a["wexp2"][bass.ds(e, 1)].rearrange("e p n -> (e p) n")
                    sp.dma_start(part(arenaD, 1536 * q, 1024), src[:, 0:1024]).then_inc(w2exp_in[q], 16)

                def down_in(e, q):
                    src = a["wexp2"][e] if isinstance(e, int) else a["wexp2"][bass.ds(e, 1)].rearrange("e p n -> (e p) n")
                    sp.dma_start(part(arenaD, 1536 * q + 1024, 512), src[:, 1024:1536]).then_inc(wdown_in[q], 16)

                def following(e, q):
                    sp.wait_ge(up_ready, 4 * e + 4)
                    gateup_in(e + 2, q)
                    sp.wait_ge(e2_ready, 8 * e)
                    down_in(e + 1, 1 - q)

                for q in range(2):
                    gateup_in(q, q)
                    down_in(q, q)
                sp.dma_start(part(arenaC, 2048, 2048), a["w3"]).then_inc(w3_in, 16)
                sp.dma_start(part(arenaD, 5120, 2048), a["wff3"][:, 2048:4096]).then_inc(w3_in, 16)
                sp.wait_ge(up_ready, 4)
                gateup_in(2, 0)
                with sp.Fori(0, E2 // 2 - 2) as pair:
                    following(2 * pair + 1, 1)
                    following(2 * pair + 2, 0)
                following(E2 - 3, 1)
                sp.wait_ge(e2_ready, 8 * E2 - 16)
                down_in(E2 - 1, 1)
                sp.wait_ge(e2_ready, 8 * E2)
                sp.dma_start(part(arenaD, 3072, 2048), a["wff3"][:, 0:2048]).then_inc(wgate3_in, 16)
            sp.wait_ge(x_done, layers * NT // 2)
            sp.dma_start(out.rearrange("(n p) d -> p n d", p=P), x[:, :, :]).then_inc(x_out, 16)
            sp.wait_ge(x_out, 16)

        @block.gpsimd
        def _(pool):
            pool.memset(mhalf[:, :], -0.5).then_inc(mhalf_set, 1)
            pool.memset(ones[:, :], 1.0).then_inc(ones_set, 1)
            pool.memset(arenaB[:, 0:NE * SLOTS // P * D], 0.0).then_inc(zeros_set, 1)
            for q in range(2):
                pool.sem_inc(rows_out[q], ROWS0)

            def rsqrt(layer):
                pool.wait_ge(mhalf_set, 1)
                pool.wait_ge(ln_var, layer + 1)
                pool.tensor_tensor(rstd[:, :], veps[:, :], mhalf[:, 0:NT], ALU.pow).then_inc(ln_rstd, 1)

            def rotary_attention():
                def heads(s0, which):
                    return qkv2[:, 4 * s0:4 * s0 + 4, which * D:(which + 1) * D]

                def table(at, half=None):
                    v = con[:, at:at + D]
                    if half is None:
                        return v.unsqueeze(1).to_broadcast([P, 4, D])
                    return v.rearrange("p (h two i) -> p h two i", h=H2, two=2)[:, :, half, :].unsqueeze(1).to_broadcast([P, 4, H2, 8])

                def halves(v, half):
                    return v.rearrange("p t (h two i) -> p t h two i", h=H2, two=2)[:, :, :, half, :]

                pool.wait_ge(qkv_done, 2 * NT)
                r3, p3 = (m.rearrange("p t h e -> p t (h e)") for m in (rot, prod))
                for which in range(2):
                    v = heads(1, which)
                    for half in range(2):
                        link(pool.tensor_tensor(halves(r3, half), halves(v, 1 - half), table(C_SIN, half), ALU.mult))
                    link(pool.tensor_tensor(v, v, table(C_COS), ALU.mult))
                    link(pool.tensor_tensor(v, v, r3, ALU.add))
                link(pool.memset(sc2[:, 0, 1, :], 4.0 * BLOCKED))
                for s0, u0 in ((0, 0), (1, 0), (1, 1)):
                    link(pool.tensor_tensor(p3, heads(s0, 0), heads(u0, 1), ALU.mult))
                    src = p3.rearrange("p t (h e) -> p (t h) e", h=H2)
                    for lv, w in enumerate((8, 4, 2, 1)):
                        dst = tree[:, 0:64 * w].rearrange("p (m e) -> p m e", e=w) if w > 1 and lv % 2 == 0 else \
                            tree[:, 512:512 + 64 * w].rearrange("p (m e) -> p m e", e=w) if w > 1 else \
                            sc2[:, s0, u0, :].unsqueeze(2)
                        link(pool.tensor_tensor(dst, src[:, :, 0:w], src[:, :, w:2 * w], ALU.add))
                        src = dst
                pool.tensor_scalar(sc2, sc2, HD2 ** -0.5, None, ALU.mult).then_inc(sc_done, 1)
                pool.wait_ge(prob2_done, 2)
                for s0 in range(2):
                    for u0 in range(2):
                        w = sc2[:, s0, u0, :].rearrange("p (t h) -> p t h", h=H2).unsqueeze(3).to_broadcast([P, 4, H2, HD2])
                        v = heads(u0, 2).rearrange("p t (h e) -> p t h e", h=H2)
                        link(pool.tensor_tensor(rot if u0 == 0 else prod, v, w, ALU.mult))
                    pool.tensor_tensor(ctx_tok[:, 4 * s0:4 * s0 + 4, :], r3, p3, ALU.add).then_inc(ctx_done, 1)
                    pool.wait_ge(ctx_done, s0 + 1)

            link = Link(pool, pool_link)
            rsqrt(0)

            def split_qkv(h, q, turn):
                pool.wait_ge(wqkv_in[q], 16 * turn + 16)
                pool.tensor_tensor(r(wqkv_hi[q]), wqkv[q], ones[:, 0:1].unsqueeze(1).to_broadcast([P, DC, 3 * DH]), ALU.mult
                                   ).then_inc(wqkv_rounded, 1)
                pool.wait_ge(wqkv_rounded, h + 1)
                pool.tensor_tensor(r(wqkv[q]), wqkv[q], rounded(wqkv_hi[q]), ALU.subtract).then_inc(wqkv_split, 1)

            def rest_k(h, q, b):
                sl = slice(b * S, (b + 1) * S)
                pool.wait_ge(kfull_done, 2 * h + b + 1)
                pool.tensor_tensor(r(klo[q][:, sl]), klo[q][:, sl], rounded(kT[q][:, sl]), ALU.subtract).then_inc(klo_done, 1)

            def head(h, q, turn):
                split_qkv(h + 2, q, turn)
                rest_k(h + 1, 1 - q, 0)
                rest_k(h + 1, 1 - q, 1)

            pool.wait_ge(ones_set, 1)
            split_qkv(0, 0, 0)
            split_qkv(1, 1, 0)
            rest_k(0, 0, 0)
            rest_k(0, 0, 1)
            head(0, 0, 1)
            with pool.Fori(0, NH // 2 - 2) as pair:
                head(2 * pair + 1, 1, pair + 1)
                head(2 * pair + 2, 0, pair + 2)
            head(NH - 3, 1, NH // 2 - 1)
            rest_k(NH - 1, 1, 0)
            rest_k(NH - 1, 1, 1)
            pool.wait_ge(at_done, 2)
            pool.wait_ge(slots_zero, 16)
            for t in range(NT):
                for k in range(2):
                    pool.indirect_dma_start(out=slots_d, out_offset=bass.IndirectOffsetOnAxis(put_at[:, t, k:k + 1], 0),
                                            in_=xn[:, t, :], in_offset=None, bounds_check=NE * SLOTS - 1,
                                            oob_is_err=False).then_inc(slots_put, 16)

            def split_expert(e, w, hi, wd_hi_):
                for n, (v, h) in ((4, (w[:, 0:W_D], hi[:, 0:W_D])), (5, (w[:, W_D:W_B], wd_hi_)),
                                  (7, (w[:, W_2:W_2 + 1024], hi[:, -2048:-1024])), (9, (w[:, W_2 + 1024:WPACK], hi[:, -1024:]))):
                    pool.wait_ge(w_rounded, 9 * e + n)
                    pool.tensor_tensor(r(v), v, rounded(h), ALU.subtract).then_inc(w_split, 1)

            wd_flat = [v.rearrange("p c r -> p (c r)") for v in wd_hi]
            split_expert(0, wexp[0], wexp_hi[0], wd_flat[0])
            with pool.Fori(0, NE // 2 - 1) as pair:
                split_expert(2 * pair + 1, wexp[1], wexp_hi[1], wd_flat[1])
                split_expert(2 * pair + 2, wexp[0], wexp_hi[0], wd_flat[0])
            split_expert(NE - 1, wexp[1], wexp_hi[1], wd_flat[1])
            split_expert(NE, sw, sw_hi, sw_hi[:, W_D:W_B])
            for q in range(2):
                pool.wait_ge(rows_out[q], ROWS0 + 32 * NE // 2)
            for t in range(NT):
                for k in range(2):
                    pool.indirect_dma_start(out=got[k][:, t, :], out_offset=None, in_=rows_d,
                                            in_offset=bass.IndirectOffsetOnAxis(get_at[:, t, k:k + 1], 0),
                                            bounds_check=NE * SLOTS - 1, oob_is_err=False).then_inc(rows_got, 16)

            if layers > 1:
                rsqrt(1)
            def split_flat(n, v, hi):
                pool.tensor_tensor(r(hi), v, ones[:, 0:1].to_broadcast([P, v.shape[1]]), ALU.mult).then_inc(wq_rounded, 1)
                pool.wait_ge(wq_rounded, n)
                pool.tensor_tensor(r(v), v, rounded(hi), ALU.subtract).then_inc(wq_split, 1)

            if layers > 2:
                pool.wait_ge(w2_in, 16)
                split_flat(1, part(arenaC, 0, DC * 768), part(arenaC, 10752, DC * 768))
                pool.wait_ge(had_copied, 4)
                for stage, (src, dst) in enumerate([(had_b, w_down3), (w_down3, had_b), (had_b, w_down3)]):
                    step = 1 << stage
                    v = [m.rearrange("p (u two w) d -> p u two (w d)", two=2, w=step) for m in (src, dst)]
                    pool.tensor_tensor(v[1][:, :, 0], v[0][:, :, 0], v[0][:, :, 1], ALU.add).then_inc(had_done, 1)
                    pool.tensor_tensor(v[1][:, :, 1], v[0][:, :, 0], v[0][:, :, 1], ALU.subtract).then_inc(had_done, 1)
                    pool.wait_ge(had_done, 2 * stage + 2)
                rsqrt(2)
                rotary_attention()
            if layers > 3:
                pool.wait_ge(w3_in, 32)
                split_flat(2, part(arenaC, 2048, DC * 768), part(arenaB, 0, DC * 768))
                rsqrt(3)
                for i in (1, 0):
                    for n in range(2):
                        pool.wait_ge(ff3_rounded, 4 * (1 - i) + 2 * n + 2)
                        v, h = part(arenaD, 3072 + 2048 * i + 1024 * n, 1024), part(arenaB, 1536 + 2048 * i + 1024 * n, 1024)
                        pool.tensor_tensor(r(v), v, rounded(h), ALU.subtract).then_inc(ff3_split, 1)
                for t in range(NT):
                    pool.wait_ge(ms_done, t + 1)
                    pool.tensor_tensor(rmsr[:, t, :], rms[:, t, :], mhalf[:, 0:32], ALU.pow).then_inc(rms_done, 1)
                for u in range(32):
                    pool.wait_ge(exp3_done, 4 * u + 4)
                    d = prob3[:, u % 2, :, 0:P]
                    pool.tensor_tensor(d, d, con[:, C_CAUSAL:C_CAUSAL + P].unsqueeze(1).to_broadcast([P, 4, P]), ALU.mult
                                       ).then_inc(causal_done, 1)

        @block.tensor
        def _(pe):
            def turn_xn(layer):
                pe.wait_ge(con_in, 16)
                for t in range(NT):
                    pe.wait_ge(xn_done, NT * layer + t + 1)
                    for c in range(DC):
                        o = bank[t // 2][:, (t % 2) * 256 + c * P:(t % 2) * 256 + (c + 1) * P]
                        mm = pe.transpose(o, xn[:, t, c * P:(c + 1) * P], ident)
                    mm.then_inc(turn_ready, 1)
                pe.wait_ge(xnT_act, XT[layer])
                pe.wait_ge(xnT_dve, XT[layer])

            turn_xn(0)
            pe.wait_ge(gate_in, 16)
            for t in range(NT):
                for n, (v, c) in enumerate((v, c) for v in (xnT, xlo) for c in range(DC)):
                    mm = pe.matmul(bank[7][:, t * NE:(t + 1) * NE], rounded(v[:, c, t * P:(t + 1) * P]), gate[:, c, :],
                                   start=(n == 0), stop=(n == 2 * DC - 1))
            mm.then_inc(logits_ready, 1)

            PROJ = [(0, 0), (1, 0), (0, 1), (1, 1), (2, 0), (2, 1)]

            def project_tile(h, q, n, first=False):
                w, b = PROJ[n]
                if not first or n >= 3:
                    s, v = [(kfull_done, 2 * h), (v_done, 2 * h - 1), (v_done, 2 * h),
                            (qlo_done, 2 * h + 1), (kfull_done, 2 * h + 1), (qlo_done, 2 * h + 2)][n]
                    pe.wait_ge(s, v)
                for c in range(DC):
                    mm = product(pe, bank[n % 3][:, :], [m[q][:, c, w * DH:(w + 1) * DH] for m in (wqkv_hi, wqkv)],
                                 [m[:, c, b * S:(b + 1) * S] for m in (xnT, xlo)], c == 0, c == DC - 1)
                mm.then_inc(proj_ready, 1)


            def score(h, q, n):
                b = n // ST
                if n % ST == 0:
                    pe.wait_ge(qlo_done, 2 * h + 1 + b)
                    pe.wait_ge(klo_done, 2 * h + 1 + b)
                pe.wait_ge(exp_done, 8 * h + n + 1)
                product(pe, bank[3 + n % 4][:, :], [m[q][:, n * P:(n + 1) * P] for m in (qT, qlo)],
                        [m[q][:, b * S:(b + 1) * S] for m in (kT, klo)], True, True).then_inc(score_ready, 1)

            def colsum(h, b):
                pe.wait_ge(acc_done, ACC0 + 8 * h + 4 * b + 4)
                pe.wait_ge(vals_done, 2 * h + b + 1)
                pe.matmul(bank[7][:, :], ones[:, :], acc[b], start=True, stop=True).then_inc(colsum_ready, 1)

            def head(h, q, first=False, last=False):
                for n in range(8):
                    score(h, q, n)
                    if n == 2 and not first:
                        colsum(h - 1, 1)
                    if n == 6:
                        colsum(h, 0)
                    tile = {1: 0, 2: 1, 4: 2, 5: 3, 6: 4, 7: 5}.get(n)
                    if tile is not None and not last:
                        if tile == 0:
                            pe.wait_ge(wqkv_split, h + 2)
                        project_tile(h + 1, 1 - q, tile)

            pe.wait_ge(wqkv_split, 1)
            for n in range(6):
                project_tile(0, 0, n, first=True)
            pe.wait_ge(ones_set, 1)
            pe.wait_ge(oh_done, 1)
            pe.matmul(bank[7][:, 0:128], con[:, C_TRI:C_TRI + P], oh.rearrange("p t k e -> p (t k e)"), start=True, stop=False)
            pe.matmul(bank[7][:, 0:128], ones[:, :], before.rearrange("p t k e -> p (t k e)"), start=False, stop=True
                      ).then_inc(place_ready, 1)
            head(0, 0, first=True)
            with pe.Fori(0, NH // 2 - 1) as pair:
                head(2 * pair + 1, 1)
                head(2 * pair + 2, 0)
            head(NH - 1, 1, last=True)
            colsum(NH - 1, 1)

            pe.wait_ge(wo_in, 16)
            pe.wait_ge(vals_done, VALS0 + 2 * NH)
            for t in range(NT):
                for h in range(NH):
                    mm = pe.matmul(bank[t // 2][:, (t % 2) * D:(t % 2 + 1) * D], vals[:, h, t * P:(t + 1) * P], wo[:, h, :],
                                   start=(h == 0), stop=(h == NH - 1))
                mm.then_inc(s_ready, 1)

            pe.wait_ge(s_done, NT // 2)

            def turn(e, pair, q):
                pe.wait_ge(xe_in[q], 32 * pair + 32)
                pe.wait_ge(xeT_done, 2 * e + 2)
                for c in range(DC):
                    for s, rows in enumerate(SROWS):
                        mm = pe.transpose(bank[c][:, s * P:s * P + rows], xe[q][0:rows, s, c * P:(c + 1) * P],
                                          ident[0:rows, 0:rows])
                    mm.then_inc(xeT_ready, 1)

            def hidden(e, q):
                pe.wait_ge(w_split, 4 * e + 2)
                pe.wait_ge(xeT_done, TURN0 + 2 * e + 2)
                for n in range(NF + 1):
                    f = n - 1
                    pe.wait_ge(hid_done, 9 * e + n + 1)
                    for c in range(DC):
                        w = [m[q][:, c, f * P:(f + 1) * P] if n else v[q][:, c, :] for m, v in ((w1_hi, wd_hi), (w1, wd))]
                        mm = product(pe, bank[2 + n % 3][0:P if n else RANK, 0:SLOTS], w,
                                     [m[q][:, c, :] for m in (xeT, xeT_lo)], c == 0, c == DC - 1)
                    mm.then_inc(hid_ready, 1)

            def rows_of(e, turn, q):
                pe.wait_ge(w2exp0_in[q], 48 * turn + 48)
                for s, rows in enumerate(SROWS):
                    pe.wait_ge(y_done, 3 * e + s + 1)
                    o = bank[5 + s][0:rows, 0:D]
                    for f in range(NF):
                        if s == 0:
                            if f % 4 == 0:
                                pe.wait_ge(w_split, 4 * e + 3 + f // 4)
                            pe.wait_ge(h_split, NF * e + f + 1)
                        product(pe, o, [m[:, f, s * P:s * P + rows] for m in (hE_hi, hE)], [m[q][:, f, :] for m in (w2_hi, w2)],
                                f == 0, False)
                    pe.matmul(o, aE[:, s * P:s * P + rows], wu[q], start=False, stop=True).then_inc(y_ready, 1)

            turn(0, 0, 0)
            with pe.Fori(0, NE // 2 - 1) as pair:
                for q in range(2):
                    e = 2 * pair + q
                    hidden(e, q)
                    turn(e + 1, pair + q, 1 - q)
                    rows_of(e, pair, q)
            hidden(NE - 2, 0)
            turn(NE - 1, NE // 2 - 1, 1)
            rows_of(NE - 2, NE // 2 - 1, 0)
            hidden(NE - 1, 1)
            rows_of(NE - 1, NE // 2 - 1, 1)

            pe.wait_ge(w_split, 4 * NE + 2)
            for b in range(B):
                for f in range(NF + 1):
                    n = (NF + 1) * b + f
                    if n >= 4:
                        pe.wait_ge(shid_done, n - 3)
                    for c in range(DC):
                        w = [m[:, c, f * P:(f + 1) * P] if f < NF else v[:, c, :] for m, v in ((sw1_hi, swd_hi), (sw1, swd))]
                        mm = product(pe, bank[n % 4][0:P if f < NF else RANK, :], w, [m[:, c, b * S:(b + 1) * S] for m in (xnT, xlo)],
                                     c == 0, c == DC - 1)
                    mm.then_inc(shid_ready, 1)
            pe.wait_ge(shid_done, B * (NF + 1))
            pe.wait_ge(y_done, Y0 + 3 * NE)
            pe.wait_ge(w_split, 4 * NE + 4)
            pe.wait_ge(sw_in, 48)
            for t in range(NT):
                b = t // ST
                o = bank[4 + t // 2][:, (t % 2) * D:(t % 2 + 1) * D]
                for f in range(NF):
                    if t % ST == 0:
                        pe.wait_ge(hS_split, NF * b + f + 1)
                    product(pe, o, [hS_hi[b][:, f, t % ST * P:(t % ST + 1) * P], hS[:, f, t * P:(t + 1) * P]],
                            [m[:, f, :] for m in (sw2_hi, sw2)], f == 0, False)
                pe.matmul(o, aS[:, t * P:(t + 1) * P], swu, start=False, stop=True).then_inc(sh_ready, 1)

            def token_major(lhs, w, first_bank, free, ready):
                for t in range(NT):
                    if free and t % 2 == 0:
                        free(t // 2)
                    for c in range(DC):
                        mm = pe.matmul(bank[first_bank + t // 2][:, (t % 2) * D:(t % 2 + 1) * D], lhs[:, c, t * P:(t + 1) * P],
                                       w[:, c, :], start=(c == 0), stop=(c == DC - 1))
                    mm.then_inc(ready, 1)

            def qkv_rows(w, w_hi, layer):
                for t in range(NT):
                    if t >= 3:
                        pe.wait_ge(qkv_done, 2 * (NT * (layer - 2) + t) - 4)
                    b0 = 2 * (t % 3)
                    for o, w0, n in ((bank[b0][:, :], 0, 512), (bank[b0 + 1][:, 0:D], 512, D)):
                        for c in range(DC):
                            mm = product(pe, o, [m[:, c, t * P:(t + 1) * P] for m in (xnT, XLO[layer])],
                                         [m[:, c, w0:w0 + n] for m in (w_hi, w)], c == 0, c == DC - 1)
                    mm.then_inc(qkv_ready, 1)

            if layers > 1:
                turn_xn(1)
                pe.wait_ge(w1_in, 16)
                n = 0
                for b in range(B):
                    for i in range(3):
                        pe.wait_ge(mix_done, 3 * b + i + 1)
                        for o in range(DC):
                            if n >= 4:
                                m = n - 4
                                bb_, ii, oo = m // 6, m % 6 // 2, m % 2
                                if ii == 1:
                                    pe.wait_ge(vv_done, 2 * bb_ + oo + 1)
                                else:
                                    pe.wait_ge(kr_done, 4 * bb_ + (2 if ii else 0) + oo + 1)
                            for c in range(DC):
                                mm = pe.matmul(bank[4 + n % 4][:, :], w_rwkv[:, i, c, o * P:(o + 1) * P],
                                               mixed[:, i, c, b * S:(b + 1) * S], start=(c == 0), stop=(c == DC - 1))
                            mm.then_inc(kvr_ready, 1)
                            n += 1
                pe.wait_ge(wlin_done, 1)
                token_major(xnT, w_lin, 0, None, g_ready)
                pe.wait_ge(kr_done, 8)
                pe.wait_ge(rwkv_done, 2)
                token_major(rr, w_rwkv[:, 3], 4, None, s_ready)
            if layers > 2:
                pe.wait_ge(g_done, 4)
                pe.wait_ge(wff3_in, 16)
                for i in range(4):
                    pe.matmul(bank[i][:, :], con[:, C_HAD:C_HAD + P], w_down3[:, 2 * i:2 * i + 2, :].rearrange("p f d -> p (f d)"),
                              start=True, stop=True).then_inc(had_ready, 1)
                pe.wait_ge(had_copied, 4)
                turn_xn(2)
                for t in range(NT):
                    for n, (v, c) in enumerate((v, c) for v in (xnT, xlo) for c in range(DC)):
                        mm = pe.matmul(bank[7][:, t * E2:(t + 1) * E2], rounded(v[:, c, t * P:(t + 1) * P]), gate2[:, c, :],
                                       start=(n == 0), stop=(n == 2 * DC - 1))
                mm.then_inc(z_ready, 1)
                pe.wait_ge(wq_split, 1)
                qkv_rows(w_qkv2, w_qkv2_hi, 2)
                pe.wait_ge(qkv_done, 2 * NT)
                pe.wait_ge(z_done, 1)

                def gate_up(e, q):
                    pe.wait_ge(gateup_split, e + 1)
                    for n in range(4):
                        f, b = n // 2, n % 2
                        for i, (rdy, done) in enumerate(((gate_ready, silu2_done), (up_ready, gu_done))):
                            pe.wait_ge(done, 4 * e + n + 1)
                            for c in range(DC):
                                mm = product(pe, bank[2 * i + n % 2][:, :], [m[q][:, i, c, f * P:(f + 1) * P] for m in (wexp2_hi, wexp2)],
                                             [m[:, c, b * S:(b + 1) * S] for m in (xnT, xlo)], c == 0, c == DC - 1)
                            mm.then_inc(rdy, 1)

                def down(e, q):
                    pe.wait_ge(gu_split, 4 * e + 4)
                    pe.wait_ge(down_split, e + 1)
                    for t in range(NT):
                        if t % 2 == 0:
                            pe.wait_ge(e2_done, 8 * e + t + 2)
                        for f in range(DC):
                            mm = product(pe, bank[4 + t // 2][:, (t % 2) * D:(t % 2 + 1) * D], [m[q][:, f, t * P:(t + 1) * P] for m in (gu_hi, gu)],
                                         [m[q][:, 2, f, :] for m in (wexp2_hi, wexp2)], f == 0, f == DC - 1)
                        mm.then_inc(e2_ready, 1)

                gate_up(0, 0)
                with pe.Fori(0, E2 // 2 - 1) as pair:
                    for q in range(2):
                        gate_up(2 * pair + q + 1, 1 - q)
                        down(2 * pair + q, q)
                gate_up(E2 - 1, 1)
                down(E2 - 2, 0)
                pe.wait_ge(gu_done, GU0 + 4 * E2)
                pe.wait_ge(ctx_done, 2)
                for t in range(NT):
                    for c in range(DC):
                        mm = pe.transpose(bank[t // 2][:, (t % 2) * 256 + c * P:(t % 2) * 256 + (c + 1) * P],
                                          ctx_tok[:, t, c * P:(c + 1) * P], ident)
                    mm.then_inc(ctxT_ready, 1)
                down(E2 - 1, 1)
                pe.wait_ge(ctxT_done, 4)
                token_major(ctxT, w_dense, 0, None, s_ready)
            if layers > 3:
                turn_xn(3)
                pe.wait_ge(wq_split, 2)
                qkv_rows(w_qkv3, w_qkv3_hi, 3)
                pe.wait_ge(qkv_done, 4 * NT)

                def turn_qk(t):
                    pe.wait_ge(qk_done, t + 1)
                    if t >= 4:
                        pe.wait_ge(qT_done, t - 3)
                        pe.wait_ge(kT_done, t - 3)
                    for j in range(4):
                        mm = pe.transpose(bank[4 + t % 4][:, j * P:(j + 1) * P], qk3[:, t, j * P:(j + 1) * P], ident)
                    mm.then_inc(qkT_ready, 1)

                pe.wait_ge(ff3_split, 4)
                for n in range(2 * NF):
                    f, b = n // 2, n % 2
                    for i, (w, rdy, done) in enumerate((((w_gate3_hi, w_gate3), gate3_ready, silu3_done),
                                                        ((w_up3_hi, w_up3), up3_ready, hid3_done))):
                        if n >= 2:
                            pe.wait_ge(done, n - 1)
                        for c in range(DC):
                            mm = product(pe, bank[2 * i + n % 2][:, :], [m[:, c, f * P:(f + 1) * P] for m in w],
                                         [m[:, c, b * S:(b + 1) * S] for m in (xnT, xlo3)], c == 0, c == DC - 1)
                        mm.then_inc(rdy, 1)
                    if n >= 6 and n % 2 == 0 and (n - 6) // 2 < 5:
                        turn_qk((n - 6) // 2)
                for t in range(5, NT):
                    turn_qk(t)
                pe.wait_ge(qT_done, NT)
                pe.wait_ge(kT_done, NT)
                pe.wait_ge(silu3_done, 2 * NF)
                pe.wait_ge(hid3_done, 2 * NF)

                def unit(u):
                    return u // 16, u // 8 % 2, u // 4 % 2, u % 4

                def scores3(u):
                    b, c, j, kt = unit(u)
                    if u % 8 == 0:
                        pe.wait_ge(kz_done, 8 * (u // 8) + 8)
                    for hh in range(4):
                        if u:
                            pe.wait_ge(exp3_done, 4 * u - 3 + hh)
                        pe.matmul(bank[hh][:, 0:S - kt * P], kz[:, c, 2 * hh + j, kt * P:(kt + 1) * P],
                                  q3T[:, c, b * S + kt * P:(b + 1) * S], start=True, stop=True).then_inc(sc3_ready, 1)

                def mix3(u):
                    b, c, j, kt = unit(u)
                    pe.wait_ge(causal_done, u + 1)
                    if kt == 0 and u >= 8:
                        pe.wait_ge(norm3_done, u // 4 - 1)
                    for o, which in ((bank[4 + j], 0), (bank[6 + j], 1)):
                        for hh in range(4):
                            head = 4 * c + hh
                            w = ones[:, 0:32] if which else v3[:, ST * b + kt, 32 * head:32 * head + 32]
                            mm = pe.matmul(o[32 * hh:32 * hh + 32, kt * P:S], w, prob3[:, u % 2, hh, 0:S - kt * P],
                                           start=(kt == 0), stop=(kt == ST - 1), tile_position=(0, 32 * hh))
                    mm.then_inc(av_ready, 1)

                scores3(0)
                for u in range(32):
                    if u < 31:
                        scores3(u + 1)
                    mix3(u)
                pe.wait_ge(had_done, 6)
                for t in range(NT):
                    for f in range(NF):
                        mm = pe.matmul(bank[t // 2][:, (t % 2) * D:(t % 2 + 1) * D], hid3[:, f, t * P:(t + 1) * P], w_down3[:, f, :],
                                       start=(f == 0), stop=(f == NF - 1))
                    mm.then_inc(g3_ready, 1)
                pe.wait_ge(norm3_done, 8)
                token_major(yT3, w_out3, 4, None, s_ready)

        @block.vector
        def _(dve):
            link = Link(dve, dve_link)
            dve.sem_inc(vals_done, VALS0)
            dve.sem_inc(y_done, Y0)
            dve.sem_inc(acc_done, ACC0)

            def layernorm(layer):
                for t in range(NT):
                    ins = dve.bn_stats(stats[:, t, :], x[:, t, :])
                link(ins)
                for t in range(NT):
                    ins = dve.bn_aggr(meanvar[:, t, :], stats[:, t, :])
                link(ins)
                dve.tensor_scalar(veps[:, :], meanvar[:, :, 1], LN_EPS, None, ALU.add).then_inc(ln_var, 1)
                dve.wait_ge(ln_rstd, layer + 1)
                for t in range(NT):
                    dve.tensor_scalar(xn[:, t, :], x[:, t, :], meanvar[:, t, 0:1], rstd[:, t:t + 1],
                                      ALU.subtract, ALU.mult).then_inc(xn_done, 1)
                if SPLIT[layer]:
                    for i in range(4):
                        dve.wait_ge(xnT_act, XT[layer] - 3 + i)
                        dve.tensor_tensor(r(quarter(XLO[layer], i)), turned_bank(i), rounded(quarter(xnT, i)), ALU.subtract).then_inc(xnT_dve, 1)
                    return
                for i in (1, 3):
                    dve.wait_ge(turn_ready, NT * layer + 2 * i + 2)
                    dve.tensor_copy(quarter(xnT, i), turned_bank(i)).then_inc(xnT_dve, 1)

            dve.wait_ge(x_in, 16)
            layernorm(0)

            def bc(v):
                return v.unsqueeze(2).to_broadcast([P, NT, NE])

            iota = con[:, C_IOTA:C_IOTA + 64].rearrange("p (t e) -> p t e", t=NT)
            dve.wait_ge(con_in, 16)
            dve.wait_ge(logits_ready, 1)
            link(dve.tensor_copy(lg, bank[7][:, 0:64].rearrange("p (t e) -> p t e", t=NT)))

            def choose(k):
                link(dve.tensor_reduce(top[:, k, :], lg, AX.X, ALU.max))
                link(dve.tensor_tensor(eq, lg, bc(top[:, k, :]), ALU.is_equal))
                link(dve.tensor_tensor(eq, eq, iota, ALU.mult))
                link(dve.tensor_reduce(idx[:, :, k], eq, AX.X, ALU.min))
                link(dve.tensor_tensor(oh[:, :, k, :], iota, bc(idx[:, :, k]), ALU.is_equal))

            choose(0)
            dve.tensor_tensor(ex, lg, bc(top[:, 0, :]), ALU.subtract).then_inc(lg_shift, 1)
            link(dve.scalar_tensor_tensor(lg, oh[:, :, 0, :], OUT_OF_REACH, lg, ALU.mult, ALU.add))
            choose(1)
            dve.tensor_tensor(gap, top[:, 1, :], top[:, 0, :], ALU.subtract).then_inc(lg_shift, 1)
            dve.memset(before[:, 0, :, :], 0.0)
            for t in range(1, NT):
                if t == 1:
                    link(dve.tensor_copy(before[:, 1, :, :], oh[:, 0, :, :]))
                else:
                    link(dve.tensor_tensor(before[:, t, :, :], before[:, t - 1, :, :], oh[:, t - 1, :, :], ALU.add))
            dve.memset(kslot[:, :, 0], 8.0 * SLOTS).then_inc(oh_done, 1)
            link(dve.memset(kslot[:, :, 1], 8.0 * SLOTS + CAP))
            def rest_q(h, q, b):
                dve.wait_ge(q_done, 2 * h + b + 1)
                sl = slice(b * S, (b + 1) * S)
                dve.scalar_tensor_tensor(r(qlo[q][:, sl]), bank[2 if b else 0][:, :], DH ** -0.5, rounded(qT[q][:, sl]),
                                         ALU.mult, ALU.subtract).then_inc(qlo_done, 1)

            for b in range(B):
                rest_q(0, 0, b)
            dve.wait_ge(place_ready, 1)
            link(dve.tensor_tensor(ohp.rearrange("p t k e -> p (t k e)"), oh.rearrange("p t k e -> p (t k e)"),
                                   bank[7][:, 0:128], ALU.mult))
            link(dve.tensor_reduce(pos.rearrange("p t k -> p (t k)"), ohp.rearrange("p t k e -> p (t k) e"), AX.X, ALU.add))
            link(dve.tensor_scalar(keep, pos, float(CAP), None, ALU.is_lt))
            link(dve.scalar_tensor_tensor(base, idx, float(SLOTS), kslot, ALU.mult, ALU.add))
            link(dve.tensor_tensor(slot, base, pos, ALU.add))
            link(dve.scalar_tensor_tensor(slot, keep, -NO_SLOT, slot, ALU.mult, ALU.add))
            dve.tensor_scalar(put_at[:, :, :], slot, NO_SLOT, None, ALU.add).then_inc(at_done, 1)
            link(dve.tensor_scalar(pos, pos, CAP - 1.0, None, ALU.min))
            dve.tensor_tensor(get_at[:, :, :], base, pos, ALU.add).then_inc(at_done, 1)
            dve.wait_ge(ex_done, 2)
            link(dve.tensor_reduce(esum, ex, AX.X, ALU.add))
            link(dve.reciprocal(einv, esum))
            link(dve.tensor_tensor(wt[:, :, 0], keep[:, :, 0], einv, ALU.mult))
            link(dve.tensor_tensor(wt[:, :, 1], keep[:, :, 1], einv, ALU.mult))
            link(dve.tensor_tensor(wt[:, :, 1], wt[:, :, 1], gap, ALU.mult))

            def row_max(h, n):
                dve.wait_ge(score_ready, 8 * h + n + 1)
                dve.tensor_reduce(negmax[:, n % 4:n % 4 + 1], bank[3 + n % 4][:, :], AX.X, ALU.max, negate=True
                                  ).then_inc(max_done, 1)

            def invert(h, n):
                dve.wait_ge(exp_done, EXP0 + 8 * h + n + 1)
                dve.reciprocal(rowinv[:, n % 4:n % 4 + 1], rowsum[:, n % 4:n % 4 + 1]).then_inc(inv_done, 1)

            def accumulate(h, n):
                inv = rowinv[:, n % 4:n % 4 + 1]
                dve.wait_ge(inv_done, 8 * h + n + 1)
                if n % ST == 0:
                    ins = dve.tensor_scalar(acc[n // ST], prob[n % 4], inv, None, ALU.mult)
                else:
                    dve.wait_ge(acc_done, ACC0 + 8 * h + n)
                    ins = dve.scalar_tensor_tensor(acc[n // ST], prob[n % 4], inv, acc[n // ST], ALU.mult, ALU.add)
                ins.then_inc(acc_done, 1)

            def values(h, q, b):
                dve.wait_ge(colsum_ready, 2 * h + b + 1)
                dve.wait_ge(v_done, 2 * h + b + 1)
                o = vals[:, h, b * S:(b + 1) * S] if isinstance(h, int) else \
                    vals[:, bass.ds(h, 1), b * S:(b + 1) * S].rearrange("p h t -> p (h t)")
                dve.tensor_tensor(o, bank[7][:, :], vT[q][:, b * S:(b + 1) * S], ALU.mult).then_inc(vals_done, 1)

            def head(h, q, first=False, last=False):
                for n in range(8):
                    before = None if first and n == 0 else (h - 1, 7) if n == 0 else (h, n - 1)
                    if before:
                        invert(*before)
                    row_max(h, n)
                    if before:
                        accumulate(*before)
                    if n in (3, 5) and not last:
                        rest_q(h + 1, 1 - q, n // 5)
                    if n == 3 and not first:
                        values(h - 1, 1 - q, 1)
                    if n == 7:
                        values(h, q, 0)

            dve.wait_ge(slots_zero, 16)
            head(0, 0, first=True)
            with dve.Fori(0, NH // 2 - 1) as pair:
                head(2 * pair + 1, 1)
                head(2 * pair + 2, 0)
            head(NH - 1, 1, last=True)
            invert(NH - 1, 7)
            accumulate(NH - 1, 7)
            values(NH - 1, 1, 1)
            for i in (1, 3):
                dve.wait_ge(s_ready, 2 * i + 2)
                dve.tensor_copy(g_tok[:, 2 * i:2 * i + 2, :].rearrange("p a d -> p (a d)"), bank[i][:, :]).then_inc(s_done, 1)

            def rest_rows(e, q):
                for c in range(DC):
                    dve.wait_ge(xeT_rounded, 2 * e + c + 1)
                    dve.tensor_tensor(r(xeT_lo[q][:, c, :]), bank[c][:, 0:SLOTS], rounded(xeT[q][:, c, :]), ALU.subtract).then_inc(xeT_done, 1)

            def expert(e, q, pair, last=False):
                for f in range(NF + 1):
                    if f < NF:
                        dve.wait_ge(hid_done, HID0 + 9 * e + f + 2)
                        dve.tensor_copy(r(hE_hi[:, f, :]), hE[:, f, :]).then_inc(h_rounded, 1)
                    if f:
                        dve.wait_ge(h_rounded, NF * e + f)
                        dve.tensor_tensor(r(hE[:, f - 1, :]), hE[:, f - 1, :], rounded(hE_hi[:, f - 1, :]), ALU.subtract).then_inc(h_split, 1)
                if not last:
                    rest_rows(e + 1, 1 - q)
                dve.wait_ge(rows_out[q], 32 * pair + 32)
                for s, rows in enumerate(SROWS):
                    dve.wait_ge(y_ready, 3 * e + s + 1)
                    dve.tensor_tensor(yE[q][0:rows, s, :], bank[5 + s][0:rows, 0:D], b2[q][0:rows, :], ALU.add
                                      ).then_inc(y_done, 1)

            rest_rows(0, 0)
            with dve.Fori(0, NE // 2 - 1) as pair:
                expert(2 * pair, 0, pair)
                expert(2 * pair + 1, 1, pair)
            expert(NE - 2, 0, NE // 2 - 1)
            expert(NE - 1, 1, NE // 2 - 1, last=True)
            for b in range(B):
                for f in range(NF + 1):
                    sl = slice(b * S, (b + 1) * S)
                    if f < NF:
                        dve.wait_ge(shid_done, (NF + 1) * b + f + 1)
                        dve.tensor_copy(r(hS_hi[b][:, f, :]), hS[:, f, sl]).then_inc(hS_rounded, 1)
                    if f:
                        dve.wait_ge(hS_rounded, NF * b + f)
                        dve.tensor_tensor(r(hS[:, f - 1, sl]), hS[:, f - 1, sl], rounded(hS_hi[b][:, f - 1, :]), ALU.subtract).then_inc(hS_split, 1)
            for i in range(NT // 2):
                dve.wait_ge(sh_ready, 2 * i + 2)
                dve.tensor_tensor(s_tok[:, 2 * i:2 * i + 2, :], bank[4 + i][:, :].rearrange("p (t d) -> p t d", t=2),
                                  sb2.unsqueeze(1).to_broadcast([P, 2, D]), ALU.add).then_inc(sh_done, 1)
            dve.wait_ge(sh_done, NT // 2)
            link(dve.tensor_scalar(s_tok[:, :, :], s_tok[:, :, :], 0.2, None, ALU.mult))
            dve.wait_ge(rows_got, 16 * 2 * NT)
            for k in range(2):
                for t in range(NT):
                    ins = dve.scalar_tensor_tensor(s_tok[:, t, :], got[k][:, t, :], wt[:, t, k:k + 1], s_tok[:, t, :],
                                                   ALU.mult, ALU.add)
                link(ins)
            dve.sem_inc(ffn_done, 1)

            def residual(layer):
                dve.wait_ge(silu_done, layer + 1)
                dve.wait_ge(s_done, (layer + 1) * NT // 2)
                link(dve.tensor_tensor(g_tok[:, :, :], g_tok[:, :, :], s_tok[:, :, :], ALU.mult))
                for i in range(NT // 2):
                    ins = dve.tensor_tensor(x[:, 2 * i:2 * i + 2, :], x[:, 2 * i:2 * i + 2, :], g_tok[:, 2 * i:2 * i + 2, :], ALU.add)
                    ins.then_inc(x_done, 1)
                link(dve.memset(veps[:, :], 0.0))

            def golden():
                def per(v):
                    return v.unsqueeze(2).to_broadcast([P, NT, E2])

                dve.wait_ge(vec_in, 48)
                dve.wait_ge(z_ready, 1)
                link(dve.reciprocal(temp, temp))
                link(dve.tensor_scalar(z2, bank[7][:, 0:64].rearrange("p (t e) -> p t e", t=NT), temp, None, ALU.mult))
                dve.sem_inc(z_done, 1)
                dve.wait_ge(inh_done, 1)
                link(dve.tensor_scalar(dist, inh, GOLD_C, None, ALU.subtract))
                dve.scalar_tensor_tensor(dist, dist, -1.0, dist, ALU.mult, ALU.max).then_inc(dist_done, 1)
                link(dve.tensor_scalar(zone, z2, Z_LO, None, ALU.is_ge))
                link(dve.scalar_tensor_tensor(zone, z2, 0.0, zone, ALU.is_le, ALU.mult))
                dve.wait_ge(gexp_done, 2)
                link(dve.tensor_tensor(gw, gw, zone, ALU.mult))
                link(dve.tensor_reduce(red8[:, 0, :], gw, AX.X, ALU.add))
                link(dve.tensor_scalar(red8[:, 1, :], red8[:, 0, :], 1e-8, None, ALU.is_lt))
                link(dve.tensor_copy(cand, fb))
                link(dve.memset(mask2, 0.0))
                for k in range(2):
                    link(dve.tensor_reduce(red8[:, 2, :], cand, AX.X, ALU.max))
                    link(dve.tensor_tensor(zone, cand, per(red8[:, 2, :]), ALU.is_equal))
                    link(dve.tensor_tensor(zone, zone, iota, ALU.mult))
                    link(dve.tensor_reduce(red8[:, 3, :], zone, AX.X, ALU.min))
                    link(dve.tensor_tensor(zone, iota, per(red8[:, 3, :]), ALU.is_equal))
                    link(dve.tensor_tensor(mask2, mask2, zone, ALU.add))
                    link(dve.scalar_tensor_tensor(cand, zone, -4.0, cand, ALU.mult, ALU.add))
                link(dve.tensor_tensor(fb, fb, mask2, ALU.mult))

                def normal(v):
                    link(dve.tensor_reduce(red8[:, 4, :], v, AX.X, ALU.add))
                    link(dve.tensor_scalar(red8[:, 4, :], red8[:, 4, :], 1e-8, None, ALU.max))
                    link(dve.reciprocal(red8[:, 4, :], red8[:, 4, :]))
                    link(dve.tensor_tensor(v, v, per(red8[:, 4, :]), ALU.mult))

                normal(fb)
                link(dve.tensor_tensor(fb, fb, per(red8[:, 1, :]), ALU.mult))
                link(dve.tensor_scalar(red8[:, 1, :], red8[:, 1, :], -1.0, 1.0, ALU.mult, ALU.add))
                link(dve.tensor_tensor(gw, gw, per(red8[:, 1, :]), ALU.mult))
                link(dve.tensor_tensor(gw, gw, fb, ALU.add))
                normal(gw)

            residual(0)


            def s_copy(layer):
                first_bank = (0, 4, 0, 4)[layer]
                for i in (1, 3):
                    dve.wait_ge(s_ready, NT * layer + 2 * i + 2)
                    o, v = s_tok[:, 2 * i:2 * i + 2, :].rearrange("p a d -> p (a d)"), bank[first_bank + i][:, :]
                    if layer == 3:
                        dve.tensor_scalar(o, v, 1.0 - LAMBDA_INIT, None, ALU.mult).then_inc(s_done, 1)
                    else:
                        dve.tensor_copy(o, v).then_inc(s_done, 1)

            if layers > 1:
                layernorm(1)
                dve.wait_ge(vec_in, 48)
                link(dve.tensor_scalar(offs, vec[:, 0:3, :], -1.0, 1.0, ALU.mult, ALU.add))
                link(dve.tensor_tensor(offs, offs, vec[:, 3:4, :].to_broadcast([P, 3, DC]), ALU.mult))
                dve.wait_ge(xnT_act, XT[1])
                dve.wait_ge(xnT_dve, XT[1])
                for b in range(B):
                    for i in range(3):
                        for c in range(DC):
                            ins = dve.tensor_scalar(mixed[:, i, c, b * S:(b + 1) * S], xnT[:, c, b * S:(b + 1) * S],
                                                    vec[:, i, c:c + 1], offs[:, i, c:c + 1], ALU.mult, ALU.add)
                        ins.then_inc(mix_done, 1)
                dve.wait_ge(wlin_in, 48)
                dve.tensor_tensor(w_lin, w_lin, lin_scale.unsqueeze(1).to_broadcast([P, DC, D]), ALU.mult).then_inc(wlin_done, 1)
                for b in range(B):
                    for o in range(DC):
                        dve.wait_ge(kvr_ready, 6 * b + 2 + o + 1)
                        dve.tensor_copy(vv[:, o, b * S:(b + 1) * S], bank[4 + (6 * b + 2 + o) % 4][:, :]).then_inc(vv_done, 1)
                for b in range(B):
                    sl = slice(b * S, (b + 1) * S)
                    dve.wait_ge(kr_done, 4 * b + 2)
                    w0 = kk[:, :, b * S:b * S + 1]
                    f = [first[:, i, :, b:b + 1] for i in range(4)]
                    pp, aa, bb = (vec[:, i, :].unsqueeze(2) for i in (6, 4, 5))
                    link(dve.tensor_tensor(f[0], w0, pp, ALU.max))
                    link(dve.tensor_tensor(f[1], pp, f[0], ALU.subtract))
                    link(dve.tensor_tensor(f[2], w0, f[0], ALU.subtract))
                    link(dve.tensor_scalar(kk[:, :, sl], kk[:, :, sl], 0.0, None, ALU.min))
                    dve.tensor_copy(w0, f[2]).then_inc(low_done, 1)
                for b in range(B):
                    sl = slice(b * S, (b + 1) * S)
                    dve.wait_ge(e_done, 2 * b + 2)
                    dve.wait_ge(vv_done, 2 * b + 2)
                    f = [first[:, i, :, b:b + 1] for i in range(4)]
                    aa, bb = (vec[:, i, :].unsqueeze(2) for i in (4, 5))
                    n0, d0 = vv[:, :, b * S:b * S + 1], kk[:, :, b * S:b * S + 1]
                    link(dve.tensor_tensor(vv[:, :, sl], vv[:, :, sl], kk[:, :, sl], ALU.mult))
                    link(dve.tensor_tensor(f[2], f[1], aa, ALU.mult))
                    link(dve.tensor_tensor(f[3], f[1], bb, ALU.mult))
                    link(dve.tensor_tensor(n0, n0, f[2], ALU.add))
                    link(dve.tensor_tensor(d0, d0, f[3], ALU.add))
                    link(dve.reciprocal(kk[:, :, sl], kk[:, :, sl]))
                    link(dve.tensor_tensor(vv[:, :, sl], vv[:, :, sl], kk[:, :, sl], ALU.mult))
                    dve.wait_ge(kr_done, 4 * b + 4)
                    dve.tensor_tensor(rr[:, :, sl], rr[:, :, sl], vv[:, :, sl], ALU.mult).then_inc(rwkv_done, 1)
                for i in range(NT // 2):
                    dve.wait_ge(g_ready, 2 * i + 2)
                    dve.tensor_tensor(g_tok[:, 2 * i:2 * i + 2, :], bank[i][:, :].rearrange("p (t d) -> p t d", t=2),
                                      lin_bias.unsqueeze(1).to_broadcast([P, 2, D]), ALU.add).then_inc(g_done, 1)
                dve.wait_ge(g_done, 4)
                dve.sem_inc(ffn_done, 1)
                s_copy(1)
                residual(1)
            if layers > 2:
                dve.sem_inc(gu_done, GU0)
                dve.sem_inc(e2_done, E20)
                layernorm(2)

                def gateup_rest(e, q):
                    dve.wait_ge(gateup_rounded, 2 * e + 2)
                    dve.tensor_tensor(r(wexp2[q][:, 0:2]), wexp2[q][:, 0:2], rounded(wexp2_hi[q][:, 0:2]), ALU.subtract).then_inc(gateup_split, 1)

                def down_rest(e, q):
                    dve.wait_ge(down_rounded, e + 1)
                    dve.tensor_tensor(r(wexp2[q][:, 2]), wexp2[q][:, 2], rounded(wexp2_hi[q][:, 2]), ALU.subtract).then_inc(down_split, 1)

                golden()
                gateup_rest(0, 0)
                dve.wait_ge(had_done, 6)
                link(dve.memset(g_tok[:, :, :], 0.0))

                def mult(e, q, n):
                    f, b = n // 2, n % 2
                    dve.wait_ge(up_ready, 4 * e + n + 1)
                    dve.wait_ge(silu2_done, 2 + 4 * e + n + 1)
                    v, h = (m[q][:, f, b * S:(b + 1) * S] for m in (gu, gu_hi))
                    dve.tensor_tensor(v, bank[2 + n % 2][:, :], gs[n % 2], ALU.mult).then_inc(gu_done, 1)
                    if n:
                        rest_gu(e, q, n - 1)
                    dve.wait_ge(gu_done, GU0 + 4 * e + n + 1)
                    dve.tensor_copy(r(h), v).then_inc(gu_rounded, 1)
                    if n == 3:
                        rest_gu(e, q, n)

                def rest_gu(e, q, n):
                    v, h = (m[q][:, n // 2, n % 2 * S:(n % 2 + 1) * S] for m in (gu, gu_hi))
                    dve.wait_ge(gu_rounded, 4 * e + n + 1)
                    dve.tensor_tensor(r(v), v, rounded(h), ALU.subtract).then_inc(gu_split, 1)

                def add_expert(e, q):
                    for t in range(NT):
                        dve.wait_ge(e2_ready, 8 * e + 2 * (t // 2) + 2)
                        w = gw[:, t, e:e + 1] if isinstance(e, int) else gw[:, t, bass.ds(e, 1)]
                        dve.scalar_tensor_tensor(g_tok[:, t, :], bank[4 + t // 2][:, (t % 2) * D:(t % 2 + 1) * D], w,
                                                 g_tok[:, t, :], ALU.mult, ALU.add).then_inc(e2_done, 1)
                    dve.wait_ge(e2_done, E20 + 8 * e + 8)

                for n in range(4):
                    mult(0, 0, n)
                gateup_rest(1, 1)
                down_rest(0, 0)
                with dve.Fori(0, E2 // 2 - 1) as pair:
                    for q in range(2):
                        for n in range(4):
                            mult(2 * pair + q + 1, 1 - q, n)
                        gateup_rest(2 * pair + q + 2, q)
                        down_rest(2 * pair + q + 1, 1 - q)
                        add_expert(2 * pair + q, q)
                dve.wait_ge(sc_done, 1)
                link(dve.tensor_tensor(mx2, sc2[:, :, 0, :], sc2[:, :, 1, :], ALU.max))
                for u0 in range(2):
                    dve.tensor_tensor(sc2[:, :, u0, :], sc2[:, :, u0, :], mx2, ALU.subtract).then_inc(low2_done, 1)
                mult(E2 - 1, 1, 0)
                mult(E2 - 1, 1, 1)
                dve.wait_ge(sexp_done, 1)
                link(dve.tensor_tensor(mx2, sc2[:, :, 0, :], sc2[:, :, 1, :], ALU.add))
                link(dve.reciprocal(mx2, mx2))
                for u0 in range(2):
                    dve.tensor_tensor(sc2[:, :, u0, :], sc2[:, :, u0, :], mx2, ALU.mult).then_inc(prob2_done, 1)
                mult(E2 - 1, 1, 2)
                mult(E2 - 1, 1, 3)
                down_rest(E2 - 1, 1)
                add_expert(E2 - 2, 0)
                for i in (1, 3):
                    dve.wait_ge(ctxT_ready, 2 * i + 2)
                    dve.tensor_copy(ctxT[:, :, i * 256:(i + 1) * 256].rearrange("p c (t n) -> p t c n", t=2),
                                    bank[i][:, :].rearrange("p (t c n) -> p t c n", t=2, c=DC)).then_inc(ctxT_done, 1)
                add_expert(E2 - 1, 1)
                dve.sem_inc(ffn_done, 1)
                s_copy(2)
                residual(2)
            if layers > 3:
                layernorm(3)
                dve.wait_ge(lam_in_s, 16)
                for i in range(2):
                    link(dve.tensor_tensor(lam_in[:, 2 * i, :], lam_in[:, 2 * i, :], lam_in[:, 2 * i + 1, :], ALU.mult))
                    dve.tensor_reduce(lam[:, i:i + 1], lam_in[:, 2 * i, :], AX.X, ALU.add).then_inc(lam_sum, 1)
                dve.wait_ge(lam_exp, 1)
                link(dve.tensor_tensor(lam[:, 2:3], lam[:, 1:2], lam[:, 0:1], ALU.subtract))
                link(dve.tensor_scalar(lam[:, 2:3], lam[:, 2:3], LAMBDA_INIT, None, ALU.subtract))

                def norm_qk(t):
                    v = qk3[:, t, :].rearrange("p (g e) -> p g e", e=G3)
                    dve.wait_ge(qkv_done, 2 * NT + 2 * t + 2)
                    link(dve.tensor_tensor(sq3[:, t % 2, :], qk3[:, t, :], qk3[:, t, :], ALU.mult))
                    link(dve.tensor_reduce(ms3, sq3[:, t % 2, :].rearrange("p (g e) -> p g e", e=G3), AX.X, ALU.add))
                    dve.tensor_scalar(rms[:, t, :], ms3, 1.0 / G3, RMS_EPS, ALU.mult, ALU.add).then_inc(ms_done, 1)

                def scale_qk(t):
                    v = qk3[:, t, :].rearrange("p (g e) -> p g e", e=G3)
                    dve.wait_ge(rms_done, t + 1)
                    dve.tensor_tensor(v, v, rmsr[:, t, :].unsqueeze(2).to_broadcast([P, 32, G3]), ALU.mult).then_inc(qk_done, 1)

                def keys3(t):
                    dve.wait_ge(qT_done, t + 1)
                    dve.wait_ge(qkT_ready, t + 1)
                    dve.tensor_copy(k3T[:, :, t * P:(t + 1) * P], bank[4 + t % 4][:, 256:512].rearrange("p (c n) -> p c n", c=DC)
                                    ).then_inc(kT_done, 1)

                def masked_keys(b, c):
                    dve.wait_ge(kT_done, NT)
                    if b:
                        dve.wait_ge(av_ready, 8 * c + 8)
                    for g in range(8):
                        dve.tensor_scalar(kz[:, c, g, :], k3T[:, c, b * S:(b + 1) * S], con[:, C_SEL + g:C_SEL + g + 1], None, ALU.mult
                                          ).then_inc(kz_done, 1)

                for t in range(NT):
                    norm_qk(t)
                    if t:
                        scale_qk(t - 1)
                scale_qk(NT - 1)
                for n in range(2 * NF):
                    f, b = n // 2, n % 2
                    dve.wait_ge(up3_ready, n + 1)
                    dve.wait_ge(silu3_done, n + 1)
                    dve.tensor_tensor(hid3[:, f, b * S:(b + 1) * S], bank[2 + n % 2][:, :], gs3[n % 2], ALU.mult).then_inc(hid3_done, 1)
                    if n >= 7 and n % 2 == 1 and (n - 7) // 2 < 5:
                        keys3((n - 7) // 2)
                for t in range(5, NT):
                    keys3(t)
                masked_keys(0, 0)
                masked_keys(0, 1)

                def normalise(b, c, j):
                    i = 4 * b + 2 * c + j
                    dve.wait_ge(av_ready, 4 * i + 4)
                    if i:
                        dve.wait_ge(norm3_done, i)
                    link(dve.reciprocal(zinv, bank[6 + j][:, :]))
                    if j == 0:
                        dve.tensor_tensor(y3[:, 0, :], bank[4][:, :], zinv, ALU.mult).then_inc(norm3_done, 1)
                    else:
                        link(dve.tensor_tensor(y3[:, 1, :], bank[5][:, :], zinv, ALU.mult))
                        dve.scalar_tensor_tensor(yT3[:, c, b * S:(b + 1) * S], y3[:, 1, :], lam[:, 2:3], y3[:, 0, :],
                                                 ALU.mult, ALU.add).then_inc(norm3_done, 1)

                for b in range(B):
                    for c in range(DC):
                        normalise(b, c, 0)
                        normalise(b, c, 1)
                        if b == 0:
                            masked_keys(1, c)
                for i in range(NT // 2):
                    dve.wait_ge(g3_ready, 2 * i + 2)
                    dve.tensor_scalar(g_tok[:, 2 * i:2 * i + 2, :].rearrange("p a d -> p (a d)"), bank[i][:, :], FF ** -0.5, None, ALU.mult
                                      ).then_inc(g_done, 1)
                dve.wait_ge(g_done, 8)
                dve.sem_inc(ffn_done, 1)
                s_copy(3)
                residual(3)

        @block.scalar
        def _(act):
            link = Link(act, act_link)
            act.sem_inc(exp_done, EXP0)
            act.sem_inc(hid_done, HID0)
            act.sem_inc(xeT_done, TURN0)

            def turned(layer):
                for i in range(4) if SPLIT[layer] else (0, 2):
                    act.wait_ge(turn_ready, NT * layer + 2 * i + 2)
                    act.copy(r(quarter(xnT, i)) if SPLIT[layer] else quarter(xnT, i), turned_bank(i)).then_inc(xnT_act, 1)

            turned(0)

            def queries(h, q, b):
                act.wait_ge(proj_ready, 6 * h + 1 + 2 * b)
                act.mul(r(qT[q][:, b * S:(b + 1) * S]), bank[2 if b else 0][:, :], DH ** -0.5).then_inc(q_done, 1)

            def keys(h, q, b):
                act.wait_ge(proj_ready, 6 * h + 2 + 2 * b)
                act.copy(r(kT[q][:, b * S:(b + 1) * S]), bank[0 if b else 1][:, :]).then_inc(k_done, 1)
                act.copy(klo[q][:, b * S:(b + 1) * S], bank[0 if b else 1][:, :]).then_inc(kfull_done, 1)

            def value_rows(h, q, b):
                act.wait_ge(proj_ready, 6 * h + 5 + b)
                act.copy(vT[q][:, b * S:(b + 1) * S], bank[1 + b][:, :]).then_inc(v_done, 1)

            def exponent(h, n):
                r = n % 4
                act.wait_ge(max_done, 8 * h + n + 1)
                act.activation(prob[r], bank[3 + r][:, :], ACT.Exp, bias=negmax[:, r:r + 1],
                               accum_out=rowsum[:, r:r + 1]).then_inc(exp_done, 1)

            def head(h, q, first=False, last=False):
                for n in range(8):
                    act.wait_ge(acc_done, 8 * h + n + 1)
                    exponent(h, n)
                    if last:
                        continue
                    if n in (1, 4):
                        queries(h + 1, 1 - q, n // 4)
                    if n in (2, 5):
                        keys(h + 1, 1 - q, n // 5)
                    if n >= 6:
                        if n == 6 and not first:
                            act.wait_ge(vals_done, VALS0 + 2 * h)
                        value_rows(h + 1, 1 - q, n - 6)

            for b in range(B):
                queries(0, 0, b)
                keys(0, 0, b)
            value_rows(0, 0, 0)
            value_rows(0, 0, 1)
            act.wait_ge(lg_shift, 1)
            act.activation(ex, ex, ACT.Exp).then_inc(ex_done, 1)
            act.wait_ge(lg_shift, 2)
            act.activation(gap, gap, ACT.Exp).then_inc(ex_done, 1)
            head(0, 0, first=True)
            with act.Fori(0, NH // 2 - 1) as pair:
                head(2 * pair + 1, 1)
                head(2 * pair + 2, 0)
            head(NH - 1, 1, last=True)

            def round_weights(w, hi, wd_hi_, n):
                if n < 4:
                    v, h = w[:, 512 * n:512 * n + 512], hi[:, 512 * n:512 * n + 512]
                elif n == 4:
                    v, h = w[:, W_D:W_B], wd_hi_
                else:
                    v, h = w[:, W_2 + 512 * (n - 5):W_2 + 512 * (n - 4)], hi[:, hi.shape[1] - 512 * (9 - n):hi.shape[1] - 512 * (8 - n)]
                act.copy(r(h), v).then_inc(w_rounded, 1)

            wd_flat = [v.rearrange("p c r -> p (c r)") for v in wd_hi]

            def round_rows(e, q):
                for c in range(DC):
                    act.wait_ge(xeT_ready, 2 * e + c + 1)
                    act.copy(r(xeT[q][:, c, :]), bank[c][:, 0:SLOTS]).then_inc(xeT_rounded, 1)

            def expert(e, q, turn):
                last = turn is None
                act.wait_ge(y_done, Y0 + 3 * e)
                for n in range(NF + 1):
                    act.wait_ge(hid_ready, 9 * e + n + 1)
                    if n == 0:
                        act.activation(aE, bank[2][0:RANK, 0:SLOTS], ACT.Gelu).then_inc(hid_done, 1)
                    else:
                        act.activation(hE[:, n - 1, :], bank[2 + n % 3][:, 0:SLOTS], ACT.Gelu, bias=b1[q][:, n - 1:n]
                                       ).then_inc(hid_done, 1)
                    if n < 5:
                        if n == 0:
                            act.wait_ge(sw_in if last else w1exp_in[1 - q], 48 if last else 16 * turn + 16)
                        round_weights(*((sw, sw_hi, sw_hi[:, W_D:W_B]) if last else (wexp[1 - q], wexp_hi[1 - q], wd_flat[1 - q])), n)
                if not last:
                    round_rows(e + 1, 1 - q)
                    act.wait_ge(w2exp0_in[1 - q], 48 * turn + 48)
                for n in range(5, 9):
                    round_weights(*((sw, sw_hi, sw_hi[:, W_D:W_B]) if last else (wexp[1 - q], wexp_hi[1 - q], wd_flat[1 - q])), n)

            act.wait_ge(w1exp_in[0], 16)
            act.wait_ge(w2exp0_in[0], 48)
            for n in range(9):
                round_weights(wexp[0], wexp_hi[0], wd_flat[0], n)
            for i in (0, 2):
                act.wait_ge(s_ready, 2 * i + 2)
                act.copy(g_tok[:, 2 * i:2 * i + 2, :].rearrange("p a d -> p (a d)"), bank[i][:, :]).then_inc(s_done, 1)
            round_rows(0, 0)
            with act.Fori(0, NE // 2 - 1) as pair:
                expert(2 * pair, 0, pair)
                expert(2 * pair + 1, 1, pair + 1)
            expert(NE - 2, 0, NE // 2 - 1)
            expert(NE - 1, 1, None)
            for b in range(B):
                for f in range(NF + 1):
                    n = (NF + 1) * b + f
                    act.wait_ge(shid_ready, n + 1)
                    if f < NF:
                        ins = act.activation(hS[:, f, b * S:(b + 1) * S], bank[n % 4][:, :], ACT.Gelu, bias=sb1[:, f:f + 1])
                    else:
                        ins = act.activation(aS[:, b * S:(b + 1) * S], bank[n % 4][0:RANK, :], ACT.Gelu)
                    ins.then_inc(shid_done, 1)

            def gate_silu(layer):
                act.wait_ge(ffn_done, layer + 1)
                g = g_tok if layer else s_tok
                act.activation(g[:, :, :], g[:, :, :], ACT.Silu).then_inc(silu_done, 1)

            gate_silu(0)

            def s_copy(layer):
                first_bank = (0, 4, 0, 4)[layer]
                for i in (0, 2):
                    act.wait_ge(s_ready, NT * layer + 2 * i + 2)
                    o, v = s_tok[:, 2 * i:2 * i + 2, :].rearrange("p a d -> p (a d)"), bank[first_bank + i][:, :]
                    if layer == 3:
                        act.mul(o, v, 1.0 - LAMBDA_INIT).then_inc(s_done, 1)
                    else:
                        act.copy(o, v).then_inc(s_done, 1)

            if layers > 1:
                turned(1)
                act.wait_ge(vec_in, 48)
                for b in range(B):
                    for i in (0, 2):
                        for o in range(DC):
                            n = 6 * b + 2 * i + o
                            act.wait_ge(kvr_ready, n + 1)
                            v = bank[4 + n % 4][:, :]
                            if i == 0:
                                ins = act.activation(kk[:, o, b * S:(b + 1) * S], v, ACT.Identity, bias=vec[:, 7, o:o + 1])
                            else:
                                ins = act.activation(rr[:, o, b * S:(b + 1) * S], v, ACT.Sigmoid)
                            ins.then_inc(kr_done, 1)
                for b in range(B):
                    act.wait_ge(low_done, b + 1)
                    act.activation(kk[:, :, b * S:(b + 1) * S], kk[:, :, b * S:(b + 1) * S], ACT.Exp).then_inc(e_done, 1)
                    act.activation(first[:, 1, :, b:b + 1], first[:, 1, :, b:b + 1], ACT.Exp).then_inc(e_done, 1)
                gate_silu(1)
                s_copy(1)

            def qkv_copy(layer):
                for t in range(NT):
                    act.wait_ge(qkv_ready, NT * (layer - 2) + t + 1)
                    b0 = 2 * (t % 3)
                    qk, v = (qkv2[:, t, 0:512], qkv2[:, t, 512:768]) if layer == 2 else (qk3[:, t, :], v3[:, t, :])
                    act.copy(qk, bank[b0][:, :]).then_inc(qkv_done, 1)
                    act.copy(v, bank[b0 + 1][:, 0:D]).then_inc(qkv_done, 1)

            if layers > 2:
                for i in range(4):
                    act.wait_ge(had_ready, i + 1)
                    act.copy(had_b[:, 2 * i:2 * i + 2, :].rearrange("p f d -> p (f d)"), bank[i][:, :]).then_inc(had_copied, 1)
                turned(2)
                act.sem_inc(silu2_done, 2)
                act.wait_ge(z_done, 1)
                act.activation(inh, z2, ACT.Sigmoid).then_inc(inh_done, 1)
                act.wait_ge(dist_done, 1)
                act.activation(gw, dist, ACT.Exp, scale=-1.0 / 0.1).then_inc(gexp_done, 1)
                act.activation(fb, dist, ACT.Exp, scale=-1.0 / 0.3).then_inc(gexp_done, 1)

                def round_gateup(e, q, turn):
                    act.wait_ge(w2exp_in[q], 16 * turn + 16)
                    for i in range(2):
                        act.copy(r(wexp2_hi[q][:, i]), wexp2[q][:, i]).then_inc(gateup_rounded, 1)

                def round_down(e, q, turn):
                    act.wait_ge(wdown_in[q], 16 * turn + 16)
                    act.copy(r(wexp2_hi[q][:, 2]), wexp2[q][:, 2]).then_inc(down_rounded, 1)

                round_gateup(0, 0, 0)
                qkv_copy(2)
                round_gateup(1, 1, 0)
                round_down(0, 0, 0)

                def silu2(e, n):
                    act.wait_ge(gate_ready, 4 * e + n + 1)
                    act.wait_ge(gu_done, 4 * e + n + 1)
                    act.activation(gs[n % 2], bank[n % 2][:, :], ACT.Silu).then_inc(silu2_done, 1)

                for n in range(4):
                    silu2(0, n)
                with act.Fori(0, E2 // 2 - 1) as pair:
                    for q in range(2):
                        for n in range(4):
                            silu2(2 * pair + q + 1, n)
                            if n == 1:
                                round_gateup(2 * pair + q + 2, q, pair + 1)
                            if n == 2:
                                round_down(2 * pair + q + 1, 1 - q, pair + q)
                act.wait_ge(low2_done, 2)
                act.activation(sc2, sc2, ACT.Exp).then_inc(sexp_done, 1)
                for n in range(4):
                    silu2(E2 - 1, n)
                    if n == 2:
                        round_down(E2 - 1, 1, E2 // 2 - 1)
                if layers > 3:
                    act.wait_ge(w3_in, 32)
                    act.wait_ge(ctx_done, 2)
                    for n in range(4):
                        act.copy(r(part(arenaB, 3584 + 512 * n, 512)), part(arenaD, 5120 + 512 * n, 512)).then_inc(ff3_rounded, 1)
                for i in (0, 2):
                    act.wait_ge(ctxT_ready, 2 * i + 2)
                    act.copy(ctxT[:, :, i * 256:(i + 1) * 256].rearrange("p c (t n) -> p t c n", t=2),
                             bank[i][:, :].rearrange("p (t c n) -> p t c n", t=2, c=DC)).then_inc(ctxT_done, 1)
                gate_silu(2)
                s_copy(2)
            if layers > 3:
                act.wait_ge(wgate3_in, 16)
                for n in range(4):
                    act.copy(r(part(arenaB, 1536 + 512 * n, 512)), part(arenaD, 3072 + 512 * n, 512)).then_inc(ff3_rounded, 1)
                turned(3)
                act.wait_ge(lam_sum, 2)
                act.activation(lam[:, 0:2], lam[:, 0:2], ACT.Exp).then_inc(lam_exp, 1)
                qkv_copy(3)

                def queries3(t):
                    act.wait_ge(qkT_ready, t + 1)
                    act.copy(q3T[:, :, t * P:(t + 1) * P], bank[4 + t % 4][:, 0:256].rearrange("p (c n) -> p c n", c=DC)
                             ).then_inc(qT_done, 1)

                for n in range(2 * NF):
                    act.wait_ge(gate3_ready, n + 1)
                    if n >= 2:
                        act.wait_ge(hid3_done, n - 1)
                    act.activation(gs3[n % 2], bank[n % 2][:, :], ACT.Silu).then_inc(silu3_done, 1)
                    if n >= 7 and n % 2 == 1 and (n - 7) // 2 < 5:
                        queries3((n - 7) // 2)
                for t in range(5, NT):
                    queries3(t)
                for u in range(32):
                    w = S - u % 4 * P
                    for hh in range(4):
                        act.wait_ge(sc3_ready, 4 * u + hh + 1)
                        if u >= 2 and hh == 0:
                            act.wait_ge(av_ready, u - 1)
                        act.activation(prob3[:, u % 2, hh, 0:w], bank[hh][:, 0:w], ACT.Exp, scale=G3 ** -0.5).then_inc(exp3_done, 1)
                gate_silu(3)
                s_copy(3)


def _rows(w):
    k, n = w.shape
    return np.ascontiguousarray(w.reshape(k // P, P, n).transpose(1, 0, 2).reshape(P, -1))


def layout(i):
    f = {k: np.asarray(v) for k, v in i.items()}
    w = f["L0_attn_w_qkv"].reshape(DC, P, 3, NH, DH).transpose(3, 1, 0, 2, 4)
    d = {
        "x": f["L0_attn_x"].reshape(T, D),
        "con": constants(),
        "gate": _rows(f["L0_ffn_gate_w"]),
        "wqkv": w.reshape(NH, P, DC * 3 * DH),
        "wo": _rows(f["L0_attn_w_o"]),
        "wexp": np.stack([np.concatenate([_rows(f["L0_ffn_w1"][e]), _rows(f["L0_ffn_wd"][e]),
                                          f["L0_ffn_b1"][e].reshape(NF, P).T, _rows(f["L0_ffn_w2"][e])], 1) for e in range(NE)]),
        "wu": f["L0_ffn_wu"],
        "b2": f["L0_ffn_b2"].reshape(NE, 1, D),
        "sw": np.concatenate([_rows(f["L0_ffn_sw1"]), _rows(f["L0_ffn_swd"]),
                              f["L0_ffn_sb1"].reshape(NF, P).T, _rows(f["L0_ffn_sw2"])], 1),
        "swu": f["L0_ffn_swu"],
        "sb2": f["L0_ffn_sb2"].reshape(1, D),
        "w_rwkv": np.concatenate([_rows(f[f"L1_attn_w_{k}"].T) for k in ("key", "value", "rec", "out")], 1),
        "w_lin": _rows(f["L1_ffn_weight"].T),
        "lin_scale": f["L1_ffn_scale_weight"].reshape(1, D),
        "lin_bias": f["L1_ffn_bias"].reshape(1, D),
        "vec": np.concatenate([_rows(f[f"L1_attn_{k}"].reshape(D, 1)) for k in
                               ("time_mix_k", "time_mix_v", "time_mix_r", "xx", "aa", "bb", "pp", "time_first")], 1),
        "gate2": _rows(f["L2_ffn_Wr"]),
        "temp": f["L2_ffn_temperature"].reshape(1, 1),
        "lam": np.concatenate([f[f"L3_attn_{k}"] for k in ("lq1", "lk1", "lq2", "lk2")]).reshape(1, 128),
        "w2": np.concatenate([_rows(f["L2_attn_w_qkv"].reshape(D, H2, 3, HD2).transpose(0, 2, 1, 3).reshape(D, 3 * D)),
                              _rows(f["L2_attn_w_dense"])], 1),
        "wexp2": np.stack([np.concatenate([_rows(f[f"L2_ffn_{k}"][e]) for k in ("Wg", "Wu", "Wd")], 1) for e in range(E2)]),
        "w3": np.concatenate([_rows(np.concatenate([f[f"L3_attn_{k}"].T for k in ("wq", "wk", "wv")], 1)),
                              _rows(f["L3_attn_wo"].T)], 1),
        "wff3": np.concatenate([_rows(f["L3_ffn_W1"].T), _rows(f["L3_ffn_W3"].T)], 1),
        "w_down3": _rows(f["L3_ffn_W2"].T),
    }
    return {k: np.ascontiguousarray(v) for k, v in d.items()}


def kernel(**inputs):
    import concourse.bacc as bacc
    from concourse.bass_utils import run_bass_kernel_spmd

    nc = bacc.Bacc("TRN2", target_bir_lowering=False, num_devices=1)
    arrays, args = {}, {}
    for name, v in layout(inputs).items():
        arrays[f"in_{name}"] = v
        args[name] = nc.dram_tensor(f"in_{name}", v.shape, F32, kind="ExternalInput").ap()
    out = nc.dram_tensor("out_x", (T, D), F32, kind="ExternalOutput").ap()
    build(nc, args, out)
    r = run_bass_kernel_spmd(nc, [arrays], core_ids=[0])
    return r.results[0]["out_x"].reshape(B, S, D)
```

```python
from contextlib import ExitStack

import numpy as np

import concourse.bass as bass
from concourse import mybir

F32 = mybir.dt.float32
I32 = mybir.dt.int32
F32R = mybir.dt.float32r
ALU = mybir.AluOpType
ACT = mybir.ActivationFunctionType
AX = mybir.AxisListType

P = 128
B, S, D = 2, 512, 256
T = B * S
NT = T // P
DC = D // P
ST = S // P
LN_EPS = 1e-5

NH, DH = 16, 128
NE, CAP, FF, RANK = 8, 160, 1024, 32
NF = FF // P
SLOTS = 2 * CAP
SROWS = [128, 128, SLOTS - 256]
W_D, W_B, W_2 = DC * FF, DC * FF + DC * RANK, DC * FF + DC * RANK + NF
WPACK = W_2 + NF * D
NO_SLOT = 4096.0
OUT_OF_REACH = -3.0e38

H2, HD2 = 16, 16
E2 = 8
GOLD_C = float(1.0 / np.e)
GOLD_LO = 0.5 - np.log(4.0 / 3.0)
Z_LO = float(np.log(GOLD_LO / (1.0 - GOLD_LO)))
BLOCKED = -10000.0

H3, G3 = 8, 16
RMS_EPS = 1.1920929e-07
LAMBDA_INIT = 0.8

C_ID, C_TRI, C_HAD, C_CAUSAL, C_IOTA, C_COS, C_SIN, C_SEL = 0, 128, 256, 384, 512, 576, 832, 1088
C_END = 1096


def constants():
    c = np.zeros((P, C_END), np.float32)
    i = np.arange(P)
    c[:, C_ID:C_ID + P] = np.eye(P)
    c[:, C_TRI:C_TRI + P] = i[:, None] < i[None, :]
    had = np.array([[1.0]])
    while had.shape[0] < P:
        had = np.block([[had, had], [had, -had]])
    c[:, C_HAD:C_HAD + P] = had
    c[:, C_CAUSAL:C_CAUSAL + P] = i[:, None] <= i[None, :]
    c[:, C_IOTA:C_IOTA + 64] = np.tile(np.arange(8) - 8.0, 8)
    inv = 1.0 / 10000.0 ** (np.arange(0, HD2, 2, dtype=np.float32) / np.float32(HD2))
    ang = np.concatenate([inv, inv]).astype(np.float32)
    sign = np.where(np.arange(HD2) < HD2 // 2, -1.0, 1.0)
    c[:, C_COS:C_COS + D] = np.tile(np.cos(ang), H2)
    c[:, C_SIN:C_SIN + D] = np.tile(np.sin(ang) * sign, H2)
    c[:, C_SEL:C_SEL + 8] = (i[:, None] // G3) == np.arange(8)[None, :]
    return c


TWIN = {}


def rounded(v):
    return bass.AP(tensor=TWIN[v.tensor.name], offset=v.offset, ap=v.ap)


def r(v):
    return rounded(v).bitcast(F32R)


def product(pe, o, lhs, rhs, start, stop):
    pe.matmul(o, r(lhs[0]), r(rhs[0]), start=start, stop=False)
    pe.matmul(o, r(lhs[0]), r(rhs[1]), start=False, stop=False)
    return pe.matmul(o, r(lhs[1]), r(rhs[0]), start=False, stop=stop)


class Link:

    def __init__(self, eng, sem):
        self.eng, self.sem, self.n = eng, sem, 0

    def __call__(self, ins):
        self.n += 1
        ins.then_inc(self.sem, 1)
        self.eng.wait_ge(self.sem, self.n)


def build(nc, a, out, layers=4):
    ctx = ExitStack()
    with ctx:
        def sem(name):
            return ctx.enter_context(nc.semaphore(name))

        def sb(name, shape, dt=F32):
            return ctx.enter_context(nc.sbuf_tensor(name, shape, dt))

        def twinned(name, shape):
            with nc.sbuf_tensor(name + "_rounded", shape, F32) as second:
                TWIN[name] = second
            return sb(name, shape)

        bank = [ctx.enter_context(nc.psum_tensor(f"bank{i}", [P, 512], F32)) for i in range(8)]

        x = sb("x", [P, NT, D])
        xn = twinned("xn", [P, NT, D])
        xnT = twinned("xnT", [P, DC, T])
        s_tok = twinned("s_tok", [P, NT, D])
        g_tok = sb("g_tok", [P, NT, D])
        con = sb("con", [P, C_END])
        ones = sb("ones", [P, P])
        ones_r = sb("ones_r", [P, P])
        stats = sb("stats", [P, NT, 6])
        meanvar = sb("meanvar", [P, NT, 2])
        veps = sb("veps", [P, NT])
        rstd = sb("rstd", [P, NT])
        mhalf = sb("mhalf", [P, 256])
        ident = con[:, C_ID:C_ID + P]

        arenaB = twinned("arenaB", [P, 16384])
        arenaC = twinned("arenaC", [P, 12800])
        arenaD = twinned("arenaD", [P, 2 * (WPACK + 2 * D)])
        small = twinned("small", [P, 1536])

        def part(arena, at, n, **kw):
            v = arena[:, at:at + n]
            return v.rearrange(kw.pop("r"), **kw) if "r" in kw else v

        vals = part(arenaB, 0, NH * T, r="p (h t) -> p h t", h=NH)
        wqkv = [part(arenaC, 768 * q, 768, r="p (c w) -> p c w", c=DC) for q in range(2)]
        wo = part(arenaC, 1536, NH * D, r="p (h d) -> p h d", h=NH)
        qT = [part(arenaC, 5632 + 1024 * q, T) for q in range(2)]
        kT = [part(arenaC, 7680 + 1024 * q, T) for q in range(2)]
        vT = [part(arenaC, 9728 + 1024 * q, T) for q in range(2)]
        acc = [part(arenaC, 11776 + S * b, S) for b in range(B)]
        xlo = s_tok[:, :, :].rearrange("p a d -> p (a d)").rearrange("p (c t) -> p c t", c=DC)
        wqkv_hi = [part(arenaD, 768 * q, 768, r="p (c w) -> p c w", c=DC) for q in range(2)]
        qlo = [part(arenaD, 1536 + 1024 * q, T) for q in range(2)]
        klo = [part(arenaD, 3584 + 1024 * q, T) for q in range(2)]
        acc_hi = [part(arenaD, 5632 + S * b, S) for b in range(B)]
        prob = [g_tok[:, 2 * q:2 * q + 2, :].rearrange("p a d -> p (a d)") for q in range(4)]
        wexp = [part(arenaD, (WPACK + 2 * D) * q, WPACK + 2 * D) for q in range(2)]
        def w1_of(w):
            return w[:, 0:W_D].rearrange("p (c f) -> p c f", c=DC)

        def wd_of(w):
            return w[:, W_D:W_B].rearrange("p (c r) -> p c r", c=DC)

        def w2_of(w):
            return w[:, W_2:WPACK].rearrange("p (f d) -> p f d", f=NF)

        w1, wd, w2 = ([of(w) for w in wexp] for of in (w1_of, wd_of, w2_of))
        b1 = [w[:, W_B:W_2] for w in wexp]
        wu = [w[0:RANK, WPACK:WPACK + D] for w in wexp]
        b2 = [w[:, WPACK + D:WPACK + 2 * D] for w in wexp]
        xe = [part(arenaC, 5632 + 768 * q, 768, r="p (s d) -> p s d", s=3) for q in range(2)]
        xeT = [part(arenaC, 640 * q, 640, r="p (c n) -> p c n", c=DC) for q in range(2)]
        hE = part(arenaC, 1280, NF * SLOTS, r="p (f n) -> p f n", f=NF)
        aE = arenaC[0:RANK, 3840:3840 + SLOTS]
        yE = [part(arenaC, 7168 + 768 * q, 768, r="p (s d) -> p s d", s=3) for q in range(2)]
        wexp_hi = [part(arenaC, 8704, 4096), part(arenaB, 0, 4096)]
        w1_hi = [w[:, 0:DC * FF].rearrange("p (c f) -> p c f", c=DC) for w in wexp_hi]
        w2_hi = [w[:, DC * FF:4096].rearrange("p (f d) -> p f d", f=NF) for w in wexp_hi]
        wd_hi = [part(small, 820 + DC * RANK * q, DC * RANK, r="p (c r) -> p c r", c=DC) for q in range(2)]
        hE_hi = part(arenaB, 4096, NF * SLOTS, r="p (f n) -> p f n", f=NF)
        xeT_lo = [part(arenaB, 6656 + 640 * q, 640, r="p (c n) -> p c n", c=DC) for q in range(2)]
        hS = part(arenaB, 0, NF * T, r="p (f t) -> p f t", f=NF)
        sw = part(arenaB, 8192, DC * FF + NF * D + DC * RANK + NF + D)
        sw1, swd, sw2 = w1_of(sw), wd_of(sw), w2_of(sw)
        sb1 = sw[:, W_B:W_2]
        sw_hi = part(arenaD, 0, WPACK)
        sw1_hi, swd_hi, sw2_hi = w1_of(sw_hi), wd_of(sw_hi), w2_of(sw_hi)
        hS_hi = [part(arenaD, WPACK + 2 * D, NF * S, r="p (f t) -> p f t", f=NF), part(arenaC, 0, NF * S, r="p (f t) -> p f t", f=NF)]
        sb2 = sw[:, WPACK:WPACK + D]
        swu = arenaB[0:RANK, 12616:12616 + D]
        aS = arenaB[0:RANK, 12872:12872 + T]
        got = [part(arenaC, 8704 + NT * D * k, NT * D, r="p (t d) -> p t d", t=NT) for k in range(2)]
        gate = part(small, 0, DC * NE, r="p (c e) -> p c e", c=DC)
        lg = part(small, 16, 64, r="p (t e) -> p t e", t=NT)
        eq = part(small, 80, 64, r="p (t e) -> p t e", t=NT)
        ex = part(small, 144, 64, r="p (t e) -> p t e", t=NT)
        oh = part(small, 208, 128, r="p (t k e) -> p t k e", t=NT, k=2)
        before = part(small, 336, 128, r="p (t k e) -> p t k e", t=NT, k=2)
        ohp = part(small, 464, 128, r="p (t k e) -> p t k e", t=NT, k=2)
        top = part(small, 592, 16, r="p (k t) -> p k t", k=2)
        idx = part(small, 608, 16, r="p (t k) -> p t k", k=2)
        pos = part(small, 624, 16, r="p (t k) -> p t k", k=2)
        keep = part(small, 640, 16, r="p (t k) -> p t k", k=2)
        base = part(small, 656, 16, r="p (t k) -> p t k", k=2)
        slot = part(small, 672, 16, r="p (t k) -> p t k", k=2)
        wt = part(small, 688, 16, r="p (t k) -> p t k", k=2)
        esum = part(small, 704, 8)
        einv = part(small, 712, 8)
        kslot = part(small, 720, 16, r="p (t k) -> p t k", k=2)
        gap = part(small, 748, 8)
        negmax = part(small, 736, 4)
        rowsum = part(small, 740, 4)
        rowinv = part(small, 744, 4)
        w_rwkv = part(arenaB, 13896, 4 * DC * D, r="p (i c o) -> p i c o", i=4, c=DC)
        w_lin = part(arenaC, 4160, DC * D, r="p (c o) -> p c o", c=DC)
        lin_scale, lin_bias = part(arenaC, 4672, D), part(arenaC, 4928, D)
        vec = part(small, 756, 16, r="p (i c) -> p i c", i=8)
        offs = part(small, 772, 6, r="p (i c) -> p i c", i=3)
        mixed = part(arenaB, 0, 3 * DC * T, r="p (i c t) -> p i c t", i=3, c=DC)
        kk, vv, rr = (part(arenaB, 6144 + 2048 * i, DC * T, r="p (c t) -> p c t", c=DC) for i in range(3))
        first = part(small, 780, 16, r="p (i c b) -> p i c b", i=4, c=DC)
        w_qkv2 = part(arenaC, 0, DC * 768, r="p (c n) -> p c n", c=DC)
        w_dense = part(arenaC, 1536, DC * D, r="p (c n) -> p c n", c=DC)
        w_qkv3 = part(arenaC, 2048, DC * 768, r="p (c n) -> p c n", c=DC)
        w_out3 = part(arenaC, 3584, DC * D, r="p (c n) -> p c n", c=DC)
        qkv2 = part(arenaB, 0, NT * 768, r="p (t n) -> p t n", t=NT)
        rot = part(arenaB, 6144, 1024, r="p (t h e) -> p t h e", t=4, h=H2)
        prod = part(arenaB, 7168, 1024, r="p (t h e) -> p t h e", t=4, h=H2)
        ctx_tok = part(arenaB, 8192, NT * D, r="p (t n) -> p t n", t=NT)
        ctxT = part(arenaB, 10240, DC * T, r="p (c t) -> p c t", c=DC)
        tree = part(arenaB, 12288, 1024)
        sc2 = part(arenaB, 13312, 256, r="p (s u m) -> p s u m", s=2, u=2)
        mx2 = part(arenaB, 13568, 128, r="p (s m) -> p s m", s=2)
        wexp2 = [part(arenaD, 1536 * q, 1536, r="p (i c n) -> p i c n", i=3, c=DC) for q in range(2)]
        w_qkv2_hi = part(arenaC, 10752, DC * 768, r="p (c n) -> p c n", c=DC)
        wexp2_hi = [m.rearrange("p (i c n) -> p i c n", i=3, c=DC)
                    for m in (arenaB[:, 13696:15232], xn[:, 0:6, :].rearrange("p t d -> p (t d)"))]
        gu_hi = [part(arenaC, 6208, DC * T, r="p (f t) -> p f t", f=DC), part(arenaD, 3072, DC * T, r="p (f t) -> p f t", f=DC)]
        gu = [part(arenaC, 8704 + 2048 * q, DC * T, r="p (f t) -> p f t", f=DC) for q in range(2)]
        gs = [part(arenaC, 5184 + 512 * q, S) for q in range(2)]
        gate2 = part(small, 800, DC * E2, r="p (c e) -> p c e", c=DC)
        temp = part(small, 816, 1)
        z2, inh, dist, gw, fb, zone, cand, mask2 = (part(small, 820 + 64 * i, 64, r="p (t e) -> p t e", t=NT) for i in range(8))
        red8 = part(small, 1332, 48, r="p (i t) -> p i t", i=6)
        xlo3 = part(arenaC, 0, DC * T, r="p (c t) -> p c t", c=DC)
        w_qkv3_hi = part(arenaB, 0, DC * 768, r="p (c n) -> p c n", c=DC)
        w_gate3_hi = part(arenaB, 1536, DC * FF, r="p (c n) -> p c n", c=DC)
        w_up3_hi = part(arenaB, 3584, DC * FF, r="p (c n) -> p c n", c=DC)
        w_gate3 = part(arenaD, 3072, DC * FF, r="p (c n) -> p c n", c=DC)
        w_up3 = part(arenaD, 5120, DC * FF, r="p (c n) -> p c n", c=DC)
        w_down3 = part(arenaD, 7168, NF * D, r="p (f d) -> p f d", f=NF)
        had_b = part(arenaC, 6208, NF * D, r="p (f d) -> p f d", f=NF)
        qk3 = part(arenaC, 4096, NT * 512, r="p (t n) -> p t n", t=NT)
        v3 = part(arenaC, 8192, NT * D, r="p (t n) -> p t n", t=NT)
        prob3 = part(arenaC, 4096, 4096, r="p (q h n) -> p q h n", q=2, h=4)
        y3 = part(arenaC, 10240, 1024, r="p (i n) -> p i n", i=2)
        zinv = part(arenaC, 11264, 512)
        gs3 = [part(arenaC, 11776 + 512 * q, S) for q in range(2)]
        yT3 = part(arenaC, 0, DC * T, r="p (c t) -> p c t", c=DC)
        q3T = g_tok[:, :, :].rearrange("p a d -> p (a d)").rearrange("p (c t) -> p c t", c=DC)
        k3T = s_tok[:, :, :].rearrange("p a d -> p (a d)").rearrange("p (c t) -> p c t", c=DC)
        kz = part(arenaB, 0, 8192, r="p (c g t) -> p c g t", c=DC, g=8)
        hid3 = part(arenaB, 8192, NF * T, r="p (f t) -> p f t", f=NF)
        sq3 = part(arenaD, 0, 1024, r="p (q n) -> p q n", q=2)
        step3 = part(small, 820, 256)
        rms = sb("rms", [P, NT, 32])
        rmsr = sb("rmsr", [P, NT, 32])
        lam_in = sb("lam_in", [P, 4, 32])
        lam = part(small, 1420, 8)
        put_at = sb("put_at", [P, NT, 2], I32)
        get_at = sb("get_at", [P, NT, 2], I32)

        slots_d = nc.dram_tensor("slots", (NE * SLOTS, D), F32, kind="Internal").ap()
        rows_d = nc.dram_tensor("rows", (NE * SLOTS, D), F32, kind="Internal").ap()

        x_in = [sem(f"x_in{i}") for i in range(NT // 2)]
        con_in, gate_in, wo_in = sem("con_in"), sem("gate_in"), sem("wo_in")
        wqkv_in = [sem(f"wqkv_in{q}") for q in range(2)]
        w1exp_in = [sem(f"w1exp_in{q}") for q in range(2)]
        w2exp0_in = [sem(f"w2exp0_in{q}") for q in range(2)]
        xe_in = [sem(f"xe_in{q}") for q in range(2)]
        sw_in, x_out = sem("sw_in"), sem("x_out")
        slots_zero, slots_put, rows_got = sem("slots_zero"), sem("slots_put"), sem("rows_got")
        rows_out = [sem(f"rows_out{q}") for q in range(2)]
        dve_link, act_link, pool_link = sem("dve_link"), sem("act_link"), sem("pool_link")
        ones_set, zeros_set, mhalf_set = sem("ones_set"), sem("zeros_set"), sem("mhalf_set")
        ln_var, ln_rstd, xn_done = sem("ln_var"), sem("ln_rstd"), sem("xn_done")
        turn_ready, xnT_act, xnT_dve = sem("turn_ready"), sem("xnT_act"), sem("xnT_dve")
        logits_ready, lg_shift, ex_done = sem("logits_ready"), sem("lg_shift"), sem("ex_done")
        oh_done, place_ready, at_done = sem("oh_done"), sem("place_ready"), sem("at_done")
        proj_ready = sem("proj_ready")
        q_done, k_done, v_done = sem("q_done"), sem("k_done"), sem("v_done")
        qlo_done, kfull_done, klo_done, inv_done = sem("qlo_done"), sem("kfull_done"), sem("klo_done"), sem("inv_done")
        wqkv_rounded, wqkv_split = sem("wqkv_rounded"), sem("wqkv_split")
        score_ready, max_done, exp_done, acc_done = sem("score_ready"), sem("max_done"), sem("exp_done"), sem("acc_done")
        acc_rounded, acc_split, ones_rounded = sem("acc_rounded"), sem("acc_split"), sem("ones_rounded")
        colsum_ready, vals_done = sem("colsum_ready"), sem("vals_done")
        s_ready, s_done = sem("s_ready"), sem("s_done")
        xeT_ready, xeT_done, hid_ready, hid_done = sem("xeT_ready"), sem("xeT_done"), sem("hid_ready"), sem("hid_done")
        y_ready, y_done = sem("y_ready"), sem("y_done")
        w_rounded, w_split = sem("w_rounded"), sem("w_split")
        h_rounded, h_split, xeT_rounded = sem("h_rounded"), sem("h_split"), sem("xeT_rounded")
        hS_rounded, hS_split = sem("hS_rounded"), sem("hS_split")
        shid_ready, shid_done, sh_ready = sem("shid_ready"), sem("shid_done"), sem("sh_ready")
        w1_in, wlin_in, mix_done, kvr_ready = sem("w1_in"), sem("wlin_in"), sem("mix_done"), sem("kvr_ready")
        kr_done, low_done, e_done, rwkv_done, inv1_done = sem("kr_done"), sem("low_done"), sem("e_done"), sem("rwkv_done"), sem("inv1_done")
        wlin_done, g_ready, vec_in = sem("wlin_done"), sem("g_ready"), sem("vec_in")
        w2_in, w3_in, wff3_in, wgate3_in = sem("w2_in"), sem("w3_in"), sem("wff3_in"), sem("wgate3_in")
        wq_rounded, wq_split = sem("wq_rounded"), sem("wq_split")
        gateup_rounded, gateup_split, down_rounded, down_split = sem("gateup_rounded"), sem("gateup_split"), sem("down_rounded"), sem("down_split")
        gu_rounded, gu_split, ff3_rounded, ff3_split = sem("gu_rounded"), sem("gu_split"), sem("ff3_rounded"), sem("ff3_split")
        wdown_in = [sem(f"wdown_in{q}") for q in range(2)]
        had_ready, had_copied, had_done = sem("had_ready"), sem("had_copied"), sem("had_done")
        qkv_ready, qkv_done = sem("qkv_ready"), sem("qkv_done")
        z_ready, z_done, inh_done, dist_done, gexp_done = sem("z_ready"), sem("z_done"), sem("inh_done"), sem("dist_done"), sem("gexp_done")
        w2exp_in = [sem(f"w2exp_in{q}") for q in range(2)]
        gate_ready, up_ready, silu2_done, gu_done = sem("gate_ready"), sem("up_ready"), sem("silu2_done"), sem("gu_done")
        e2_ready, e2_done = sem("e2_ready"), sem("e2_done")
        sc_done, low2_done, sexp_done, prob2_done, ctx_done = sem("sc_done"), sem("low2_done"), sem("sexp_done"), sem("prob2_done"), sem("ctx_done")
        ctxT_ready, ctxT_done = sem("ctxT_ready"), sem("ctxT_done")
        sq_done, inverse_done, root_done = sem("sq_done"), sem("inverse_done"), sem("root_done")
        ms_done, rms_done, qk_done = sem("ms_done"), sem("rms_done"), sem("qk_done")
        qkT_ready, qT_done, kT_done, kz_done = sem("qkT_ready"), sem("qT_done"), sem("kT_done"), sem("kz_done")
        gate3_ready, up3_ready, silu3_done, hid3_done = sem("gate3_ready"), sem("up3_ready"), sem("silu3_done"), sem("hid3_done")
        sc3_ready, exp3_done, causal_done, av_ready, norm3_done = sem("sc3_ready"), sem("exp3_done"), sem("causal_done"), sem("av_ready"), sem("norm3_done")
        g3_ready, lam_in_s, lam_exp, lam_sum = sem("g3_ready"), sem("lam_in_s"), sem("lam_exp"), sem("lam_sum")
        ffn_done, silu_done, x_done = sem("ffn_done"), sem("silu_done"), sem("x_done")

        EXP0, ACC0, VALS0, HID0, Y0, TURN0, ROWS0, GU0, E20 = 4, 4, 1, 3, 3, 2, 32, 2, 8

        SPLIT = [True, False, True, True]
        QKV_BANK = (4, 0, 2)
        XLO = [xlo, None, xlo, xlo3]
        XT_ACT = [4 * n for n in range(5)]
        XT_DVE = [4 * sum(SPLIT[:n]) for n in range(5)]

        def quarter(v, i):
            return v[:, :, i * 256:(i + 1) * 256].rearrange("p c (t n) -> p t c n", t=2)

        def turned_bank(i):
            return bank[i][:, :].rearrange("p (t c n) -> p t c n", t=2, c=DC)

        block = ctx.enter_context(nc.Block())

        @block.sync
        def _(sp):
            for i in range(NT // 2):
                sp.dma_start(x[:, 2 * i:2 * i + 2, :], a["x"][256 * i:256 * i + 256, :].rearrange("(n p) d -> p n d", p=P)).then_inc(x_in[i], 16)
            sp.dma_start(con[:, :], a["con"]).then_inc(con_in, 16)
            sp.dma_start(gate, a["gate"].rearrange("p (c e) -> p c e", c=DC)).then_inc(gate_in, 16)
            sp.dma_start(part(small, 756, 16), a["vec"]).then_inc(vec_in, 16)
            sp.dma_start(part(small, 800, DC * E2), a["gate2"]).then_inc(vec_in, 16)
            sp.dma_start(temp, a["temp"].to_broadcast([P, 1])).then_inc(vec_in, 16)
            sp.dma_start(lam_in[:, :, :], a["lam"].to_broadcast([P, 128]).rearrange("p (i n) -> p i n", i=4)).then_inc(lam_in_s, 16)
            for h in range(2):
                sp.dma_start(wqkv[h], a["wqkv"][h].rearrange("p (c w) -> p c w", c=DC)).then_inc(wqkv_in[h], 16)
            sp.wait_ge(zeros_set, 1)
            sp.dma_start(slots_d.rearrange("(p n) d -> p n d", p=P),
                         arenaB[:, 0:NE * SLOTS // P * D].rearrange("p (n d) -> p n d", d=D)).then_inc(slots_zero, 16)
            sp.dma_start(wo, a["wo"].rearrange("p (h d) -> p h d", h=NH)).then_inc(wo_in, 16)

            def load_first(e, q):
                sp.dma_start(wexp[q][:, 0:W_2], a["wexp"][e][:, 0:W_2] if isinstance(e, int) else
                             a["wexp"][bass.ds(e, 1), :, 0:W_2].rearrange("e p n -> (e p) n")).then_inc(w1exp_in[q], 16)

            def load_second(e, q):
                sp.dma_start(wexp[q][:, W_2:WPACK], a["wexp"][e][:, W_2:WPACK] if isinstance(e, int) else
                             a["wexp"][bass.ds(e, 1), :, W_2:WPACK].rearrange("e p n -> (e p) n")).then_inc(w2exp0_in[q], 16)
                sp.dma_start(wu[q], a["wu"][e]).then_inc(w2exp0_in[q], 16)
                sp.dma_start(b2[q], a["b2"][e].to_broadcast([P, D])).then_inc(w2exp0_in[q], 16)

            with sp.Fori(1, NH // 2) as pair:
                for q in range(2):
                    sp.wait_ge(proj_ready, 12 * pair + 6 * q - 6)
                    sp.dma_start(wqkv[q], a["wqkv"][bass.ds(2 * pair + q, 1)].rearrange("h p (c w) -> (h p) c w", c=DC)
                                 ).then_inc(wqkv_in[q], 16)

            def load_slots(e, q):
                r = a_slots(e)
                sp.dma_start(xe[q][:, 0:2, :], r[0:256, :].rearrange("(s p) d -> p s d", p=P)).then_inc(xe_in[q], 16)
                sp.dma_start(xe[q][0:SROWS[2], 2, :], r[256:SLOTS, :]).then_inc(xe_in[q], 16)

            def a_slots(e):
                if isinstance(e, int):
                    return slots_d[e * SLOTS:(e + 1) * SLOTS, :]
                return slots_d.rearrange("(e r) d -> e r d", e=NE)[bass.ds(e, 1)].rearrange("e r d -> (e r) d")

            sp.wait_ge(vals_done, VALS0 + 2 * NH)
            for e in range(2):
                load_first(e, e)
                load_second(e, e)
            sp.wait_ge(slots_put, 16 * 2 * NT)
            for e in range(2):
                load_slots(e, e)
            sp.wait_ge(s_done, NT // 2)
            sp.dma_start(sw[:, 0:WPACK], a["sw"]).then_inc(sw_in, 16)
            sp.dma_start(swu, a["swu"]).then_inc(sw_in, 16)
            sp.dma_start(sb2, a["sb2"].to_broadcast([P, D])).then_inc(sw_in, 16)

            rows_e = rows_d.rearrange("(e r) d -> e r d", e=NE)

            def store_rows(e, q):
                sp.wait_ge(y_done, Y0 + 3 * e + 3)
                r = rows_e[bass.ds(e, 1)].rearrange("e r d -> (e r) d")
                sp.dma_start(r[0:256, :].rearrange("(s p) d -> p s d", p=P), yE[q][:, 0:2, :]).then_inc(rows_out[q], 16)
                sp.dma_start(r[256:SLOTS, :], yE[q][0:SROWS[2], 2, :]).then_inc(rows_out[q], 16)

            with sp.Fori(0, NE // 2 - 1) as pair:
                for q in range(2):
                    e = 2 * pair + q
                    sp.wait_ge(hid_done, HID0 + 9 * e + 9)
                    load_first(e + 2, q)
                    store_rows(e, q)
                    load_second(e + 2, q)
                    load_slots(e + 2, q)
            for q in range(2):
                store_rows(NE - 2 + q, q)

            if layers > 1:
                sp.dma_start(w_rwkv, a["w_rwkv"].rearrange("p (i c o) -> p i c o", i=4, c=DC)).then_inc(w1_in, 16)
                sp.dma_start(part(arenaC, 4160, DC * D), a["w_lin"]).then_inc(wlin_in, 16)
                sp.dma_start(lin_scale, a["lin_scale"].to_broadcast([P, D])).then_inc(wlin_in, 16)
                sp.dma_start(lin_bias, a["lin_bias"].to_broadcast([P, D])).then_inc(wlin_in, 16)
            if layers > 2:
                sp.wait_ge(x_done, NT // 2)
                sp.dma_start(part(arenaD, 7168, NF * D), a["w_down3"]).then_inc(wff3_in, 16)
                sp.dma_start(part(arenaC, 0, 2048), a["w2"]).then_inc(w2_in, 16)

                def gateup_in(e, q):
                    src = a["wexp2"][e] if isinstance(e, int) else a["wexp2"][bass.ds(e, 1)].rearrange("e p n -> (e p) n")
                    sp.dma_start(part(arenaD, 1536 * q, 1024), src[:, 0:1024]).then_inc(w2exp_in[q], 16)

                def down_in(e, q):
                    src = a["wexp2"][e] if isinstance(e, int) else a["wexp2"][bass.ds(e, 1)].rearrange("e p n -> (e p) n")
                    sp.dma_start(part(arenaD, 1536 * q + 1024, 512), src[:, 1024:1536]).then_inc(wdown_in[q], 16)

                def following(e, q):
                    sp.wait_ge(up_ready, 4 * e + 4)
                    gateup_in(e + 2, q)
                    sp.wait_ge(e2_ready, 8 * e)
                    down_in(e + 1, 1 - q)

                for q in range(2):
                    gateup_in(q, q)
                    down_in(q, q)
                sp.dma_start(part(arenaC, 2048, 2048), a["w3"]).then_inc(w3_in, 16)
                sp.dma_start(part(arenaD, 5120, 2048), a["wff3"][:, 2048:4096]).then_inc(w3_in, 16)
                sp.wait_ge(up_ready, 4)
                gateup_in(2, 0)
                with sp.Fori(0, E2 // 2 - 2) as pair:
                    following(2 * pair + 1, 1)
                    following(2 * pair + 2, 0)
                following(E2 - 3, 1)
                sp.wait_ge(e2_ready, 8 * E2 - 16)
                down_in(E2 - 1, 1)
                sp.wait_ge(e2_ready, 8 * E2)
                sp.dma_start(part(arenaD, 3072, 2048), a["wff3"][:, 0:2048]).then_inc(wgate3_in, 16)
            for i in range(NT // 2):
                sp.wait_ge(x_done, (layers - 1) * NT // 2 + i + 1)
                sp.dma_start(out[256 * i:256 * i + 256, :].rearrange("(n p) d -> p n d", p=P), x[:, 2 * i:2 * i + 2, :]).then_inc(x_out, 16)
            sp.wait_ge(x_out, 16 * NT // 2)

        @block.gpsimd
        def _(pool):
            pool.memset(mhalf[:, :], -0.5).then_inc(mhalf_set, 1)
            pool.memset(ones[:, :], 1.0).then_inc(ones_set, 1)
            pool.memset(arenaB[:, 0:NE * SLOTS // P * D], 0.0).then_inc(zeros_set, 1)
            for q in range(2):
                pool.sem_inc(rows_out[q], ROWS0)

            def rsqrt(layer):
                pool.wait_ge(mhalf_set, 1)
                for i in range(NT // 2):
                    sl = slice(2 * i, 2 * i + 2)
                    pool.wait_ge(ln_var, NT // 2 * layer + i + 1)
                    pool.tensor_tensor(rstd[:, sl], veps[:, sl], mhalf[:, sl], ALU.pow).then_inc(ln_rstd, 1)

            def rotary_attention():
                def heads(s0, which):
                    return qkv2[:, 4 * s0:4 * s0 + 4, which * D:(which + 1) * D]

                def table(at, half=None):
                    v = con[:, at:at + D]
                    if half is None:
                        return v.unsqueeze(1).to_broadcast([P, 4, D])
                    return v.rearrange("p (h two i) -> p h two i", h=H2, two=2)[:, :, half, :].unsqueeze(1).to_broadcast([P, 4, H2, 8])

                def halves(v, half):
                    return v.rearrange("p t (h two i) -> p t h two i", h=H2, two=2)[:, :, :, half, :]

                pool.wait_ge(qkv_done, 2 * NT)
                r3, p3 = (m.rearrange("p t h e -> p t (h e)") for m in (rot, prod))
                for which in range(2):
                    v = heads(1, which)
                    for half in range(2):
                        link(pool.tensor_tensor(halves(r3, half), halves(v, 1 - half), table(C_SIN, half), ALU.mult))
                    link(pool.tensor_tensor(v, v, table(C_COS), ALU.mult))
                    link(pool.tensor_tensor(v, v, r3, ALU.add))
                link(pool.memset(sc2[:, 0, 1, :], 4.0 * BLOCKED))
                for s0, u0 in ((0, 0), (1, 0), (1, 1)):
                    link(pool.tensor_tensor(p3, heads(s0, 0), heads(u0, 1), ALU.mult))
                    src = p3.rearrange("p t (h e) -> p (t h) e", h=H2)
                    for lv, w in enumerate((8, 4, 2, 1)):
                        dst = tree[:, 0:64 * w].rearrange("p (m e) -> p m e", e=w) if w > 1 and lv % 2 == 0 else \
                            tree[:, 512:512 + 64 * w].rearrange("p (m e) -> p m e", e=w) if w > 1 else \
                            sc2[:, s0, u0, :].unsqueeze(2)
                        link(pool.tensor_tensor(dst, src[:, :, 0:w], src[:, :, w:2 * w], ALU.add))
                        src = dst
                pool.tensor_scalar(sc2, sc2, HD2 ** -0.5, None, ALU.mult).then_inc(sc_done, 1)
                pool.wait_ge(prob2_done, 2)
                for s0 in range(2):
                    for u0 in range(2):
                        w = sc2[:, s0, u0, :].rearrange("p (t h) -> p t h", h=H2).unsqueeze(3).to_broadcast([P, 4, H2, HD2])
                        v = heads(u0, 2).rearrange("p t (h e) -> p t h e", h=H2)
                        link(pool.tensor_tensor(rot if u0 == 0 else prod, v, w, ALU.mult))
                    pool.tensor_tensor(ctx_tok[:, 4 * s0:4 * s0 + 4, :], r3, p3, ALU.add).then_inc(ctx_done, 1)
                    pool.wait_ge(ctx_done, s0 + 1)

            link = Link(pool, pool_link)
            rsqrt(0)

            def split_qkv(h, q, turn):
                pool.wait_ge(wqkv_in[q], 16 * turn + 16)
                pool.tensor_tensor(r(wqkv_hi[q]), wqkv[q], ones[:, 0:1].unsqueeze(1).to_broadcast([P, DC, 3 * DH]), ALU.mult
                                   ).then_inc(wqkv_rounded, 1)
                pool.wait_ge(wqkv_rounded, h + 1)
                pool.tensor_tensor(r(wqkv[q]), wqkv[q], rounded(wqkv_hi[q]), ALU.subtract).then_inc(wqkv_split, 1)

            def rest_k(h, q, b):
                sl = slice(b * S, (b + 1) * S)
                pool.wait_ge(kfull_done, 2 * h + b + 1)
                pool.tensor_tensor(r(klo[q][:, sl]), klo[q][:, sl], rounded(kT[q][:, sl]), ALU.subtract).then_inc(klo_done, 1)

            def split_sums(h, b):
                pool.wait_ge(acc_done, ACC0 + 8 * h + 4 * b + 4)
                pool.tensor_tensor(r(acc_hi[b]), acc[b], ones[:, 0:1].to_broadcast([P, S]), ALU.mult).then_inc(acc_rounded, 1)
                pool.wait_ge(acc_rounded, 2 * h + b + 1)
                pool.tensor_tensor(r(acc[b]), acc[b], rounded(acc_hi[b]), ALU.subtract).then_inc(acc_split, 1)

            def head(h, q, turn, first=False):
                if not first:
                    split_sums(h - 1, 1)
                split_qkv(h + 2, q, turn)
                rest_k(h + 1, 1 - q, 0)
                split_sums(h, 0)
                rest_k(h + 1, 1 - q, 1)

            pool.wait_ge(ones_set, 1)
            split_qkv(0, 0, 0)
            split_qkv(1, 1, 0)
            rest_k(0, 0, 0)
            rest_k(0, 0, 1)
            head(0, 0, 1, first=True)
            with pool.Fori(0, NH // 2 - 2) as pair:
                head(2 * pair + 1, 1, pair + 1)
                head(2 * pair + 2, 0, pair + 2)
            head(NH - 3, 1, NH // 2 - 1)
            split_sums(NH - 3, 1)
            rest_k(NH - 1, 1, 0)
            split_sums(NH - 2, 0)
            rest_k(NH - 1, 1, 1)
            split_sums(NH - 2, 1)
            pool.wait_ge(at_done, 2)
            pool.wait_ge(slots_zero, 16)
            for t in range(NT):
                for k in range(2):
                    pool.indirect_dma_start(out=slots_d, out_offset=bass.IndirectOffsetOnAxis(put_at[:, t, k:k + 1], 0),
                                            in_=xn[:, t, :], in_offset=None, bounds_check=NE * SLOTS - 1,
                                            oob_is_err=False).then_inc(slots_put, 16)

            def split_expert(e, w, hi, wd_hi_):
                for n, (v, h) in ((4, (w[:, 0:W_D], hi[:, 0:W_D])), (5, (w[:, W_D:W_B], wd_hi_)),
                                  (7, (w[:, W_2:W_2 + 1024], hi[:, -2048:-1024])), (9, (w[:, W_2 + 1024:WPACK], hi[:, -1024:]))):
                    pool.wait_ge(w_rounded, 9 * e + n)
                    pool.tensor_tensor(r(v), v, rounded(h), ALU.subtract).then_inc(w_split, 1)

            wd_flat = [v.rearrange("p c r -> p (c r)") for v in wd_hi]
            split_expert(0, wexp[0], wexp_hi[0], wd_flat[0])
            with pool.Fori(0, NE // 2 - 1) as pair:
                split_expert(2 * pair + 1, wexp[1], wexp_hi[1], wd_flat[1])
                split_expert(2 * pair + 2, wexp[0], wexp_hi[0], wd_flat[0])
            split_expert(NE - 1, wexp[1], wexp_hi[1], wd_flat[1])
            split_expert(NE, sw, sw_hi, sw_hi[:, W_D:W_B])
            for q in range(2):
                pool.wait_ge(rows_out[q], ROWS0 + 32 * NE // 2)
            for t in range(NT):
                for k in range(2):
                    pool.indirect_dma_start(out=got[k][:, t, :], out_offset=None, in_=rows_d,
                                            in_offset=bass.IndirectOffsetOnAxis(get_at[:, t, k:k + 1], 0),
                                            bounds_check=NE * SLOTS - 1, oob_is_err=False).then_inc(rows_got, 16)

            if layers > 1:
                rsqrt(1)
            def split_flat(n, v, hi):
                pool.tensor_tensor(r(hi), v, ones[:, 0:1].to_broadcast([P, v.shape[1]]), ALU.mult).then_inc(wq_rounded, 1)
                pool.wait_ge(wq_rounded, n)
                pool.tensor_tensor(r(v), v, rounded(hi), ALU.subtract).then_inc(wq_split, 1)

            if layers > 2:
                pool.wait_ge(w2_in, 16)
                split_flat(1, part(arenaC, 0, DC * 768), part(arenaC, 10752, DC * 768))
                pool.wait_ge(had_copied, 4)
                for stage, (src, dst) in enumerate([(had_b, w_down3), (w_down3, had_b), (had_b, w_down3)]):
                    step = 1 << stage
                    v = [m.rearrange("p (u two w) d -> p u two (w d)", two=2, w=step) for m in (src, dst)]
                    pool.tensor_tensor(v[1][:, :, 0], v[0][:, :, 0], v[0][:, :, 1], ALU.add).then_inc(had_done, 1)
                    pool.tensor_tensor(v[1][:, :, 1], v[0][:, :, 0], v[0][:, :, 1], ALU.subtract).then_inc(had_done, 1)
                    pool.wait_ge(had_done, 2 * stage + 2)
                rsqrt(2)
                rotary_attention()
            if layers > 3:
                pool.wait_ge(w3_in, 32)
                split_flat(2, part(arenaC, 2048, DC * 768), part(arenaB, 0, DC * 768))
                for i in (1, 0):
                    if i == 0:
                        rsqrt(3)
                    for n in range(2):
                        pool.wait_ge(ff3_rounded, 4 * (1 - i) + 2 * n + 2)
                        v, h = part(arenaD, 3072 + 2048 * i + 1024 * n, 1024), part(arenaB, 1536 + 2048 * i + 1024 * n, 1024)
                        pool.tensor_tensor(r(v), v, rounded(h), ALU.subtract).then_inc(ff3_split, 1)
                for t in range(NT):
                    pool.wait_ge(qkv_done, 2 * NT + 2 * t + 2)
                    if t >= 2:
                        pool.wait_ge(ms_done, t - 1)
                    pool.tensor_tensor(sq3[:, t % 2, :], qk3[:, t, :], qk3[:, t, :], ALU.mult).then_inc(sq_done, 1)
                pool.wait_ge(rms_done, 1)
                for t in range(NT):
                    v = qk3[:, t, :].rearrange("p (g e) -> p g e", e=G3)
                    pool.tensor_tensor(v, v, rmsr[:, t, :].unsqueeze(2).to_broadcast([P, 32, G3]), ALU.mult).then_inc(qk_done, 1)
                for u in range(32):
                    pool.wait_ge(exp3_done, 4 * u + 4)
                    d = prob3[:, u % 2, :, 0:P]
                    pool.tensor_tensor(d, d, con[:, C_CAUSAL:C_CAUSAL + P].unsqueeze(1).to_broadcast([P, 4, P]), ALU.mult
                                       ).then_inc(causal_done, 1)

        @block.tensor
        def _(pe):
            def turn_xn(layer):
                pe.wait_ge(con_in, 16)
                for t in range(NT):
                    pe.wait_ge(xn_done, NT * layer + t + 1)
                    for c in range(DC):
                        o = bank[t // 2][:, (t % 2) * 256 + c * P:(t % 2) * 256 + (c + 1) * P]
                        mm = pe.transpose(o, xn[:, t, c * P:(c + 1) * P], ident)
                    mm.then_inc(turn_ready, 1)

            def turned(layer, i):
                if SPLIT[layer]:
                    pe.wait_ge(xnT_dve, XT_DVE[layer] + i + 1)
                else:
                    pe.wait_ge(xnT_act, XT_ACT[layer] + i + 1)

            turn_xn(0)
            turned(0, 3)
            pe.wait_ge(gate_in, 16)
            for t in range(NT):
                for n, (v, c) in enumerate((v, c) for v in (xnT, xlo) for c in range(DC)):
                    mm = pe.matmul(bank[7][:, t * NE:(t + 1) * NE], rounded(v[:, c, t * P:(t + 1) * P]), gate[:, c, :],
                                   start=(n == 0), stop=(n == 2 * DC - 1))
            mm.then_inc(logits_ready, 1)

            PROJ = [(0, 0), (1, 0), (0, 1), (1, 1), (2, 0), (2, 1)]

            def project_tile(h, q, n, first=False):
                w, b = PROJ[n]
                if not first or n >= 3:
                    s, v = [(kfull_done, 2 * h), (v_done, 2 * h - 1), (v_done, 2 * h),
                            (qlo_done, 2 * h + 1), (kfull_done, 2 * h + 1), (qlo_done, 2 * h + 2)][n]
                    pe.wait_ge(s, v)
                for c in range(DC):
                    mm = product(pe, bank[n % 3][:, :], [m[q][:, c, w * DH:(w + 1) * DH] for m in (wqkv_hi, wqkv)],
                                 [m[:, c, b * S:(b + 1) * S] for m in (xnT, xlo)], c == 0, c == DC - 1)
                mm.then_inc(proj_ready, 1)


            def score(h, q, n):
                b = n // ST
                if n % ST == 0:
                    pe.wait_ge(qlo_done, 2 * h + 1 + b)
                    pe.wait_ge(klo_done, 2 * h + 1 + b)
                pe.wait_ge(exp_done, 8 * h + n + 1)
                product(pe, bank[3 + n % 4][:, :], [m[q][:, n * P:(n + 1) * P] for m in (qT, qlo)],
                        [m[q][:, b * S:(b + 1) * S] for m in (kT, klo)], True, True).then_inc(score_ready, 1)

            def colsum(h, b, whole=False):
                pe.wait_ge(vals_done, 2 * h + b + 1)
                if whole:
                    pe.wait_ge(acc_done, ACC0 + 8 * h + 4 * b + 4)
                    pe.matmul(bank[7][:, :], ones[:, :], acc[b], start=True, stop=True).then_inc(colsum_ready, 1)
                    return
                pe.wait_ge(acc_split, 2 * h + b + 1)
                pe.matmul(bank[7][:, :], ones_r[:, :].bitcast(F32R), r(acc_hi[b]), start=True, stop=False)
                pe.matmul(bank[7][:, :], ones_r[:, :].bitcast(F32R), r(acc[b]), start=False, stop=True).then_inc(colsum_ready, 1)

            def head(h, q, first=False, last=False):
                for n in range(8):
                    score(h, q, n)
                    if n == 3 and not first:
                        colsum(h - 1, 1)
                    tile = {1: 0, 2: 1, 4: 2, 5: 3, 6: 4, 7: 5}.get(n)
                    if tile is not None and not last:
                        if tile == 0:
                            pe.wait_ge(wqkv_split, h + 2)
                        project_tile(h + 1, 1 - q, tile)
                    if n == 7:
                        colsum(h, 0, whole=last)

            pe.wait_ge(wqkv_split, 1)
            for n in range(6):
                project_tile(0, 0, n, first=True)
            pe.wait_ge(ones_set, 1)
            pe.wait_ge(oh_done, 1)
            pe.matmul(bank[7][:, 0:128], con[:, C_TRI:C_TRI + P], oh.rearrange("p t k e -> p (t k e)"), start=True, stop=False)
            pe.matmul(bank[7][:, 0:128], ones[:, :], before.rearrange("p t k e -> p (t k e)"), start=False, stop=True
                      ).then_inc(place_ready, 1)
            pe.wait_ge(ones_rounded, 1)
            head(0, 0, first=True)
            with pe.Fori(0, NH // 2 - 1) as pair:
                head(2 * pair + 1, 1)
                head(2 * pair + 2, 0)
            head(NH - 1, 1, last=True)
            pe.wait_ge(wo_in, 16)
            pe.wait_ge(v_done, 2 * NH)
            pe.wait_ge(vals_done, VALS0 + 2 * NH - 2)
            for t in range(NT):
                for h in range(NH):
                    if t == 0 and h == NH - 1:
                        colsum(NH - 1, 1, whole=True)
                        pe.wait_ge(vals_done, VALS0 + 2 * NH)
                    mm = pe.matmul(bank[t // 2][:, (t % 2) * D:(t % 2 + 1) * D], vals[:, h, t * P:(t + 1) * P], wo[:, h, :],
                                   start=(h == 0), stop=(h == NH - 1))
                mm.then_inc(s_ready, 1)

            pe.wait_ge(s_done, NT // 2)

            def turn(e, pair, q):
                pe.wait_ge(xe_in[q], 32 * pair + 32)
                pe.wait_ge(xeT_done, 2 * e + 2)
                for c in range(DC):
                    for s, rows in enumerate(SROWS):
                        mm = pe.transpose(bank[c][:, s * P:s * P + rows], xe[q][0:rows, s, c * P:(c + 1) * P],
                                          ident[0:rows, 0:rows])
                    mm.then_inc(xeT_ready, 1)

            def hidden(e, q):
                pe.wait_ge(w_split, 4 * e + 2)
                pe.wait_ge(xeT_done, TURN0 + 2 * e + 2)
                for n in range(NF + 1):
                    f = n - 1
                    pe.wait_ge(hid_done, 9 * e + n + 1)
                    for c in range(DC):
                        w = [m[q][:, c, f * P:(f + 1) * P] if n else v[q][:, c, :] for m, v in ((w1_hi, wd_hi), (w1, wd))]
                        mm = product(pe, bank[2 + n % 3][0:P if n else RANK, 0:SLOTS], w,
                                     [m[q][:, c, :] for m in (xeT, xeT_lo)], c == 0, c == DC - 1)
                    mm.then_inc(hid_ready, 1)

            def rows_of(e, turn, q):
                pe.wait_ge(w2exp0_in[q], 48 * turn + 48)
                for s, rows in enumerate(SROWS):
                    pe.wait_ge(y_done, 3 * e + s + 1)
                    o = bank[5 + s][0:rows, 0:D]
                    for f in range(NF):
                        if s == 0:
                            if f % 4 == 0:
                                pe.wait_ge(w_split, 4 * e + 3 + f // 4)
                            pe.wait_ge(h_split, NF * e + f + 1)
                        product(pe, o, [m[:, f, s * P:s * P + rows] for m in (hE_hi, hE)], [m[q][:, f, :] for m in (w2_hi, w2)],
                                f == 0, False)
                    pe.matmul(o, aE[:, s * P:s * P + rows], wu[q], start=False, stop=True).then_inc(y_ready, 1)

            turn(0, 0, 0)
            with pe.Fori(0, NE // 2 - 1) as pair:
                for q in range(2):
                    e = 2 * pair + q
                    hidden(e, q)
                    turn(e + 1, pair + q, 1 - q)
                    rows_of(e, pair, q)
            hidden(NE - 2, 0)
            turn(NE - 1, NE // 2 - 1, 1)
            rows_of(NE - 2, NE // 2 - 1, 0)
            hidden(NE - 1, 1)
            rows_of(NE - 1, NE // 2 - 1, 1)

            pe.wait_ge(w_split, 4 * NE + 2)
            for b in range(B):
                for f in range(NF + 1):
                    n = (NF + 1) * b + f
                    if n >= 4:
                        pe.wait_ge(shid_done, n - 3)
                    for c in range(DC):
                        w = [m[:, c, f * P:(f + 1) * P] if f < NF else v[:, c, :] for m, v in ((sw1_hi, swd_hi), (sw1, swd))]
                        mm = product(pe, bank[n % 4][0:P if f < NF else RANK, :], w, [m[:, c, b * S:(b + 1) * S] for m in (xnT, xlo)],
                                     c == 0, c == DC - 1)
                    mm.then_inc(shid_ready, 1)
            pe.wait_ge(shid_done, B * (NF + 1))
            pe.wait_ge(y_done, Y0 + 3 * NE)
            pe.wait_ge(w_split, 4 * NE + 4)
            pe.wait_ge(sw_in, 48)
            for t in range(NT):
                b = t // ST
                o = bank[4 + t // 2][:, (t % 2) * D:(t % 2 + 1) * D]
                for f in range(NF):
                    if t % ST == 0:
                        pe.wait_ge(hS_split, NF * b + f + 1)
                    product(pe, o, [hS_hi[b][:, f, t % ST * P:(t % ST + 1) * P], hS[:, f, t * P:(t + 1) * P]],
                            [m[:, f, :] for m in (sw2_hi, sw2)], f == 0, False)
                pe.matmul(o, aS[:, t * P:(t + 1) * P], swu, start=False, stop=True).then_inc(sh_ready, 1)

            def token_major(lhs, w, first_bank, free, ready):
                for t in range(NT):
                    if free and t % 2 == 0:
                        free(t // 2)
                    for c in range(DC):
                        mm = pe.matmul(bank[first_bank + t // 2][:, (t % 2) * D:(t % 2 + 1) * D], lhs[:, c, t * P:(t + 1) * P],
                                       w[:, c, :], start=(c == 0), stop=(c == DC - 1))
                    mm.then_inc(ready, 1)

            def qkv_rows(w, w_hi, layer):
                for t in range(NT):
                    if t >= 3:
                        pe.wait_ge(qkv_done, 2 * (NT * (layer - 2) + t) - 4)
                    b0 = QKV_BANK[t % 3]
                    if t < 3:
                        turned(layer, (0, 1, 3)[t])
                    if layer == 2 and t == 4:
                        router2()
                    for o, w0, n in ((bank[b0][:, :], 0, 512), (bank[b0 + 1][:, 0:D], 512, D)):
                        for c in range(DC):
                            mm = product(pe, o, [m[:, c, t * P:(t + 1) * P] for m in (xnT, XLO[layer])],
                                         [m[:, c, w0:w0 + n] for m in (w_hi, w)], c == 0, c == DC - 1)
                    mm.then_inc(qkv_ready, 1)

            if layers > 1:
                turn_xn(1)
                pe.wait_ge(w1_in, 16)
                n = 0
                for i in (0, 2, 1):
                    for b in range(B):
                        pe.wait_ge(mix_done, B * (0, 2, 1)[i] + b + 1)
                        for o in range(DC):
                            if n >= 4:
                                pe.wait_ge(kr_done, n - 3)
                            for c in range(DC):
                                mm = pe.matmul(bank[4 + n % 4][:, :], w_rwkv[:, i, c, o * P:(o + 1) * P],
                                               mixed[:, i, c, b * S:(b + 1) * S], start=(c == 0), stop=(c == DC - 1))
                            mm.then_inc(kvr_ready, 1)
                            n += 1
                if layers > 2:
                    pe.wait_ge(wff3_in, 16)
                    turned(1, 3)
                    for i in range(4):
                        pe.matmul(bank[i][:, :], con[:, C_HAD:C_HAD + P], w_down3[:, 2 * i:2 * i + 2, :].rearrange("p f d -> p (f d)"),
                                  start=True, stop=True).then_inc(had_ready, 1)
                    pe.wait_ge(had_copied, 4)
                pe.wait_ge(wlin_done, 1)
                turned(1, 3)
                token_major(xnT, w_lin, 0, None, g_ready)
                token_major(rr, w_rwkv[:, 3], 4, lambda i: pe.wait_ge(rwkv_done, i // 2 + 1), s_ready)
            if layers > 2:
                turn_xn(2)

                def router2():
                    for t in range(NT):
                        for n, (v, c) in enumerate((v, c) for v in (xnT, xlo) for c in range(DC)):
                            mm = pe.matmul(bank[7][:, t * E2:(t + 1) * E2], rounded(v[:, c, t * P:(t + 1) * P]), gate2[:, c, :],
                                           start=(n == 0), stop=(n == 2 * DC - 1))
                    mm.then_inc(z_ready, 1)

                pe.wait_ge(wq_split, 1)
                qkv_rows(w_qkv2, w_qkv2_hi, 2)
                pe.wait_ge(qkv_done, 2 * NT)
                pe.wait_ge(z_done, 1)

                def gate_up(e, q):
                    pe.wait_ge(gateup_split, e + 1)
                    for n in range(4):
                        f, b = n // 2, n % 2
                        for i, (rdy, done) in enumerate(((gate_ready, silu2_done), (up_ready, gu_done))):
                            pe.wait_ge(done, 4 * e + n + 1)
                            for c in range(DC):
                                mm = product(pe, bank[2 * i + n % 2][:, :], [m[q][:, i, c, f * P:(f + 1) * P] for m in (wexp2_hi, wexp2)],
                                             [m[:, c, b * S:(b + 1) * S] for m in (xnT, xlo)], c == 0, c == DC - 1)
                            mm.then_inc(rdy, 1)

                def down(e, q):
                    pe.wait_ge(gu_split, 4 * e + 4)
                    pe.wait_ge(down_split, e + 1)
                    for t in range(NT):
                        if t % 2 == 0:
                            pe.wait_ge(e2_done, 8 * e + t + 2)
                        for f in range(DC):
                            mm = product(pe, bank[4 + t // 2][:, (t % 2) * D:(t % 2 + 1) * D], [m[q][:, f, t * P:(t + 1) * P] for m in (gu_hi, gu)],
                                         [m[q][:, 2, f, :] for m in (wexp2_hi, wexp2)], f == 0, f == DC - 1)
                        mm.then_inc(e2_ready, 1)

                gate_up(0, 0)
                with pe.Fori(0, E2 // 2 - 1) as pair:
                    for q in range(2):
                        gate_up(2 * pair + q + 1, 1 - q)
                        down(2 * pair + q, q)
                gate_up(E2 - 1, 1)
                down(E2 - 2, 0)
                pe.wait_ge(gu_done, GU0 + 4 * E2)
                pe.wait_ge(ctx_done, 2)
                for t in range(NT):
                    for c in range(DC):
                        mm = pe.transpose(bank[t // 2][:, (t % 2) * 256 + c * P:(t % 2) * 256 + (c + 1) * P],
                                          ctx_tok[:, t, c * P:(c + 1) * P], ident)
                    mm.then_inc(ctxT_ready, 1)
                down(E2 - 1, 1)
                pe.wait_ge(ctxT_done, 4)
                token_major(ctxT, w_dense, 0, None, s_ready)
            if layers > 3:
                turn_xn(3)
                pe.wait_ge(wq_split, 2)
                qkv_rows(w_qkv3, w_qkv3_hi, 3)
                pe.wait_ge(qkv_done, 4 * NT)

                def turn_qk(t):
                    pe.wait_ge(qk_done, t + 1)
                    if t >= 4:
                        pe.wait_ge(qT_done, t - 3)
                        pe.wait_ge(kT_done, t - 3)
                    for j in range(4):
                        mm = pe.transpose(bank[4 + t % 4][:, j * P:(j + 1) * P], qk3[:, t, j * P:(j + 1) * P], ident)
                    mm.then_inc(qkT_ready, 1)

                pe.wait_ge(ff3_split, 4)
                for n in range(2 * NF):
                    f, b = n // 2, n % 2
                    for i, (w, rdy, done) in enumerate((((w_gate3_hi, w_gate3), gate3_ready, silu3_done),
                                                        ((w_up3_hi, w_up3), up3_ready, hid3_done))):
                        if n >= 2:
                            pe.wait_ge(done, n - 1)
                        for c in range(DC):
                            mm = product(pe, bank[2 * i + n % 2][:, :], [m[:, c, f * P:(f + 1) * P] for m in w],
                                         [m[:, c, b * S:(b + 1) * S] for m in (xnT, xlo3)], c == 0, c == DC - 1)
                        mm.then_inc(rdy, 1)
                    if n >= 6 and n % 2 == 0 and (n - 6) // 2 < 5:
                        turn_qk((n - 6) // 2)
                for t in range(5, NT):
                    turn_qk(t)
                pe.wait_ge(qT_done, NT)
                pe.wait_ge(kT_done, NT)
                pe.wait_ge(silu3_done, 2 * NF)
                pe.wait_ge(hid3_done, 2 * NF)

                def unit(u):
                    return u // 16, u // 8 % 2, u // 4 % 2, u % 4

                def scores3(u):
                    b, c, j, kt = unit(u)
                    if u % 8 == 0:
                        pe.wait_ge(kz_done, 8 * (u // 8) + 8)
                    for hh in range(4):
                        if u:
                            pe.wait_ge(exp3_done, 4 * u - 3 + hh)
                        pe.matmul(bank[hh][:, 0:S - kt * P], kz[:, c, 2 * hh + j, kt * P:(kt + 1) * P],
                                  q3T[:, c, b * S + kt * P:(b + 1) * S], start=True, stop=True).then_inc(sc3_ready, 1)

                def mix3(u):
                    b, c, j, kt = unit(u)
                    pe.wait_ge(causal_done, u + 1)
                    if kt == 0 and u >= 8:
                        pe.wait_ge(norm3_done, u // 4 - 1)
                    for o, which in ((bank[4 + j], 0), (bank[6 + j], 1)):
                        for hh in range(4):
                            head = 4 * c + hh
                            w = ones[:, 0:32] if which else v3[:, ST * b + kt, 32 * head:32 * head + 32]
                            mm = pe.matmul(o[32 * hh:32 * hh + 32, kt * P:S], w, prob3[:, u % 2, hh, 0:S - kt * P],
                                           start=(kt == 0), stop=(kt == ST - 1), tile_position=(0, 32 * hh))
                    mm.then_inc(av_ready, 1)

                scores3(0)
                for u in range(32):
                    if u < 31:
                        scores3(u + 1)
                    mix3(u)
                pe.wait_ge(had_done, 6)
                for t in range(NT):
                    for f in range(NF):
                        mm = pe.matmul(bank[t // 2][:, (t % 2) * D:(t % 2 + 1) * D], hid3[:, f, t * P:(t + 1) * P], w_down3[:, f, :],
                                       start=(f == 0), stop=(f == NF - 1))
                    mm.then_inc(g3_ready, 1)
                pe.wait_ge(norm3_done, 8)
                token_major(yT3, w_out3, 4, None, s_ready)

        @block.vector
        def _(dve):
            link = Link(dve, dve_link)
            dve.sem_inc(vals_done, VALS0)
            dve.sem_inc(y_done, Y0)
            dve.sem_inc(acc_done, ACC0)

            def residual(layer, i):
                sl = slice(2 * i, 2 * i + 2)
                pair = [m[:, sl, :].rearrange("p a d -> p (a d)") for m in (x, s_tok, g_tok)]
                dve.wait_ge(silu_done, NT // 2 * layer + i + 1)
                if layer == 0:
                    dve.wait_ge(s_done, NT // 2)
                    link(dve.tensor_tensor(pair[1], pair[1], pair[2], ALU.mult))
                    g = pair[1]
                else:
                    dve.wait_ge(s_ready, NT * layer + 2 * i + 2)
                    v = bank[(0, 4, 0, 4)[layer] + i][:, :]
                    g = pair[2]
                    if layer == 3:
                        link(dve.scalar_tensor_tensor(g, v, 1.0 - LAMBDA_INIT, g, ALU.mult, ALU.mult))
                    else:
                        link(dve.tensor_tensor(g, g, v, ALU.mult))
                dve.tensor_tensor(pair[0], pair[0], g, ALU.add).then_inc(x_done, 1)
                dve.wait_ge(x_done, NT // 2 * layer + i + 1)

            def statistics(layer, i):
                for t in (2 * i, 2 * i + 1):
                    ins = dve.bn_stats(stats[:, t, :], x[:, t, :])
                link(ins)
                for t in (2 * i, 2 * i + 1):
                    ins = dve.bn_aggr(meanvar[:, t, :], stats[:, t, :])
                link(ins)
                sl = slice(2 * i, 2 * i + 2)
                dve.tensor_scalar(veps[:, sl], meanvar[:, sl, 1], LN_EPS, None, ALU.add).then_inc(ln_var, 1)

            def normalised(layer, i):
                dve.wait_ge(ln_rstd, NT // 2 * layer + i + 1)
                for t in (2 * i, 2 * i + 1):
                    dve.tensor_scalar(xn[:, t, :], x[:, t, :], meanvar[:, t, 0:1], rstd[:, t:t + 1],
                                      ALU.subtract, ALU.mult).then_inc(xn_done, 1)

            def turned_rest(layer, i):
                if SPLIT[layer]:
                    dve.wait_ge(xnT_act, XT_ACT[layer] + i + 1)
                    dve.tensor_tensor(r(quarter(XLO[layer], i)), turned_bank(i), rounded(quarter(xnT, i)), ALU.subtract).then_inc(xnT_dve, 1)

            def between(layer):
                for i in range(NT // 2 + 2):
                    if i < NT // 2:
                        if layer >= 0:
                            residual(layer, i)
                        else:
                            dve.wait_ge(x_in[i], 16)
                        if layer + 1 < layers:
                            statistics(layer + 1, i)
                    if layer + 1 < layers:
                        if 1 <= i <= NT // 2:
                            normalised(layer + 1, i - 1)
                        if i >= 2:
                            turned_rest(layer + 1, i - 2)

            between(-1)

            def bc(v):
                return v.unsqueeze(2).to_broadcast([P, NT, NE])

            iota = con[:, C_IOTA:C_IOTA + 64].rearrange("p (t e) -> p t e", t=NT)
            dve.wait_ge(con_in, 16)
            dve.wait_ge(logits_ready, 1)
            link(dve.tensor_copy(lg, bank[7][:, 0:64].rearrange("p (t e) -> p t e", t=NT)))

            def choose(k):
                link(dve.tensor_reduce(top[:, k, :], lg, AX.X, ALU.max))
                link(dve.tensor_tensor(eq, lg, bc(top[:, k, :]), ALU.is_equal))
                link(dve.tensor_tensor(eq, eq, iota, ALU.mult))
                link(dve.tensor_reduce(idx[:, :, k], eq, AX.X, ALU.min))
                link(dve.tensor_tensor(oh[:, :, k, :], iota, bc(idx[:, :, k]), ALU.is_equal))

            choose(0)
            dve.tensor_tensor(ex, lg, bc(top[:, 0, :]), ALU.subtract).then_inc(lg_shift, 1)
            link(dve.scalar_tensor_tensor(lg, oh[:, :, 0, :], OUT_OF_REACH, lg, ALU.mult, ALU.add))
            choose(1)
            dve.tensor_tensor(gap, top[:, 1, :], top[:, 0, :], ALU.subtract).then_inc(lg_shift, 1)
            dve.memset(before[:, 0, :, :], 0.0)
            for t in range(1, NT):
                if t == 1:
                    link(dve.tensor_copy(before[:, 1, :, :], oh[:, 0, :, :]))
                else:
                    link(dve.tensor_tensor(before[:, t, :, :], before[:, t - 1, :, :], oh[:, t - 1, :, :], ALU.add))
            dve.memset(kslot[:, :, 0], 8.0 * SLOTS).then_inc(oh_done, 1)
            link(dve.memset(kslot[:, :, 1], 8.0 * SLOTS + CAP))
            def rest_q(h, q, b):
                dve.wait_ge(q_done, 2 * h + b + 1)
                sl = slice(b * S, (b + 1) * S)
                dve.scalar_tensor_tensor(r(qlo[q][:, sl]), bank[2 if b else 0][:, :], DH ** -0.5, rounded(qT[q][:, sl]),
                                         ALU.mult, ALU.subtract).then_inc(qlo_done, 1)

            for b in range(B):
                rest_q(0, 0, b)
            dve.wait_ge(place_ready, 1)
            link(dve.tensor_tensor(ohp.rearrange("p t k e -> p (t k e)"), oh.rearrange("p t k e -> p (t k e)"),
                                   bank[7][:, 0:128], ALU.mult))
            link(dve.tensor_reduce(pos.rearrange("p t k -> p (t k)"), ohp.rearrange("p t k e -> p (t k) e"), AX.X, ALU.add))
            link(dve.tensor_scalar(keep, pos, float(CAP), None, ALU.is_lt))
            link(dve.scalar_tensor_tensor(base, idx, float(SLOTS), kslot, ALU.mult, ALU.add))
            link(dve.tensor_tensor(slot, base, pos, ALU.add))
            link(dve.scalar_tensor_tensor(slot, keep, -NO_SLOT, slot, ALU.mult, ALU.add))
            dve.tensor_scalar(put_at[:, :, :], slot, NO_SLOT, None, ALU.add).then_inc(at_done, 1)
            link(dve.tensor_scalar(pos, pos, CAP - 1.0, None, ALU.min))
            dve.tensor_tensor(get_at[:, :, :], base, pos, ALU.add).then_inc(at_done, 1)
            dve.wait_ge(ex_done, 2)
            link(dve.tensor_reduce(esum, ex, AX.X, ALU.add))
            link(dve.reciprocal(einv, esum))
            link(dve.tensor_tensor(wt[:, :, 0], keep[:, :, 0], einv, ALU.mult))
            link(dve.tensor_tensor(wt[:, :, 1], keep[:, :, 1], einv, ALU.mult))
            link(dve.tensor_tensor(wt[:, :, 1], wt[:, :, 1], gap, ALU.mult))

            def row_max(h, n):
                dve.wait_ge(score_ready, 8 * h + n + 1)
                dve.tensor_reduce(negmax[:, n % 4:n % 4 + 1], bank[3 + n % 4][:, :], AX.X, ALU.max, negate=True
                                  ).then_inc(max_done, 1)

            def invert(h, n):
                dve.wait_ge(exp_done, EXP0 + 8 * h + n + 1)
                dve.reciprocal(rowinv[:, n % 4:n % 4 + 1], rowsum[:, n % 4:n % 4 + 1]).then_inc(inv_done, 1)

            def accumulate(h, n):
                inv = rowinv[:, n % 4:n % 4 + 1]
                dve.wait_ge(inv_done, 8 * h + n + 1)
                if n % ST == 0:
                    ins = dve.tensor_scalar(acc[n // ST], prob[n % 4], inv, None, ALU.mult)
                else:
                    dve.wait_ge(acc_done, ACC0 + 8 * h + n)
                    ins = dve.scalar_tensor_tensor(acc[n // ST], prob[n % 4], inv, acc[n // ST], ALU.mult, ALU.add)
                ins.then_inc(acc_done, 1)

            def values(h, q, b):
                dve.wait_ge(colsum_ready, 2 * h + b + 1)
                dve.wait_ge(v_done, 2 * h + b + 1)
                o = vals[:, h, b * S:(b + 1) * S] if isinstance(h, int) else \
                    vals[:, bass.ds(h, 1), b * S:(b + 1) * S].rearrange("p h t -> p (h t)")
                dve.tensor_tensor(o, bank[7][:, :], vT[q][:, b * S:(b + 1) * S], ALU.mult).then_inc(vals_done, 1)

            def head(h, q, first=False, last=False):
                for n in range(8):
                    before = None if first and n == 0 else (h - 1, 7) if n == 0 else (h, n - 1)
                    if before:
                        invert(*before)
                    row_max(h, n)
                    if before:
                        accumulate(*before)
                    if n in (3, 5) and not last:
                        rest_q(h + 1, 1 - q, n // 5)
                    if n == 0 and not first:
                        values(h - 1, 1 - q, 0)
                    if n == 4 and not first:
                        values(h - 1, 1 - q, 1)

            dve.wait_ge(slots_zero, 16)
            head(0, 0, first=True)
            with dve.Fori(0, NH // 2 - 1) as pair:
                head(2 * pair + 1, 1)
                head(2 * pair + 2, 0)
            head(NH - 1, 1, last=True)
            invert(NH - 1, 7)
            accumulate(NH - 1, 7)
            values(NH - 1, 1, 0)
            values(NH - 1, 1, 1)
            for i in (1, 3):
                dve.wait_ge(s_ready, 2 * i + 2)
                dve.tensor_copy(g_tok[:, 2 * i:2 * i + 2, :].rearrange("p a d -> p (a d)"), bank[i][:, :]).then_inc(s_done, 1)

            def rest_rows(e, q):
                for c in range(DC):
                    dve.wait_ge(xeT_rounded, 2 * e + c + 1)
                    dve.tensor_tensor(r(xeT_lo[q][:, c, :]), bank[c][:, 0:SLOTS], rounded(xeT[q][:, c, :]), ALU.subtract).then_inc(xeT_done, 1)

            def expert(e, q, pair, last=False):
                for f in range(NF + 1):
                    if f < NF:
                        dve.wait_ge(hid_done, HID0 + 9 * e + f + 2)
                        dve.tensor_copy(r(hE_hi[:, f, :]), hE[:, f, :]).then_inc(h_rounded, 1)
                    if f:
                        dve.wait_ge(h_rounded, NF * e + f)
                        dve.tensor_tensor(r(hE[:, f - 1, :]), hE[:, f - 1, :], rounded(hE_hi[:, f - 1, :]), ALU.subtract).then_inc(h_split, 1)
                if not last:
                    rest_rows(e + 1, 1 - q)
                dve.wait_ge(rows_out[q], 32 * pair + 32)
                for s, rows in enumerate(SROWS):
                    dve.wait_ge(y_ready, 3 * e + s + 1)
                    dve.tensor_tensor(yE[q][0:rows, s, :], bank[5 + s][0:rows, 0:D], b2[q][0:rows, :], ALU.add
                                      ).then_inc(y_done, 1)

            rest_rows(0, 0)
            with dve.Fori(0, NE // 2 - 1) as pair:
                expert(2 * pair, 0, pair)
                expert(2 * pair + 1, 1, pair)
            expert(NE - 2, 0, NE // 2 - 1)
            expert(NE - 1, 1, NE // 2 - 1, last=True)
            for b in range(B):
                for f in range(NF + 1):
                    sl = slice(b * S, (b + 1) * S)
                    if f < NF:
                        dve.wait_ge(shid_done, (NF + 1) * b + f + 1)
                        dve.tensor_copy(r(hS_hi[b][:, f, :]), hS[:, f, sl]).then_inc(hS_rounded, 1)
                    if f:
                        dve.wait_ge(hS_rounded, NF * b + f)
                        dve.tensor_tensor(r(hS[:, f - 1, sl]), hS[:, f - 1, sl], rounded(hS_hi[b][:, f - 1, :]), ALU.subtract).then_inc(hS_split, 1)
            link(dve.tensor_scalar(sb2, sb2, 0.2, None, ALU.mult))
            dve.wait_ge(rows_got, 16 * 2 * NT)
            for k in range(2):
                for t in range(NT):
                    ins = dve.scalar_tensor_tensor(got[0][:, t, :], got[k][:, t, :], wt[:, t, k:k + 1], got[0][:, t, :] if k else sb2,
                                                   ALU.mult, ALU.add)
                link(ins)
            for i in range(NT // 2):
                dve.wait_ge(sh_ready, 2 * i + 2)
                dve.scalar_tensor_tensor(s_tok[:, 2 * i:2 * i + 2, :], bank[4 + i][:, :].rearrange("p (t d) -> p t d", t=2), 0.2,
                                         got[0][:, 2 * i:2 * i + 2, :], ALU.mult, ALU.add).then_inc(ffn_done, 1)

            def golden():
                def per(v):
                    return v.unsqueeze(2).to_broadcast([P, NT, E2])

                dve.wait_ge(vec_in, 48)
                dve.wait_ge(z_ready, 1)
                link(dve.reciprocal(temp, temp))
                link(dve.tensor_scalar(z2, bank[7][:, 0:64].rearrange("p (t e) -> p t e", t=NT), temp, None, ALU.mult))
                dve.sem_inc(z_done, 1)
                dve.wait_ge(inh_done, 1)
                link(dve.tensor_scalar(dist, inh, GOLD_C, None, ALU.subtract))
                dve.scalar_tensor_tensor(dist, dist, -1.0, dist, ALU.mult, ALU.max).then_inc(dist_done, 1)
                link(dve.tensor_scalar(zone, z2, Z_LO, None, ALU.is_ge))
                link(dve.scalar_tensor_tensor(zone, z2, 0.0, zone, ALU.is_le, ALU.mult))
                dve.wait_ge(gexp_done, 2)
                link(dve.tensor_tensor(gw, gw, zone, ALU.mult))
                link(dve.tensor_reduce(red8[:, 0, :], gw, AX.X, ALU.add))
                link(dve.tensor_scalar(red8[:, 1, :], red8[:, 0, :], 1e-8, None, ALU.is_lt))
                link(dve.tensor_copy(cand, fb))
                link(dve.memset(mask2, 0.0))
                for k in range(2):
                    link(dve.tensor_reduce(red8[:, 2, :], cand, AX.X, ALU.max))
                    link(dve.tensor_tensor(zone, cand, per(red8[:, 2, :]), ALU.is_equal))
                    link(dve.tensor_tensor(zone, zone, iota, ALU.mult))
                    link(dve.tensor_reduce(red8[:, 3, :], zone, AX.X, ALU.min))
                    link(dve.tensor_tensor(zone, iota, per(red8[:, 3, :]), ALU.is_equal))
                    link(dve.tensor_tensor(mask2, mask2, zone, ALU.add))
                    link(dve.scalar_tensor_tensor(cand, zone, -4.0, cand, ALU.mult, ALU.add))
                link(dve.tensor_tensor(fb, fb, mask2, ALU.mult))

                def normal(v):
                    link(dve.tensor_reduce(red8[:, 4, :], v, AX.X, ALU.add))
                    link(dve.tensor_scalar(red8[:, 4, :], red8[:, 4, :], 1e-8, None, ALU.max))
                    link(dve.reciprocal(red8[:, 4, :], red8[:, 4, :]))
                    link(dve.tensor_tensor(v, v, per(red8[:, 4, :]), ALU.mult))

                normal(fb)
                link(dve.tensor_tensor(fb, fb, per(red8[:, 1, :]), ALU.mult))
                link(dve.tensor_scalar(red8[:, 1, :], red8[:, 1, :], -1.0, 1.0, ALU.mult, ALU.add))
                link(dve.tensor_tensor(gw, gw, per(red8[:, 1, :]), ALU.mult))
                link(dve.tensor_tensor(gw, gw, fb, ALU.add))
                normal(gw)

            between(0)

            if layers > 1:
                dve.wait_ge(vec_in, 48)
                link(dve.tensor_scalar(offs, vec[:, 0:3, :], -1.0, 1.0, ALU.mult, ALU.add))
                link(dve.tensor_tensor(offs, offs, vec[:, 3:4, :].to_broadcast([P, 3, DC]), ALU.mult))
                def mix(i):
                    for b in range(B):
                        dve.wait_ge(xnT_act, XT_ACT[1] + 2 * b + 2)
                        for c in range(DC):
                            ins = dve.tensor_scalar(mixed[:, i, c, b * S:(b + 1) * S], xnT[:, c, b * S:(b + 1) * S],
                                                    vec[:, i, c:c + 1], offs[:, i, c:c + 1], ALU.mult, ALU.add)
                        ins.then_inc(mix_done, 1)

                for i in (0, 2, 1):
                    mix(i)
                dve.wait_ge(wlin_in, 48)
                dve.tensor_tensor(w_lin, w_lin, lin_scale.unsqueeze(1).to_broadcast([P, DC, D]), ALU.mult).then_inc(wlin_done, 1)
                for b in range(B):
                    sl = slice(b * S, (b + 1) * S)
                    dve.wait_ge(kr_done, 2 * b + 2)
                    w0 = kk[:, :, b * S:b * S + 1]
                    f = [first[:, i, :, b:b + 1] for i in range(4)]
                    pp, aa, bb = (vec[:, i, :].unsqueeze(2) for i in (6, 4, 5))
                    link(dve.tensor_tensor(f[0], w0, pp, ALU.max))
                    link(dve.tensor_tensor(f[1], pp, f[0], ALU.subtract))
                    link(dve.tensor_tensor(f[2], w0, f[0], ALU.subtract))
                    link(dve.tensor_scalar(kk[:, :, sl], kk[:, :, sl], 0.0, None, ALU.min))
                    dve.tensor_copy(w0, f[2]).then_inc(low_done, 1)
                for b in range(B):
                    sl = slice(b * S, (b + 1) * S)
                    dve.wait_ge(e_done, 2 * b + 2)
                    dve.wait_ge(kr_done, 4)
                    f = [first[:, i, :, b:b + 1] for i in range(4)]
                    aa, bb = (vec[:, i, :].unsqueeze(2) for i in (4, 5))
                    dve.tensor_tensor(f[2], f[1], aa, ALU.mult)
                    link(dve.tensor_tensor(f[3], f[1], bb, ALU.mult))
                    link(dve.tensor_tensor(f[3], f[3], kk[:, :, b * S:b * S + 1], ALU.add))
                    link(dve.reciprocal(mixed[:, 0, :, sl], kk[:, :, sl]))
                    dve.reciprocal(mixed[:, 0, :, b * S:b * S + 1], f[3]).then_inc(inv1_done, 1)
                for b in range(B):
                    sl = slice(b * S, (b + 1) * S)
                    for o in range(DC):
                        dve.wait_ge(kvr_ready, 8 + 2 * b + o + 1)
                        ins = dve.tensor_tensor(vv[:, o, sl], bank[4 + 2 * b + o][:, :], kk[:, o, sl], ALU.mult)
                    link(ins)
                    n0 = vv[:, :, b * S:b * S + 1]
                    link(dve.tensor_tensor(n0, n0, first[:, 2, :, b:b + 1], ALU.add))
                    dve.wait_ge(inv1_done, b + 1)
                    link(dve.tensor_tensor(vv[:, :, sl], vv[:, :, sl], mixed[:, 0, :, sl], ALU.mult))
                    dve.wait_ge(kr_done, 4 + 2 * b + 2)
                    dve.tensor_tensor(rr[:, :, sl], rr[:, :, sl], vv[:, :, sl], ALU.mult).then_inc(rwkv_done, 1)
                for i in range(NT // 2):
                    dve.wait_ge(g_ready, 2 * i + 2)
                    dve.tensor_tensor(g_tok[:, 2 * i:2 * i + 2, :], bank[i][:, :].rearrange("p (t d) -> p t d", t=2),
                                      lin_bias.unsqueeze(1).to_broadcast([P, 2, D]), ALU.add).then_inc(ffn_done, 1)
                between(1)
            if layers > 2:
                dve.sem_inc(gu_done, GU0)
                dve.sem_inc(e2_done, E20)

                def gateup_rest(e, q):
                    dve.wait_ge(gateup_rounded, 2 * e + 2)
                    dve.tensor_tensor(r(wexp2[q][:, 0:2]), wexp2[q][:, 0:2], rounded(wexp2_hi[q][:, 0:2]), ALU.subtract).then_inc(gateup_split, 1)

                def down_rest(e, q):
                    dve.wait_ge(down_rounded, e + 1)
                    dve.tensor_tensor(r(wexp2[q][:, 2]), wexp2[q][:, 2], rounded(wexp2_hi[q][:, 2]), ALU.subtract).then_inc(down_split, 1)

                golden()
                gateup_rest(0, 0)
                dve.wait_ge(had_done, 6)
                link(dve.memset(g_tok[:, :, :], 0.0))

                def mult(e, q, n):
                    f, b = n // 2, n % 2
                    dve.wait_ge(up_ready, 4 * e + n + 1)
                    dve.wait_ge(silu2_done, 2 + 4 * e + n + 1)
                    v, h = (m[q][:, f, b * S:(b + 1) * S] for m in (gu, gu_hi))
                    dve.tensor_tensor(v, bank[2 + n % 2][:, :], gs[n % 2], ALU.mult).then_inc(gu_done, 1)
                    if n:
                        rest_gu(e, q, n - 1)
                    dve.wait_ge(gu_done, GU0 + 4 * e + n + 1)
                    dve.tensor_copy(r(h), v).then_inc(gu_rounded, 1)
                    if n == 3:
                        rest_gu(e, q, n)

                def rest_gu(e, q, n):
                    v, h = (m[q][:, n // 2, n % 2 * S:(n % 2 + 1) * S] for m in (gu, gu_hi))
                    dve.wait_ge(gu_rounded, 4 * e + n + 1)
                    dve.tensor_tensor(r(v), v, rounded(h), ALU.subtract).then_inc(gu_split, 1)

                def add_expert(e, q, last=False):
                    for t in range(NT):
                        dve.wait_ge(e2_ready, 8 * e + 2 * (t // 2) + 2)
                        w = gw[:, t, e:e + 1] if isinstance(e, int) else gw[:, t, bass.ds(e, 1)]
                        dve.scalar_tensor_tensor(g_tok[:, t, :], bank[4 + t // 2][:, (t % 2) * D:(t % 2 + 1) * D], w,
                                                 g_tok[:, t, :], ALU.mult, ALU.add).then_inc(e2_done, 1)
                    if not last:
                        dve.wait_ge(e2_done, E20 + 8 * e + 8)

                for n in range(4):
                    mult(0, 0, n)
                gateup_rest(1, 1)
                down_rest(0, 0)
                def following(e, q, between=None):
                    for n in range(4):
                        mult(e + 1, 1 - q, n)
                        if between and n == 1:
                            between()
                    gateup_rest(e + 2, q)
                    down_rest(e + 1, 1 - q)
                    add_expert(e, q)

                with dve.Fori(0, E2 // 2 - 2) as pair:
                    following(2 * pair, 0)
                    following(2 * pair + 1, 1)
                dve.wait_ge(sc_done, 1)
                link(dve.tensor_tensor(mx2, sc2[:, :, 0, :], sc2[:, :, 1, :], ALU.max))
                for u0 in range(2):
                    dve.tensor_tensor(sc2[:, :, u0, :], sc2[:, :, u0, :], mx2, ALU.subtract).then_inc(low2_done, 1)

                def divide():
                    dve.wait_ge(sexp_done, 1)
                    link(dve.tensor_tensor(mx2, sc2[:, :, 0, :], sc2[:, :, 1, :], ALU.add))
                    link(dve.reciprocal(mx2, mx2))
                    for u0 in range(2):
                        dve.tensor_tensor(sc2[:, :, u0, :], sc2[:, :, u0, :], mx2, ALU.mult).then_inc(prob2_done, 1)

                following(E2 - 4, 0, between=divide)
                following(E2 - 3, 1)
                for n in range(4):
                    mult(E2 - 1, 1, n)
                down_rest(E2 - 1, 1)
                add_expert(E2 - 2, 0)
                for i in (1, 3):
                    dve.wait_ge(ctxT_ready, 2 * i + 2)
                    dve.tensor_copy(ctxT[:, :, i * 256:(i + 1) * 256].rearrange("p c (t n) -> p t c n", t=2),
                                    bank[i][:, :].rearrange("p (t c n) -> p t c n", t=2, c=DC)).then_inc(ctxT_done, 1)
                add_expert(E2 - 1, 1, last=True)
                between(2)
            if layers > 3:
                dve.wait_ge(lam_in_s, 16)
                for i in range(2):
                    link(dve.tensor_tensor(lam_in[:, 2 * i, :], lam_in[:, 2 * i, :], lam_in[:, 2 * i + 1, :], ALU.mult))
                    dve.tensor_reduce(lam[:, i:i + 1], lam_in[:, 2 * i, :], AX.X, ALU.add).then_inc(lam_sum, 1)
                dve.wait_ge(lam_exp, 1)
                link(dve.tensor_tensor(lam[:, 2:3], lam[:, 1:2], lam[:, 0:1], ALU.subtract))
                link(dve.tensor_scalar(lam[:, 2:3], lam[:, 2:3], LAMBDA_INIT, None, ALU.subtract))

                mean, root = (m[:, :, :].rearrange("p t g -> p (t g)") for m in (rms, rmsr))

                def newton():
                    dve.wait_ge(root_done, 1)
                    link(dve.tensor_tensor(step3, root, root, ALU.mult))
                    link(dve.tensor_tensor(step3, step3, mean, ALU.mult))
                    link(dve.tensor_scalar(step3, step3, -0.5, 1.5, ALU.mult, ALU.add))
                    dve.tensor_tensor(root, root, step3, ALU.mult).then_inc(rms_done, 1)

                def keys3(t):
                    dve.wait_ge(qT_done, t + 1)
                    dve.wait_ge(qkT_ready, t + 1)
                    dve.tensor_copy(k3T[:, :, t * P:(t + 1) * P], bank[4 + t % 4][:, 256:512].rearrange("p (c n) -> p c n", c=DC)
                                    ).then_inc(kT_done, 1)

                def masked_keys(b, c):
                    dve.wait_ge(kT_done, NT)
                    if b:
                        dve.wait_ge(av_ready, 8 * c + 8)
                    for g in range(8):
                        dve.tensor_scalar(kz[:, c, g, :], k3T[:, c, b * S:(b + 1) * S], con[:, C_SEL + g:C_SEL + g + 1], None, ALU.mult
                                          ).then_inc(kz_done, 1)

                for t in range(NT):
                    dve.wait_ge(sq_done, t + 1)
                    dve.tensor_reduce(rms[:, t, :], sq3[:, t % 2, :].rearrange("p (g e) -> p g e", e=G3), AX.X, ALU.add).then_inc(ms_done, 1)
                dve.wait_ge(ms_done, NT)
                link(dve.tensor_scalar(mean, mean, 1.0 / G3, RMS_EPS, ALU.mult, ALU.add))
                dve.reciprocal(root, mean).then_inc(inverse_done, 1)
                for n in range(2 * NF):
                    f, b = n // 2, n % 2
                    dve.wait_ge(up3_ready, n + 1)
                    dve.wait_ge(silu3_done, n + 1)
                    dve.tensor_tensor(hid3[:, f, b * S:(b + 1) * S], bank[2 + n % 2][:, :], gs3[n % 2], ALU.mult).then_inc(hid3_done, 1)
                    if n == 1:
                        newton()
                    if n >= 7 and n % 2 == 1 and (n - 7) // 2 < 5:
                        keys3((n - 7) // 2)
                for t in range(5, NT):
                    keys3(t)
                masked_keys(0, 0)
                masked_keys(0, 1)

                def normalise(b, c, j):
                    i = 4 * b + 2 * c + j
                    dve.wait_ge(av_ready, 4 * i + 4)
                    if i:
                        dve.wait_ge(norm3_done, i)
                    link(dve.reciprocal(zinv, bank[6 + j][:, :]))
                    if j == 0:
                        dve.tensor_tensor(y3[:, 0, :], bank[4][:, :], zinv, ALU.mult).then_inc(norm3_done, 1)
                    else:
                        link(dve.tensor_tensor(y3[:, 1, :], bank[5][:, :], zinv, ALU.mult))
                        dve.scalar_tensor_tensor(yT3[:, c, b * S:(b + 1) * S], y3[:, 1, :], lam[:, 2:3], y3[:, 0, :],
                                                 ALU.mult, ALU.add).then_inc(norm3_done, 1)

                for b in range(B):
                    for c in range(DC):
                        normalise(b, c, 0)
                        normalise(b, c, 1)
                        if b == 0:
                            masked_keys(1, c)
                for i in range(NT // 2):
                    dve.wait_ge(g3_ready, 2 * i + 2)
                    dve.tensor_scalar(g_tok[:, 2 * i:2 * i + 2, :].rearrange("p a d -> p (a d)"), bank[i][:, :], FF ** -0.5, None, ALU.mult
                                      ).then_inc(ffn_done, 1)
                between(3)

        @block.scalar
        def _(act):
            link = Link(act, act_link)
            act.sem_inc(exp_done, EXP0)
            act.sem_inc(hid_done, HID0)
            act.sem_inc(xeT_done, TURN0)

            def turned(layer):
                for i in range(4):
                    act.wait_ge(turn_ready, NT * layer + 2 * i + 2)
                    act.copy(r(quarter(xnT, i)) if SPLIT[layer] else quarter(xnT, i), turned_bank(i)).then_inc(xnT_act, 1)

            turned(0)

            def queries(h, q, b):
                act.wait_ge(proj_ready, 6 * h + 1 + 2 * b)
                act.mul(r(qT[q][:, b * S:(b + 1) * S]), bank[2 if b else 0][:, :], DH ** -0.5).then_inc(q_done, 1)

            def keys(h, q, b):
                act.wait_ge(proj_ready, 6 * h + 2 + 2 * b)
                act.copy(r(kT[q][:, b * S:(b + 1) * S]), bank[0 if b else 1][:, :]).then_inc(k_done, 1)
                act.copy(klo[q][:, b * S:(b + 1) * S], bank[0 if b else 1][:, :]).then_inc(kfull_done, 1)

            def value_rows(h, q, b):
                act.wait_ge(proj_ready, 6 * h + 5 + b)
                act.copy(vT[q][:, b * S:(b + 1) * S], bank[1 + b][:, :]).then_inc(v_done, 1)

            def exponent(h, n):
                r = n % 4
                act.wait_ge(max_done, 8 * h + n + 1)
                act.activation(prob[r], bank[3 + r][:, :], ACT.Exp, bias=negmax[:, r:r + 1],
                               accum_out=rowsum[:, r:r + 1]).then_inc(exp_done, 1)

            def head(h, q, first=False, last=False):
                for n in range(8):
                    act.wait_ge(acc_done, 8 * h + n + 1)
                    exponent(h, n)
                    if last:
                        continue
                    if n in (1, 4):
                        queries(h + 1, 1 - q, n // 4)
                    if n in (2, 5):
                        keys(h + 1, 1 - q, n // 5)
                    if n >= 6:
                        if n == 6 and not first:
                            act.wait_ge(vals_done, VALS0 + 2 * h)
                        value_rows(h + 1, 1 - q, n - 6)

            act.wait_ge(ones_set, 1)
            act.copy(ones_r[:, :].bitcast(F32R), ones[:, :]).then_inc(ones_rounded, 1)
            for b in range(B):
                queries(0, 0, b)
                keys(0, 0, b)
            value_rows(0, 0, 0)
            value_rows(0, 0, 1)
            act.wait_ge(lg_shift, 1)
            act.activation(ex, ex, ACT.Exp).then_inc(ex_done, 1)
            act.wait_ge(lg_shift, 2)
            act.activation(gap, gap, ACT.Exp).then_inc(ex_done, 1)
            head(0, 0, first=True)
            with act.Fori(0, NH // 2 - 1) as pair:
                head(2 * pair + 1, 1)
                head(2 * pair + 2, 0)
            head(NH - 1, 1, last=True)

            def round_weights(w, hi, wd_hi_, n):
                if n < 4:
                    v, h = w[:, 512 * n:512 * n + 512], hi[:, 512 * n:512 * n + 512]
                elif n == 4:
                    v, h = w[:, W_D:W_B], wd_hi_
                else:
                    v, h = w[:, W_2 + 512 * (n - 5):W_2 + 512 * (n - 4)], hi[:, hi.shape[1] - 512 * (9 - n):hi.shape[1] - 512 * (8 - n)]
                act.copy(r(h), v).then_inc(w_rounded, 1)

            wd_flat = [v.rearrange("p c r -> p (c r)") for v in wd_hi]

            def round_rows(e, q):
                for c in range(DC):
                    act.wait_ge(xeT_ready, 2 * e + c + 1)
                    act.copy(r(xeT[q][:, c, :]), bank[c][:, 0:SLOTS]).then_inc(xeT_rounded, 1)

            def expert(e, q, turn):
                last = turn is None
                act.wait_ge(y_done, Y0 + 3 * e)
                for n in range(NF + 1):
                    act.wait_ge(hid_ready, 9 * e + n + 1)
                    if n == 0:
                        act.activation(aE, bank[2][0:RANK, 0:SLOTS], ACT.Gelu).then_inc(hid_done, 1)
                    else:
                        act.activation(hE[:, n - 1, :], bank[2 + n % 3][:, 0:SLOTS], ACT.Gelu, bias=b1[q][:, n - 1:n]
                                       ).then_inc(hid_done, 1)
                    if n < 5:
                        if n == 0:
                            act.wait_ge(sw_in if last else w1exp_in[1 - q], 48 if last else 16 * turn + 16)
                        round_weights(*((sw, sw_hi, sw_hi[:, W_D:W_B]) if last else (wexp[1 - q], wexp_hi[1 - q], wd_flat[1 - q])), n)
                if not last:
                    round_rows(e + 1, 1 - q)
                    act.wait_ge(w2exp0_in[1 - q], 48 * turn + 48)
                for n in range(5, 9):
                    round_weights(*((sw, sw_hi, sw_hi[:, W_D:W_B]) if last else (wexp[1 - q], wexp_hi[1 - q], wd_flat[1 - q])), n)

            act.wait_ge(w1exp_in[0], 16)
            act.wait_ge(w2exp0_in[0], 48)
            for n in range(9):
                round_weights(wexp[0], wexp_hi[0], wd_flat[0], n)
            for i in (0, 2):
                act.wait_ge(s_ready, 2 * i + 2)
                act.copy(g_tok[:, 2 * i:2 * i + 2, :].rearrange("p a d -> p (a d)"), bank[i][:, :]).then_inc(s_done, 1)
            round_rows(0, 0)
            with act.Fori(0, NE // 2 - 1) as pair:
                expert(2 * pair, 0, pair)
                expert(2 * pair + 1, 1, pair + 1)
            expert(NE - 2, 0, NE // 2 - 1)
            expert(NE - 1, 1, None)
            for b in range(B):
                for f in range(NF + 1):
                    n = (NF + 1) * b + f
                    act.wait_ge(shid_ready, n + 1)
                    if f < NF:
                        ins = act.activation(hS[:, f, b * S:(b + 1) * S], bank[n % 4][:, :], ACT.Gelu, bias=sb1[:, f:f + 1])
                    else:
                        ins = act.activation(aS[:, b * S:(b + 1) * S], bank[n % 4][0:RANK, :], ACT.Gelu)
                    ins.then_inc(shid_done, 1)

            def gate_silu(layer):
                g = g_tok if layer else s_tok
                for i in range(NT // 2):
                    if layer == 2:
                        act.wait_ge(e2_done, E20 + 8 * (E2 - 1) + 2 * i + 2)
                    else:
                        act.wait_ge(ffn_done, NT // 2 * (layer if layer < 3 else 2) + i + 1)
                    act.activation(g[:, 2 * i:2 * i + 2, :], g[:, 2 * i:2 * i + 2, :], ACT.Silu).then_inc(silu_done, 1)

            gate_silu(0)

            if layers > 1:
                turned(1)
                act.wait_ge(vec_in, 48)
                def act_exponentials():
                    for b in range(B):
                        act.wait_ge(low_done, b + 1)
                        act.activation(kk[:, :, b * S:(b + 1) * S], kk[:, :, b * S:(b + 1) * S], ACT.Exp).then_inc(e_done, 1)
                        act.activation(first[:, 1, :, b:b + 1], first[:, 1, :, b:b + 1], ACT.Exp).then_inc(e_done, 1)

                for i in (0, 2):
                    if i:
                        act_exponentials()
                    for b in range(B):
                        for o in range(DC):
                            n = 2 * i + 2 * b + o
                            act.wait_ge(kvr_ready, n + 1)
                            v = bank[4 + n % 4][:, :]
                            if i == 0:
                                ins = act.activation(kk[:, o, b * S:(b + 1) * S], v, ACT.Identity, bias=vec[:, 7, o:o + 1])
                            else:
                                ins = act.activation(rr[:, o, b * S:(b + 1) * S], v, ACT.Sigmoid)
                            ins.then_inc(kr_done, 1)
                if layers > 2:
                    for i in range(4):
                        act.wait_ge(had_ready, i + 1)
                        act.copy(had_b[:, 2 * i:2 * i + 2, :].rearrange("p f d -> p (f d)"), bank[i][:, :]).then_inc(had_copied, 1)
                gate_silu(1)

            def qkv_copy(layer, first=0, end=NT):
                for t in range(first, end):
                    act.wait_ge(qkv_ready, NT * (layer - 2) + t + 1)
                    b0 = QKV_BANK[t % 3]
                    qk, v = (qkv2[:, t, 0:512], qkv2[:, t, 512:768]) if layer == 2 else (qk3[:, t, :], v3[:, t, :])
                    act.copy(qk, bank[b0][:, :]).then_inc(qkv_done, 1)
                    act.copy(v, bank[b0 + 1][:, 0:D]).then_inc(qkv_done, 1)

            if layers > 2:
                turned(2)
                act.sem_inc(silu2_done, 2)
                qkv_copy(2, 0, NT // 2)
                act.wait_ge(z_done, 1)
                act.activation(inh, z2, ACT.Sigmoid).then_inc(inh_done, 1)
                act.wait_ge(dist_done, 1)
                act.activation(gw, dist, ACT.Exp, scale=-1.0 / 0.1).then_inc(gexp_done, 1)
                act.activation(fb, dist, ACT.Exp, scale=-1.0 / 0.3).then_inc(gexp_done, 1)

                def round_gateup(e, q, turn):
                    act.wait_ge(w2exp_in[q], 16 * turn + 16)
                    for i in range(2):
                        act.copy(r(wexp2_hi[q][:, i]), wexp2[q][:, i]).then_inc(gateup_rounded, 1)

                def round_down(e, q, turn):
                    act.wait_ge(wdown_in[q], 16 * turn + 16)
                    act.copy(r(wexp2_hi[q][:, 2]), wexp2[q][:, 2]).then_inc(down_rounded, 1)

                round_gateup(0, 0, 0)
                qkv_copy(2, NT // 2)
                round_gateup(1, 1, 0)
                round_down(0, 0, 0)

                def silu2(e, n):
                    act.wait_ge(gate_ready, 4 * e + n + 1)
                    act.wait_ge(gu_done, 4 * e + n + 1)
                    act.activation(gs[n % 2], bank[n % 2][:, :], ACT.Silu).then_inc(silu2_done, 1)

                for n in range(4):
                    silu2(0, n)
                def following(e, q, turn):
                    for n in range(4):
                        silu2(e + 1, n)
                        if n == 1:
                            round_gateup(e + 2, q, turn + 1)
                        if n == 2:
                            round_down(e + 1, 1 - q, turn + q)

                with act.Fori(0, E2 // 2 - 2) as pair:
                    following(2 * pair, 0, pair)
                    following(2 * pair + 1, 1, pair)
                act.wait_ge(low2_done, 2)
                act.activation(sc2, sc2, ACT.Exp).then_inc(sexp_done, 1)
                following(E2 - 4, 0, E2 // 2 - 2)
                following(E2 - 3, 1, E2 // 2 - 2)
                for n in range(4):
                    silu2(E2 - 1, n)
                    if n == 2:
                        round_down(E2 - 1, 1, E2 // 2 - 1)
                if layers > 3:
                    act.wait_ge(w3_in, 32)
                    act.wait_ge(ctx_done, 2)
                    for n in range(4):
                        act.copy(r(part(arenaB, 3584 + 512 * n, 512)), part(arenaD, 5120 + 512 * n, 512)).then_inc(ff3_rounded, 1)
                for i in (0, 2):
                    act.wait_ge(ctxT_ready, 2 * i + 2)
                    act.copy(ctxT[:, :, i * 256:(i + 1) * 256].rearrange("p c (t n) -> p t c n", t=2),
                             bank[i][:, :].rearrange("p (t c n) -> p t c n", t=2, c=DC)).then_inc(ctxT_done, 1)
                gate_silu(2)
            if layers > 3:
                turned(3)
                act.wait_ge(wgate3_in, 16)
                for n in range(4):
                    act.copy(r(part(arenaB, 1536 + 512 * n, 512)), part(arenaD, 3072 + 512 * n, 512)).then_inc(ff3_rounded, 1)
                act.wait_ge(lam_sum, 2)
                act.activation(lam[:, 0:2], lam[:, 0:2], ACT.Exp).then_inc(lam_exp, 1)
                qkv_copy(3)

                def queries3(t):
                    act.wait_ge(qkT_ready, t + 1)
                    act.copy(q3T[:, :, t * P:(t + 1) * P], bank[4 + t % 4][:, 0:256].rearrange("p (c n) -> p c n", c=DC)
                             ).then_inc(qT_done, 1)

                for n in range(2 * NF):
                    act.wait_ge(gate3_ready, n + 1)
                    if n >= 2:
                        act.wait_ge(hid3_done, n - 1)
                    act.activation(gs3[n % 2], bank[n % 2][:, :], ACT.Silu).then_inc(silu3_done, 1)
                    if n == 1:
                        act.wait_ge(inverse_done, 1)
                        act.activation(rmsr[:, :, :], rmsr[:, :, :], ACT.Sqrt).then_inc(root_done, 1)
                    if n >= 7 and n % 2 == 1 and (n - 7) // 2 < 5:
                        queries3((n - 7) // 2)
                for t in range(5, NT):
                    queries3(t)
                for u in range(32):
                    w = S - u % 4 * P
                    for hh in range(4):
                        act.wait_ge(sc3_ready, 4 * u + hh + 1)
                        if u >= 2 and hh == 0:
                            act.wait_ge(av_ready, u - 1)
                        act.activation(prob3[:, u % 2, hh, 0:w], bank[hh][:, 0:w], ACT.Exp, scale=G3 ** -0.5).then_inc(exp3_done, 1)
                gate_silu(3)


def _rows(w):
    k, n = w.shape
    return np.ascontiguousarray(w.reshape(k // P, P, n).transpose(1, 0, 2).reshape(P, -1))


def layout(i):
    f = {k: np.asarray(v) for k, v in i.items()}
    w = f["L0_attn_w_qkv"].reshape(DC, P, 3, NH, DH).transpose(3, 1, 0, 2, 4)
    d = {
        "x": f["L0_attn_x"].reshape(T, D),
        "con": constants(),
        "gate": _rows(f["L0_ffn_gate_w"]),
        "wqkv": w.reshape(NH, P, DC * 3 * DH),
        "wo": _rows(f["L0_attn_w_o"]),
        "wexp": np.stack([np.concatenate([_rows(f["L0_ffn_w1"][e]), _rows(f["L0_ffn_wd"][e]),
                                          f["L0_ffn_b1"][e].reshape(NF, P).T, _rows(f["L0_ffn_w2"][e])], 1) for e in range(NE)]),
        "wu": f["L0_ffn_wu"],
        "b2": f["L0_ffn_b2"].reshape(NE, 1, D),
        "sw": np.concatenate([_rows(f["L0_ffn_sw1"]), _rows(f["L0_ffn_swd"]),
                              f["L0_ffn_sb1"].reshape(NF, P).T, _rows(f["L0_ffn_sw2"])], 1),
        "swu": f["L0_ffn_swu"],
        "sb2": f["L0_ffn_sb2"].reshape(1, D),
        "w_rwkv": np.concatenate([_rows(f[f"L1_attn_w_{k}"].T) for k in ("key", "value", "rec", "out")], 1),
        "w_lin": _rows(f["L1_ffn_weight"].T),
        "lin_scale": f["L1_ffn_scale_weight"].reshape(1, D),
        "lin_bias": f["L1_ffn_bias"].reshape(1, D),
        "vec": np.concatenate([_rows(f[f"L1_attn_{k}"].reshape(D, 1)) for k in
                               ("time_mix_k", "time_mix_v", "time_mix_r", "xx", "aa", "bb", "pp", "time_first")], 1),
        "gate2": _rows(f["L2_ffn_Wr"]),
        "temp": f["L2_ffn_temperature"].reshape(1, 1),
        "lam": np.concatenate([f[f"L3_attn_{k}"] for k in ("lq1", "lk1", "lq2", "lk2")]).reshape(1, 128),
        "w2": np.concatenate([_rows(f["L2_attn_w_qkv"].reshape(D, H2, 3, HD2).transpose(0, 2, 1, 3).reshape(D, 3 * D)),
                              _rows(f["L2_attn_w_dense"])], 1),
        "wexp2": np.stack([np.concatenate([_rows(f[f"L2_ffn_{k}"][e]) for k in ("Wg", "Wu", "Wd")], 1) for e in range(E2)]),
        "w3": np.concatenate([_rows(np.concatenate([f[f"L3_attn_{k}"].T for k in ("wq", "wk", "wv")], 1)),
                              _rows(f["L3_attn_wo"].T)], 1),
        "wff3": np.concatenate([_rows(f["L3_ffn_W1"].T), _rows(f["L3_ffn_W3"].T)], 1),
        "w_down3": _rows(f["L3_ffn_W2"].T),
    }
    return {k: np.ascontiguousarray(v) for k, v in d.items()}


def kernel(**inputs):
    import concourse.bacc as bacc
    from concourse.bass_utils import run_bass_kernel_spmd

    nc = bacc.Bacc("TRN2", target_bir_lowering=False, num_devices=1)
    arrays, args = {}, {}
    for name, v in layout(inputs).items():
        arrays[f"in_{name}"] = v
        args[name] = nc.dram_tensor(f"in_{name}", v.shape, F32, kind="ExternalInput").ap()
    out = nc.dram_tensor("out_x", (T, D), F32, kind="ExternalOutput").ap()
    build(nc, args, out)
    r = run_bass_kernel_spmd(nc, [arrays], core_ids=[0])
    return r.results[0]["out_x"].reshape(B, S, D)
```
